# Optimizing a Trainium2 kernel written in Bass

```python
import numpy as np
import jax
import jax.numpy as jnp

def _softmax(x, axis=-1):
    return jax.nn.softmax(x, axis=axis)

def _gelu(x):
    return jax.nn.gelu(x, approximate=True)

def _silu(x):
    return jax.nn.silu(x)

def _sigmoid(x):
    return jax.nn.sigmoid(x)

def _layernorm(x, axis=-1, eps=1e-05):
    m = jnp.mean(x, axis=axis, keepdims=True)
    v = jnp.var(x, axis=axis, keepdims=True)
    return (x - m) / jnp.sqrt(v + eps)

def _scatter_add(tgt, idx, src, axis=0):
    return tgt.at[idx].add(src)

def _segment_sum(src, seg, n):
    return jax.ops.segment_sum(src, seg, n)
kernel_name = 'mk_xattn_ffn_d4_seqx_r4_2e702f'

def setup_inputs(seed: int=0):
    np.random.seed(seed)
    _w = jnp.asarray

    def _rec_inputs():
        import jax
        import jax.numpy as jnp
        _rk = jax.random.key(seed)
        x = -0.0002928 + 1 * jax.random.normal(jax.random.fold_in(_rk, 1), (1, 2048, 256), jnp.float32)
        _lenS = 2048 - jax.random.randint(jax.random.fold_in(_rk, 7), (1,), 0, max(1, 2048 // 4) + 1, jnp.int32)
        _lenS2 = 1601 - jax.random.randint(jax.random.fold_in(_rk, 8), (1,), 0, max(1, 1601 // 4) + 1, jnp.int32)
        _ctx_1024P = jax.random.normal(jax.random.fold_in(_rk, 11), (1, 16, 256), jnp.float32)
        _ctx_1024c = jax.random.dirichlet(jax.random.fold_in(_rk, 511), 0.3 * jnp.ones((16,), jnp.float32), (1, 1601))
        _ctx_1024t = jnp.einsum('bsk,bkd->bsd', _ctx_1024c, _ctx_1024P)
        _ctx_1024t = _ctx_1024t * jax.lax.rsqrt(jnp.mean(jnp.square(_ctx_1024t)) + 1e-12) * 0.953939
        ctx_1024 = -1.39393e-06 + 0.999914 * (_ctx_1024t + 0.3 * jax.random.normal(jax.random.fold_in(_rk, 611), (1, 1601, 256), jnp.float32))
        _validS = jnp.arange(2048)[None, :] < _lenS[:, None]
        _validS2 = jnp.arange(1601)[None, :] < _lenS2[:, None]
        _causal = jnp.tril(jnp.ones((2048, 2048), dtype=bool))
        mask_BxSxS2_ik0 = jnp.where(jnp.broadcast_to(_validS2[:, None, :], (1, 2048, 1601)), 0, 1).astype(jnp.int32)
        mask_1x1xSxS2_ik0 = jnp.where(jnp.broadcast_to(_validS2[0:1, None, None, :], (1, 1, 2048, 1601)), 0, 1).astype(jnp.int32)
        return (x, ctx_1024, mask_BxSxS2_ik0, mask_1x1xSxS2_ik0)
    x, ctx_1024, mask_BxSxS2_ik0, mask_1x1xSxS2_ik0 = _rec_inputs()

    def _L0_xattn_setup():
        import jax, jax.numpy as jnp
        import numpy as np
        B, N, M = (2, 512, 512)
        Q_DIM = 256
        HEADS = 8
        DIM_HEAD = 64
        INNER = HEADS * DIM_HEAD
        key = jax.random.key(seed)
        ks = jax.random.split(key, 7)
        s_in = 1.0 / np.sqrt(Q_DIM)
        s_out = 1.0 / np.sqrt(INNER)
        return {'x': jax.random.normal(ks[0], (B, N, Q_DIM), dtype=jnp.float32), 'context': jax.random.normal(ks[1], (B, M, Q_DIM), dtype=jnp.float32), 'Wq': jax.random.normal(ks[2], (Q_DIM, INNER), dtype=jnp.float32) * s_in, 'Wk': jax.random.normal(ks[3], (Q_DIM, INNER), dtype=jnp.float32) * s_in, 'Wv': jax.random.normal(ks[4], (Q_DIM, INNER), dtype=jnp.float32) * s_in, 'Wo': jax.random.normal(ks[5], (INNER, Q_DIM), dtype=jnp.float32) * s_out, 'bo': jax.random.normal(ks[6], (Q_DIM,), dtype=jnp.float32) * 0.01}
    _L0_xattn_all = _L0_xattn_setup()
    _L0_xattn_in = {k: v for k, v in _L0_xattn_all.items() if k in ('Wq', 'Wk', 'Wv', 'Wo', 'bo')}
    del _L0_xattn_all

    def _L0_ffn_setup():
        import jax, jax.numpy as jnp
        import numpy as np
        SINKHORN_ITERS = 8
        TEMPERATURE = 1.0
        EPS = 1e-06

        def sinkhorn(t):
            t = jnp.log(jnp.clip(t, EPS)) / TEMPERATURE
            for _ in range(SINKHORN_ITERS):
                t = t - jax.nn.logsumexp(t, axis=-2, keepdims=True)
                t = t - jax.nn.logsumexp(t, axis=-1, keepdims=True)
            return jnp.exp(t)
        key = jax.random.key(seed)
        k1, k2, k3 = jax.random.split(key, 3)
        B, N, D, E = (4, 1024, 256, 8)
        x = jax.random.normal(k1, (B, N, D), dtype=jnp.float32)
        gate_w = jax.random.normal(k2, (D, E), dtype=jnp.float32) * D ** (-0.5)
        experts = jax.random.normal(k3, (E, D, D), dtype=jnp.float32) * D ** (-0.5)
        return {'x': x, 'gate_w': gate_w, 'experts': experts}
    _L0_ffn_all = _L0_ffn_setup()
    _L0_ffn_in = {k: v for k, v in _L0_ffn_all.items() if k in ('gate_w', 'experts')}
    del _L0_ffn_all

    def _L1_xattn_setup():
        import jax, jax.numpy as jnp
        import numpy as np
        import math
        B, N, M, D, HID, OUT = (8, 512, 512, 256, 256, 256)
        key = jax.random.key(seed)
        k1, k2, k3, k4, k5, k6 = jax.random.split(key, 6)
        h1 = jax.random.normal(k1, (B, N, D), dtype=jnp.float32)
        h2 = jax.random.normal(k2, (B, M, D), dtype=jnp.float32)
        mask = jax.random.randint(k3, (B, N, M), 0, 2, dtype=jnp.int32)
        Wq = jax.random.normal(k4, (HID, D), dtype=jnp.float32) / math.sqrt(D)
        Wk = jax.random.normal(k5, (HID, D), dtype=jnp.float32) / math.sqrt(D)
        Wv = jax.random.normal(k6, (OUT, D), dtype=jnp.float32) / math.sqrt(D)
        return {'h1': h1, 'h2': h2, 'mask': mask, 'Wq': Wq, 'Wk': Wk, 'Wv': Wv}
    _L1_xattn_all = _L1_xattn_setup()
    _L1_xattn_in = {k: v for k, v in _L1_xattn_all.items() if k in ('Wq', 'Wk', 'Wv')}
    del _L1_xattn_all

    def _L1_ffn_setup():
        import jax, jax.numpy as jnp
        import numpy as np

        def _bitlinear(x, w_latent):
            scale = jax.lax.stop_gradient(jnp.clip(jnp.mean(jnp.abs(w_latent), axis=1, keepdims=True), 1e-05, None))
            tern = jnp.clip(jnp.round(w_latent / scale), -1.0, 1.0)
            w = w_latent + jax.lax.stop_gradient(tern - w_latent)
            return x @ (w * scale).T
        key = jax.random.key(seed)
        ks = jax.random.split(key, 6)
        dim, hidden, rank = (256, 1024, 16)
        B, S = (4, 1024)
        x = jax.random.normal(ks[0], (B, S, dim), dtype=jnp.float32)
        w_fc = 0.02 * jax.random.normal(ks[1], (hidden, dim), dtype=jnp.float32)
        w_proj = 0.02 * jax.random.normal(ks[2], (dim, hidden), dtype=jnp.float32)
        u = 0.02 * jax.random.normal(ks[3], (hidden, rank), dtype=jnp.float32)
        v = 0.02 * jax.random.normal(ks[4], (rank, dim), dtype=jnp.float32)
        fast_b = jax.random.normal(ks[5], (rank, rank), dtype=jnp.float32)
        gate = jnp.float32(0.05)
        return {'x': x, 'fast_b': fast_b, 'w_fc': w_fc, 'w_proj': w_proj, 'u': u, 'v': v, 'gate': gate}
    _L1_ffn_all = _L1_ffn_setup()
    _L1_ffn_in = {k: v for k, v in _L1_ffn_all.items() if k in ('fast_b', 'w_fc', 'w_proj', 'u', 'v', 'gate')}
    del _L1_ffn_all

    def _L2_xattn_setup():
        import jax, jax.numpy as jnp
        import numpy as np
        DIM = 256
        key = jax.random.key(seed)
        ks = jax.random.split(key, 9)
        B, S, D = (8, 512, DIM)
        inv = 1.0 / np.sqrt(D)
        return {'image_emb': jax.random.normal(ks[0], (B, S, D), dtype=jnp.float32), 'text_emb': jax.random.normal(ks[1], (B, S, D), dtype=jnp.float32), 'edge_index': jax.random.randint(ks[2], (2, 16), 0, 512, dtype=jnp.int64), 'Wq': jax.random.normal(ks[3], (D, D), dtype=jnp.float32) * inv, 'bq': jnp.zeros((D,), dtype=jnp.float32), 'Wk': jax.random.normal(ks[4], (D, D), dtype=jnp.float32) * inv, 'bk': jnp.zeros((D,), dtype=jnp.float32), 'Wv': jax.random.normal(ks[5], (D, D), dtype=jnp.float32) * inv, 'bv': jnp.zeros((D,), dtype=jnp.float32)}
    _L2_xattn_all = _L2_xattn_setup()
    _L2_xattn_in = {k: v for k, v in _L2_xattn_all.items() if k in ('edge_index', 'Wq', 'bq', 'Wk', 'bk', 'Wv', 'bv')}
    del _L2_xattn_all

    def _L2_ffn_setup():
        import jax, jax.numpy as jnp
        import numpy as np
        EPS = 1e-08

        def _ternary_linear(x, w):
            alpha = jnp.mean(jnp.abs(w))
            w_t = jnp.sign(w) * (jnp.abs(w) > 0.5 * alpha).astype(w.dtype)
            w_q = w + jax.lax.stop_gradient(w_t - w)
            d = x.shape[-1]
            rms = jnp.sqrt(jnp.sum(x * x, axis=-1, keepdims=True)) / jnp.sqrt(jnp.asarray(d, x.dtype))
            x_norm = x / (rms + EPS)
            return jnp.einsum('bsd,fd->bsf', x_norm, w_q)
        key = jax.random.key(seed)
        k1, k2, k3 = jax.random.split(key, 3)
        d_model, d_ff = (256, 1024)
        B, S = (4, 1024)
        x = jax.random.normal(k1, (B, S, d_model), dtype=jnp.float32)
        w_up = jax.random.normal(k2, (d_ff, d_model), dtype=jnp.float32) * 0.02
        w_down = jax.random.normal(k3, (d_model, d_ff), dtype=jnp.float32) * 0.02
        return {'x': x, 'w_up': w_up, 'w_down': w_down}
    _L2_ffn_all = _L2_ffn_setup()
    _L2_ffn_in = {k: v for k, v in _L2_ffn_all.items() if k in ('w_up', 'w_down')}
    del _L2_ffn_all

    def _L3_xattn_setup():
        import jax, jax.numpy as jnp
        import numpy as np
        B, S, D, H = (2, 512, 256, 16)
        DK = D // H
        key = jax.random.key(seed)
        ks = jax.random.split(key, 12)
        std = 1.0 / np.sqrt(D)
        inp = {'query': jax.random.normal(ks[0], (B, S, D), jnp.float32), 'key': jax.random.normal(ks[1], (B, S, D), jnp.float32), 'value': jax.random.normal(ks[2], (B, S, D), jnp.float32), 'mask': jnp.tril(jnp.ones((S, S), jnp.int32))[None, None, :, :], 'Wq': jax.random.normal(ks[3], (D, D), jnp.float32) * std, 'bq': jax.random.normal(ks[4], (D,), jnp.float32) * std, 'Wk': jax.random.normal(ks[5], (D, D), jnp.float32) * std, 'bk': jax.random.normal(ks[6], (D,), jnp.float32) * std, 'Wv': jax.random.normal(ks[7], (D, D), jnp.float32) * std, 'bv': jax.random.normal(ks[8], (D,), jnp.float32) * std, 'Wo': jax.random.normal(ks[9], (D, D), jnp.float32) * std, 'bo': jax.random.normal(ks[10], (D,), jnp.float32) * std}
        return inp
    _L3_xattn_all = _L3_xattn_setup()
    _L3_xattn_in = {k: v for k, v in _L3_xattn_all.items() if k in ('Wq', 'bq', 'Wk', 'bk', 'Wv', 'bv', 'Wo', 'bo')}
    del _L3_xattn_all

    def _L3_ffn_setup():
        import jax, jax.numpy as jnp
        import numpy as np
        NUM_EXPERTS = 8
        D_MODEL = 256
        D_FF = 1024
        BATCH, SEQ = (2, 1024)
        key = jax.random.key(seed)
        k_x, k_w1, k_w2 = jax.random.split(key, 3)
        x = jax.random.normal(k_x, (BATCH, SEQ, D_MODEL), dtype=jnp.float32)
        w1 = jax.random.normal(k_w1, (NUM_EXPERTS, D_MODEL, D_FF), dtype=jnp.float32) * (1.0 / np.sqrt(D_MODEL))
        b1 = jnp.zeros((NUM_EXPERTS, D_FF), dtype=jnp.float32)
        w2 = jax.random.normal(k_w2, (NUM_EXPERTS, D_FF, D_MODEL), dtype=jnp.float32) * (1.0 / np.sqrt(D_FF))
        b2 = jnp.zeros((NUM_EXPERTS, D_MODEL), dtype=jnp.float32)
        return {'x': x, 'w1': w1, 'b1': b1, 'w2': w2, 'b2': b2}
    _L3_ffn_all = _L3_ffn_setup()
    _L3_ffn_in = {k: v for k, v in _L3_ffn_all.items() if k in ('w1', 'b1', 'w2', 'b2')}
    del _L3_ffn_all
    return {'x': x, 'ctx_1024': ctx_1024, 'mask_BxSxS2_ik0': mask_BxSxS2_ik0, 'mask_1x1xSxS2_ik0': mask_1x1xSxS2_ik0, 'L0_xattn_Wq': _L0_xattn_in['Wq'], 'L0_xattn_Wk': _L0_xattn_in['Wk'], 'L0_xattn_Wv': _L0_xattn_in['Wv'], 'L0_xattn_Wo': _L0_xattn_in['Wo'], 'L0_xattn_bo': _L0_xattn_in['bo'], 'L0_ffn_gate_w': _L0_ffn_in['gate_w'], 'L0_ffn_experts': _L0_ffn_in['experts'], 'L1_xattn_Wq': _L1_xattn_in['Wq'], 'L1_xattn_Wk': _L1_xattn_in['Wk'], 'L1_xattn_Wv': _L1_xattn_in['Wv'], 'L1_ffn_fast_b': _L1_ffn_in['fast_b'], 'L1_ffn_w_fc': _L1_ffn_in['w_fc'], 'L1_ffn_w_proj': _L1_ffn_in['w_proj'], 'L1_ffn_u': _L1_ffn_in['u'], 'L1_ffn_v': _L1_ffn_in['v'], 'L1_ffn_gate': _L1_ffn_in['gate'], 'L2_xattn_edge_index': _L2_xattn_in['edge_index'], 'L2_xattn_Wq': _L2_xattn_in['Wq'], 'L2_xattn_bq': _L2_xattn_in['bq'], 'L2_xattn_Wk': _L2_xattn_in['Wk'], 'L2_xattn_bk': _L2_xattn_in['bk'], 'L2_xattn_Wv': _L2_xattn_in['Wv'], 'L2_xattn_bv': _L2_xattn_in['bv'], 'L2_ffn_w_up': _L2_ffn_in['w_up'], 'L2_ffn_w_down': _L2_ffn_in['w_down'], 'L3_xattn_Wq': _L3_xattn_in['Wq'], 'L3_xattn_bq': _L3_xattn_in['bq'], 'L3_xattn_Wk': _L3_xattn_in['Wk'], 'L3_xattn_bk': _L3_xattn_in['bk'], 'L3_xattn_Wv': _L3_xattn_in['Wv'], 'L3_xattn_bv': _L3_xattn_in['bv'], 'L3_xattn_Wo': _L3_xattn_in['Wo'], 'L3_xattn_bo': _L3_xattn_in['bo'], 'L3_ffn_w1': _L3_ffn_in['w1'], 'L3_ffn_b1': _L3_ffn_in['b1'], 'L3_ffn_w2': _L3_ffn_in['w2'], 'L3_ffn_b2': _L3_ffn_in['b2']}

def reference(x, ctx_1024, mask_BxSxS2_ik0, mask_1x1xSxS2_ik0, L0_xattn_Wq, L0_xattn_Wk, L0_xattn_Wv, L0_xattn_Wo, L0_xattn_bo, L0_ffn_gate_w, L0_ffn_experts, L1_xattn_Wq, L1_xattn_Wk, L1_xattn_Wv, L1_ffn_fast_b, L1_ffn_w_fc, L1_ffn_w_proj, L1_ffn_u, L1_ffn_v, L1_ffn_gate, L2_xattn_edge_index, L2_xattn_Wq, L2_xattn_bq, L2_xattn_Wk, L2_xattn_bk, L2_xattn_Wv, L2_xattn_bv, L2_ffn_w_up, L2_ffn_w_down, L3_xattn_Wq, L3_xattn_bq, L3_xattn_Wk, L3_xattn_bk, L3_xattn_Wv, L3_xattn_bv, L3_xattn_Wo, L3_xattn_bo, L3_ffn_w1, L3_ffn_b1, L3_ffn_w2, L3_ffn_b2):
    import jax
    import jax.numpy as jnp

    def _L0_xattn_ref(x, context, Wq, Wk, Wv, Wo, bo):
        import jax, jax.numpy as jnp
        import numpy as np
        B, N, M = (2, 512, 512)
        Q_DIM = 256
        HEADS = 8
        DIM_HEAD = 64
        INNER = HEADS * DIM_HEAD
        scale = DIM_HEAD ** (-0.5)

        def split_heads(t):
            b, n, _ = t.shape
            return t.reshape(b, n, HEADS, DIM_HEAD).transpose(0, 2, 1, 3)
        q = split_heads(x @ Wq)
        k = split_heads(context @ Wk)
        v = split_heads(context @ Wv)
        sim = jnp.einsum('bhid,bhjd->bhij', q, k) * scale
        attn = jax.nn.softmax(sim, axis=-1)
        out = jnp.einsum('bhij,bhjd->bhid', attn, v)
        out = out.transpose(0, 2, 1, 3).reshape(x.shape[0], x.shape[1], INNER)
        return out @ Wo + bo

    def _L0_ffn_ref(x, gate_w, experts):
        import jax, jax.numpy as jnp
        import numpy as np
        SINKHORN_ITERS = 8
        TEMPERATURE = 1.0
        EPS = 1e-06

        def sinkhorn(t):
            t = jnp.log(jnp.clip(t, EPS)) / TEMPERATURE
            for _ in range(SINKHORN_ITERS):
                t = t - jax.nn.logsumexp(t, axis=-2, keepdims=True)
                t = t - jax.nn.logsumexp(t, axis=-1, keepdims=True)
            return jnp.exp(t)
        B, N, D = x.shape
        E = gate_w.shape[-1]
        M = N // E
        gate_logits = jnp.einsum('bnd,de->bne', x, gate_w)
        competitive_gates = sinkhorn(gate_logits)
        vals, idx = jax.lax.top_k(jnp.swapaxes(competitive_gates, -1, -2), M)
        gate_values = jnp.swapaxes(vals, -1, -2)
        routed_indices = jnp.swapaxes(idx, -1, -2)
        b_idx = jnp.arange(B)[:, None, None]
        routed = x[b_idx, routed_indices]
        routed = jnp.transpose(routed, (2, 0, 1, 3))
        outputs = jnp.einsum('ebmd,edf->ebmf', routed, experts)
        outputs = outputs * jnp.transpose(gate_values, (2, 0, 1))[..., None]
        vals_bmed = jnp.transpose(outputs, (1, 2, 0, 3))
        routed_back = jnp.zeros_like(x).at[b_idx, routed_indices].set(vals_bmed)
        return routed_back

    def _L1_xattn_ref(h1, h2, mask, Wq, Wk, Wv):
        import jax, jax.numpy as jnp
        import numpy as np
        import math
        B, N, M, D, HID, OUT = (8, 512, 512, 256, 256, 256)
        Q = jnp.einsum('bnd,hd->bnh', h1, Wq)
        K = jnp.einsum('bmd,hd->bmh', h2, Wk)
        V = jnp.einsum('bmd,od->bmo', h2, Wv)
        E = jnp.einsum('bnh,bmh->bnm', Q, K)
        E = jnp.where(mask == 0, jnp.float32(-10000000000.0), E)
        A = jax.nn.softmax(E / math.sqrt(HID), axis=2)
        return jnp.einsum('bnm,bmo->bno', A, V)

    def _L1_ffn_ref(x, fast_b, w_fc, w_proj, u, v, gate):
        import jax, jax.numpy as jnp
        import numpy as np

        def _bitlinear(x, w_latent):
            scale = jax.lax.stop_gradient(jnp.clip(jnp.mean(jnp.abs(w_latent), axis=1, keepdims=True), 1e-05, None))
            tern = jnp.clip(jnp.round(w_latent / scale), -1.0, 1.0)
            w = w_latent + jax.lax.stop_gradient(tern - w_latent)
            return x @ (w * scale).T
        h = _bitlinear(x, w_fc) + gate * (x @ v.T @ fast_b.T @ u.T)
        r = jnp.maximum(h, 0.0)
        return _bitlinear(r * r, w_proj)

    def _L2_xattn_ref(image_emb, text_emb, edge_index, Wq, bq, Wk, bk, Wv, bv):
        import jax, jax.numpy as jnp
        import numpy as np
        DIM = 256
        D = image_emb.shape[-1]
        scale = D ** (-0.5)
        q = jnp.einsum('bsd,ed->bse', image_emb, Wq) + bq
        k = jnp.einsum('bsd,ed->bse', text_emb, Wk) + bk
        v = jnp.einsum('bsd,ed->bse', text_emb, Wv) + bv
        scores = jnp.einsum('bqd,bkd->bqk', q, k) * scale
        probs = jax.nn.softmax(scores, axis=-1)
        attended = jnp.einsum('bqk,bkd->bqd', probs, v)
        return attended

    def _L2_ffn_ref(x, w_up, w_down):
        import jax, jax.numpy as jnp
        import numpy as np
        EPS = 1e-08

        def _ternary_linear(x, w):
            alpha = jnp.mean(jnp.abs(w))
            w_t = jnp.sign(w) * (jnp.abs(w) > 0.5 * alpha).astype(w.dtype)
            w_q = w + jax.lax.stop_gradient(w_t - w)
            d = x.shape[-1]
            rms = jnp.sqrt(jnp.sum(x * x, axis=-1, keepdims=True)) / jnp.sqrt(jnp.asarray(d, x.dtype))
            x_norm = x / (rms + EPS)
            return jnp.einsum('bsd,fd->bsf', x_norm, w_q)
        h = jax.nn.gelu(_ternary_linear(x, w_up), approximate=False)
        return _ternary_linear(h, w_down)

    def _L3_xattn_ref(query, key, value, mask, Wq, bq, Wk, bk, Wv, bv, Wo, bo):
        import jax, jax.numpy as jnp
        import numpy as np
        B, S, D, H = (2, 512, 256, 16)
        DK = D // H
        b = query.shape[0]
        Q = query @ Wq.T + bq
        K = key @ Wk.T + bk
        V = value @ Wv.T + bv
        Q = Q.reshape(b, -1, H, DK).transpose(0, 2, 1, 3)
        K = K.reshape(b, -1, H, DK).transpose(0, 2, 1, 3)
        V = V.reshape(b, -1, H, DK).transpose(0, 2, 1, 3)
        scores = jnp.einsum('bhqd,bhkd->bhqk', Q, K) / jnp.sqrt(jnp.float32(DK))
        scores = jnp.where(mask == 0, -jnp.inf, scores)
        weights = jax.nn.softmax(scores, axis=-1)
        attn = jnp.einsum('bhqk,bhkd->bhqd', weights, V)
        attn = attn.transpose(0, 2, 1, 3).reshape(b, -1, D)
        return attn @ Wo.T + bo

    def _L3_ffn_ref(x, w1, b1, w2, b2):
        import jax, jax.numpy as jnp
        import numpy as np
        NUM_EXPERTS = 8
        D_MODEL = 256
        D_FF = 1024
        BATCH, SEQ = (2, 1024)
        B, S, D = x.shape
        E = w1.shape[0]
        T = B * S // E
        tokens = x.reshape(E, T, D)
        h = jnp.einsum('etd,edf->etf', tokens, w1) + b1[:, None, :]
        h = jax.nn.gelu(h)
        y = jnp.einsum('etf,efd->etd', h, w2) + b2[:, None, :]
        return y.reshape(B, S, D)
    x = x + _L0_xattn_ref(_layernorm(x, axis=-1), ctx_1024, L0_xattn_Wq, L0_xattn_Wk, L0_xattn_Wv, L0_xattn_Wo, L0_xattn_bo)
    x = x + _L0_ffn_ref(_layernorm(x, axis=-1), L0_ffn_gate_w, L0_ffn_experts)
    x = x + _L1_xattn_ref(_layernorm(x, axis=-1), ctx_1024, mask_BxSxS2_ik0, L1_xattn_Wq, L1_xattn_Wk, L1_xattn_Wv)
    x = x + _L1_ffn_ref(_layernorm(x, axis=-1), L1_ffn_fast_b, L1_ffn_w_fc, L1_ffn_w_proj, L1_ffn_u, L1_ffn_v, L1_ffn_gate)
    x = x + _L2_xattn_ref(_layernorm(x, axis=-1), ctx_1024, L2_xattn_edge_index, L2_xattn_Wq, L2_xattn_bq, L2_xattn_Wk, L2_xattn_bk, L2_xattn_Wv, L2_xattn_bv)
    x = x + _L2_ffn_ref(_layernorm(x, axis=-1), L2_ffn_w_up, L2_ffn_w_down)
    x = x + _L3_xattn_ref(_layernorm(x, axis=-1), ctx_1024, ctx_1024, mask_1x1xSxS2_ik0, L3_xattn_Wq, L3_xattn_bq, L3_xattn_Wk, L3_xattn_bk, L3_xattn_Wv, L3_xattn_bv, L3_xattn_Wo, L3_xattn_bo)
    x = x + _L3_ffn_ref(_layernorm(x, axis=-1), L3_ffn_w1, L3_ffn_b1, L3_ffn_w2, L3_ffn_b2)
    return x

_drawn_inputs = setup_inputs


def setup_inputs(seed=0):
    import zlib

    import numpy as np

    out = dict(_drawn_inputs(seed))
    spreads = {'L2_xattn_bq': (0.0, 0.547),
     'L2_xattn_bk': (0.0, 2.0),
     'L2_xattn_bv': (0.0, 0.314),
     'L3_ffn_b1': (0.0, 2.0),
     'L3_ffn_b2': (0.0, 2.0)}
    factors = {'L1_ffn_fast_b': 8.0,
     'L1_ffn_u': 8.0,
     'L1_ffn_v': 8.0,
     'L3_xattn_Wq': 7.634,
     'L3_xattn_bq': 45.059,
     'L3_xattn_Wk': 7.363,
     'L3_xattn_bk': 64.0,
     'L3_xattn_bv': 27.288,
     'L3_xattn_bo': 25.092}
    for name, (base, spread) in spreads.items():
        noise = np.random.default_rng([zlib.crc32(name.encode()), seed]).standard_normal(out[name].shape)
        drawn = base * np.exp(spread * noise) if base else spread * noise
        out[name] = jnp.asarray(drawn.astype(out[name].dtype))
    for name, factor in factors.items():
        out[name] = (out[name] * factor).astype(out[name].dtype)
    return out
```

```python
from contextlib import ExitStack

import numpy as np
import concourse.bass as bass
from concourse import mybir

F32 = mybir.dt.float32
BF16 = mybir.dt.bfloat16
I32 = mybir.dt.int32
ALU = mybir.AluOpType
ACT = mybir.ActivationFunctionType
AX = mybir.AxisListType

N = 2048
D = 256
M = 1601
NT = N // 128
KT = 13
KROWS = [128] * 12 + [M - 12 * 128]
CHUNKS = [(0, 401), (401, 400), (801, 400), (1201, 400)]
BIG = 2.0 ** 100
LN_EPS = 1e-5


class Queue:

    def __init__(self, sem):
        self.sem = sem
        self.count = 0
        self.items = []
        self.passed = {}

    def wait(self, *tokens):
        for sem, value in tokens:
            if self.passed.get(sem, 0) < value:
                self.passed[sem] = value
                self.items.append(lambda e, s=sem, v=value: e.wait_ge(s, v))

    def do(self, fn, *after, inc=True):
        self.wait(*after)
        if not inc:
            self.items.append(fn)
            return None
        self.count += 1
        self.items.append(lambda e: fn(e).then_inc(self.sem, 1))
        return (self.sem, self.count)

    def last(self):
        return (self.sem, self.count)

    def play(self, engine):
        for item in self.items:
            item(engine)


class Landing:

    def __init__(self, sem):
        self.sem = sem
        self.count = 0

    def start(self, queue, out, in_, *after):
        queue.wait(*after)
        self.count += 16
        queue.items.append(lambda e: e.dma_start(out, in_).then_inc(self.sem, 16))
        return (self.sem, self.count)


class Slots:

    def __init__(self, views):
        self.views = views
        self.free = [()] * len(views)
        self.at = -1

    def take(self):
        self.at = (self.at + 1) % len(self.views)
        return self.at, self.views[self.at], self.free[self.at]


def build(nc, a, out, phases=99):
    with ExitStack() as ctx:
        sems = {}

        def sem(name):
            sems[name] = ctx.enter_context(nc.semaphore(name))
            return sems[name]

        pe, act, dve, pool, sp = (Queue(sem(n)) for n in ("s_pe", "s_act", "s_dve", "s_pool", "s_sp"))
        engines = (pe, act, dve, pool, sp)
        landings = []

        def landing(name):
            landings.append(Landing(sem(name)))
            return landings[-1]

        def barrier():
            ends = [q.last() for q in (pe, act, dve, pool)] + [(x.sem, x.count) for x in landings]
            for q in engines:
                q.wait(*[t for t in ends if t[1]])

        def pooled(fn, *after):
            return pool.do(fn, *([pool.last()] if pool.count else []), *after)

        def sb(scope, name, shape, dt):
            return scope.enter_context(nc.sbuf_tensor(name, shape, dt))

        PS = ctx.enter_context(nc.psum_tensor("PS", [128, 8, 512], F32))
        X = sb(ctx, "X", [128, NT, D], F32)
        xnT = sb(ctx, "xnT", [128, 2, N], F32)
        identf = sb(ctx, "identf", [128, 128], F32)
        identb = sb(ctx, "identb", [128, 128], BF16)
        onesf = sb(ctx, "onesf", [128, 128], F32)
        onesb = sb(ctx, "onesb", [128, 128], BF16)
        mv = sb(ctx, "mv", [128, NT, 2], F32)
        st = sb(ctx, "st", [128, NT, 6], F32)
        rstd = sb(ctx, "rstd", [128, NT], F32)
        xg = sb(ctx, "xg", [128, 4, D], F32)
        rden = sb(ctx, "rden", [128, 4, 4], F32)
        rr = sb(ctx, "rr", [128, 20], F32)
        big = sb(ctx, "big", [128, 4096], F32)
        ctxT = big[:, 0:2 * M].rearrange("p (h n) -> p h n", h=2)
        trash = sb(ctx, "trash", [128, 2, 401], BF16)

        l_x = landing("l_x")
        l_c = landing("l_c")
        l_w = landing("l_w")
        l_out = landing("l_out")

        x_v = a["x"].rearrange("(t p) d -> p t d", p=128)
        out_v = out.rearrange("(t p) d -> p t d", p=128)
        t_x = [l_x.start(sp, X[:, 4 * g:4 * g + 4, :], x_v[:, 4 * g:4 * g + 4, :]) for g in range(4)][-1]

        t_ctx = l_c.start(sp, ctxT, a["ctxT"].rearrange("(h p) n -> p h n", p=128))
        i0 = pooled(lambda e: e.memset(identf[:], 0.0))
        i1 = pooled(lambda e: e.memset(onesf[:], 1.0))
        i2 = pooled(lambda e: e.memset(onesb[:], 1.0))
        i3 = pooled(lambda e: e.affine_select(out=identf[:], in_=identf[:], compare_op=ALU.not_equal, fill=1.0,
                                               base=0, pattern=[[-1, 128]], channel_multiplier=1), i0)
        t_const = pooled(lambda e: e.tensor_copy(identb[:], identf[:]), i3)
        for q in (pe, act, dve):
            q.wait(t_const)

        x_ready = [t_x] * NT

        def bank(b):
            return PS[:, b, :]

        def mm(o, lhsT, rhs, start, stop, *after, inc=False, loose=False):
            return pe.do(lambda e: e.matmul(o, lhsT, rhs, start=start, stop=stop, skip_group_check=loose), *after,
                         inc=inc)

        def pull(gen, n):
            for _ in range(n):
                if next(gen, None) is None:
                    return

        class Background:

            def __init__(self):
                self.gens = []
                self.rate = 0.0
                self.due = 0.0

            def add(self, *gens):
                self.gens += gens

            def step(self):
                while self.gens:
                    if next(self.gens[0], None) is not None:
                        return
                    self.gens.pop(0)

            def tick(self):
                self.due += self.rate
                while self.due >= 1.0:
                    self.due -= 1.0
                    self.step()

            def flush(self):
                while self.gens:
                    self.step()

        def weave(*parts):
            parts = [[gen, n, lo, hi, 0] for gen, n, lo, hi in parts]
            while parts:
                part = min(parts, key=lambda q: q[2] + (q[3] - q[2]) * (q[4] + 0.5) / q[1])
                part[4] += 1
                if next(part[0], None) is None:
                    parts.remove(part)
                else:
                    yield 1

        def late(fn, args):
            yield from fn(*args)

        def take(gen, n):
            for _ in range(n):
                v = next(gen, None)
                if v is None:
                    return
                yield v

        ln = {"on": True, "rms": False, "ready": None, "x_free": (), "done": 0}

        def norm_group(g, ring, *xn_free):
            if not ln["on"]:
                return
            ln["done"] += 1
            ts = slice(4 * g, 4 * g + 4)
            toks = [dve.do(lambda e, t=t: e.bn_stats(st[:, t, :], X[:, t, :]), x_ready[t])
                    for t in range(4 * g, 4 * g + 4)]
            for t in range(4 * g, 4 * g + 4):
                a2 = dve.do(lambda e, t=t: e.bn_aggr(mv[:, t, :], st[:, t, :]), toks[t - 4 * g])
            v1 = dve.do(lambda e: e.tensor_scalar(rstd[:, ts], mv[:, ts, 1], LN_EPS, None, ALU.add), a2)
            v2 = act.do(lambda e: e.activation(rstd[:, ts], rstd[:, ts], ACT.Sqrt), v1)
            yield 1
            v3 = dve.do(lambda e: e.reciprocal(rstd[:, ts], rstd[:, ts]), v2)
            n = []
            for i in range(4):
                t = 4 * g + i
                n.append(dve.do(lambda e, t=t, i=i: e.tensor_scalar(
                    xg[:, i, :], X[:, t, :], mv[:, t, 0:1], rstd[:, t:t + 1], ALU.subtract, ALU.mult),
                    v3, *ln["x_free"]))
            if ln["rms"]:
                for i in range(4):
                    n[i] = dve.do(lambda e, i=i: e.tensor_tensor_reduce(
                        trash[:, 0, 0:D], xg[:, i, :], xg[:, i, :], 1.0, 0.0, ALU.mult, ALU.add,
                        rr[:, i:i + 1]), n[i], dve.last())
                r1 = dve.do(lambda e: e.tensor_scalar(rr[:, 4:8], rr[:, 0:4], 1.0 / D, None, ALU.mult), n[3])
                r2 = act.do(lambda e: e.activation(rr[:, 8:12], rr[:, 4:8], ACT.Sqrt), r1)
                r3 = dve.do(lambda e: e.tensor_scalar(rr[:, 12:16], rr[:, 8:12], 1e-8, None, ALU.add), r2)
                r4 = dve.do(lambda e: e.reciprocal(rr[:, 16:20], rr[:, 12:16]), r3)
                for i in range(4):
                    n[i] = dve.do(lambda e, i=i: e.tensor_scalar(
                        xg[:, i, :], xg[:, i, :], rr[:, 16 + i:17 + i], None, ALU.mult), r4)
            yield 1
            for hf in range(2):
                b, ps, free = ring.take()
                for i in range(4):
                    last = pe.do(lambda e, ps=ps, i=i, hf=hf: e.transpose(
                        ps[:, i * 128:(i + 1) * 128], xg[:, i, hf * 128:(hf + 1) * 128], identf[:]),
                        n[i], *free, inc=(i == 3))
                ev = act.do(lambda e, ps=ps, hf=hf: e.activation(
                    xnT[:, hf, g * 512:(g + 1) * 512], ps, ACT.Copy), last, *xn_free)
                ring.free[b] = (ev,)
                yield 1
            ln["x_free"] = (last,)
            ln["ready"] = ev

        def normalised():
            ring = Slots([bank(6), bank(7)])
            for g in range(ln["done"], 4):
                pull(norm_group(g, ring), 99)
            ln["done"] = 0
            return ln["ready"]

        def add_residual(t, ps, *after):
            x_ready[t] = dve.do(lambda e: e.tensor_tensor(X[:, t, :], ps, X[:, t, :], ALU.add), *after, x_ready[t])
            return x_ready[t]

        def head_max(tile_of, ring, pm, masks):
            for idx, (lhs, rhs_of, mb) in tile_of:
                for c, (k0, kn) in enumerate(CHUNKS):
                    b, ps, free = ring.take()
                    pairs = list(zip(lhs, rhs_of(k0, kn)))
                    for j, (l, r) in enumerate(pairs):
                        tok = mm(ps[:, 0:kn], l, r, j == 0, j == len(pairs) - 1, *free, inc=(j == len(pairs) - 1))
                    o = pm[:, idx * 4 + c:idx * 4 + c + 1]
                    if masks is None:
                        red = dve.do(lambda e, o=o, ps=ps, kn=kn: e.tensor_reduce(o, ps[:, 0:kn], AX.X, ALU.max), tok)
                    else:
                        s = trash_at[0] % 2
                        trash_at[0] += 1
                        red = dve.do(lambda e, o=o, ps=ps, kn=kn, k0=k0, mb=mb, s=s: e.tensor_tensor_reduce(
                            trash[:, s, 0:kn], ps[:, 0:kn], mb[0][:, k0:k0 + kn], 1.0, -3.0e38, ALU.add, ALU.max, o),
                            tok, mb[1], *trash_free[s])
                        trash_free[s] = (red,)
                    ring.free[b] = (red,)
                    yield red

        trash_at = [0]
        trash_free = [(), ()]

        def max_rows(n, pm, mx, nm, before):
            m0 = dve.do(lambda e: e.tensor_reduce(mx[:, 0:n], pm[:, 0:4 * n].rearrange("p (n c) -> p n c", c=4),
                                                  AX.X, ALU.max), dve.last(), *before)
            m1 = dve.do(lambda e: e.tensor_scalar(nm[:, 0:n, 0], mx[:, 0:n], -1.0, None, ALU.mult), m0)
            return dve.do(lambda e: e.scalar_tensor_tensor(out=nm[:, 0:n, 1], in0=mx[:, 0:n], scalar=-1.0,
                                                           in1=nm[:, 0:n, 0], op0=ALU.mult, op1=ALU.subtract), m1)

        def l0_attention(scope):
            wqk = sb(scope, "wqk0", [128, 2, 2, 2, 256], F32)
            wv = sb(scope, "wv0", [128, 2, 512], F32)
            wo = sb(scope, "wo0", [128, 4, D], F32)
            bo = sb(scope, "bo0", [1, D], F32)
            Q1 = sb(scope, "Q1", [128, 2, 2, N], BF16)
            Q2 = sb(scope, "Q2", [66, 2, 2, N], BF16)
            K1 = sb(scope, "K1", [128, 2, 2, M], BF16)
            K2 = sb(scope, "K2", [66, 2, 2, M], BF16)
            V = sb(scope, "V0", [128, KT, 512], F32)
            P = sb(scope, "P0", [128, 4, 2, 512], F32)
            On = sb(scope, "On0", [128, 2, 512], F32)
            acc = sb(scope, "acc0", [128, 2, 2, 512], F32)
            R = sb(scope, "R0", [128, 512], F32)
            pm = sb(scope, "pm0", [128, 2, 32], F32)
            mx = sb(scope, "mx0", [128, 2, 8], F32)
            nm = sb(scope, "nm0", [128, 2, 8, 2], BF16)
            l_qk = [landing(f"l_qk{i}") for i in range(2)]
            w_free = [(), ()]
            w_ready = {}

            def load_qk(p):
                s = p % 2
                for i, n in enumerate(("L0_WqD", "L0_WkD")):
                    w_ready[p] = l_qk[s].start(
                        sp, wqk[:, s, i, :, :],
                        a[n].rearrange("(h p) n -> p h n", p=128)[:, :, p * 256:(p + 1) * 256], *w_free[s])

            l_w.start(sp, wv[:], a["L0_xattn_Wv"].rearrange("(h p) n -> p h n", p=128))
            load_qk(0)
            load_qk(1)
            l_w.start(sp, wo[:], a["L0_xattn_Wo"].rearrange("(h p) n -> p h n", p=128))
            tw = l_w.start(sp, bo[:], a["L0_xattn_bo"])
            for s in range(2):
                ones_k = pooled(lambda e, s=s: e.memset(K2[64:66, s, :, :], 1.0))
            ring = Slots([bank(4), bank(5), bank(7)])
            pe.wait(t_ctx, tw, ones_k)
            v_ready = []
            for kt in range(KT):
                r = KROWS[kt]
                b, ps, free = ring.take()
                for hf in range(2):
                    tok = mm(ps[0:r, :], ctxT[:, hf, kt * 128:kt * 128 + r], wv[:, hf, :], hf == 0, hf == 1, *free,
                             inc=(hf == 1))
                ev = act.do(lambda e, ps=ps, r=r, kt=kt: e.activation(V[0:r, kt, :], ps[0:r, :], ACT.Copy), tok)
                ring.free[b] = (ev,)
                v_ready.append(ev)
            t_xn = normalised()
            stack_ready = {}
            stack_free = {0: (), 1: ()}
            xn_read = [None]

            def prepare(p):
                s = p % 2
                free_s = stack_free[s]
                toks = {}
                for hh in range(2):
                    for qb in range(4):
                        b, ps, free = ring.take()
                        for hf in range(2):
                            tok = mm(ps, wqk[:, s, 0, hf, hh * 128:(hh + 1) * 128],
                                     xnT[:, hf, qb * 512:(qb + 1) * 512], hf == 0, hf == 1, *free, t_xn, w_ready[p],
                                     inc=(hf == 1))
                        q1 = Q1[:, s, hh, qb * 512:(qb + 1) * 512]
                        q2 = Q2[0:64, s, hh, qb * 512:(qb + 1) * 512]
                        e1 = act.do(lambda e, q1=q1, ps=ps: e.activation(q1, ps, ACT.Copy), tok, *free_s)
                        e2 = dve.do(lambda e, q1=q1, q2=q2, ps=ps: e.tensor_tensor(
                            q2, ps[0:64, :], q1[0:64, :], ALU.subtract), e1)
                        ring.free[b] = (e2,)
                        toks["q"] = e2
                        xn_read[0] = tok
                        yield 1
                    for c, (k0, kn) in enumerate(CHUNKS):
                        b, ps, free = ring.take()
                        for hf in range(2):
                            tok = mm(ps[:, 0:kn], wqk[:, s, 1, hf, hh * 128:(hh + 1) * 128], ctxT[:, hf, k0:k0 + kn],
                                     hf == 0, hf == 1, *free, inc=(hf == 1))
                        k1 = K1[:, s, hh, k0:k0 + kn]
                        k2 = K2[0:64, s, hh, k0:k0 + kn]
                        e1 = act.do(lambda e, k1=k1, ps=ps, kn=kn: e.activation(k1, ps[:, 0:kn], ACT.Copy), tok,
                                    *free_s)
                        e2 = dve.do(lambda e, k1=k1, ps=ps, kn=kn: e.tensor_tensor(
                            k1[64:128, :], ps[64:128, 0:kn], k1[64:128, :], ALU.subtract), e1)
                        e3 = pooled(lambda e, k1=k1, k2=k2: e.tensor_copy(k2, k1[0:64, :]), e1)
                        ring.free[b] = (e2,)
                        toks["k"] = (e2, e3)
                        yield 1
                w_free[s] = (tok,)
                stack_ready[p] = [toks["q"], *toks["k"]]
                if p + 2 < 4:
                    load_qk(p + 2)

            unit_ready = {}
            nm_free = {0: (), 1: ()}

            def maxima(p, qb):
                s = p % 2
                u = (4 * p + qb) % 2
                pe.wait(*stack_ready[p])
                tiles = []
                for hh in range(2):
                    for qt in range(4):
                        q0 = qb * 512 + qt * 128
                        tiles.append((hh * 4 + qt, ([Q1[:, s, hh, q0:q0 + 128]],
                                                    lambda k0, kn, hh=hh: [K1[:, s, hh, k0:k0 + kn]], None)))
                yield from head_max(tiles, ring, pm[:, u, :], None)
                tn = max_rows(8, pm[:, u, :], mx[:, u, :], nm[:, u, :, :], nm_free[u])
                for _ in range(4):
                    yield 1
                for hh in range(2):
                    b, ps, free = ring.take()
                    for qt in range(4):
                        tok = mm(ps[64:66, qt * 128:(qt + 1) * 128], nm[:, u, hh * 4 + qt, :], identb[:], True, True,
                                 *free, tn, inc=(qt == 3))
                    ev = act.do(lambda e, ps=ps, hh=hh: e.activation(
                        Q2[64:66, s, hh, qb * 512:(qb + 1) * 512], ps[64:66, :], ACT.Copy), tok)
                    ring.free[b] = (ev,)
                    yield 1
                nm_free[u] = (tok,)
                unit_ready[p, qb] = ev

            S = Slots([(0, 1), (2, 3)])
            Ps = Slots([0, 1, 2, 3])
            o_free = [()]
            on_free = {0: (), 1: ()}
            r_free = [()]
            bg = Background()

            def scores(p, qb, kt):
                s = p % 2
                r = KROWS[kt]
                i, banks, free = S.take()
                q = qb * 512
                for hh in range(2):
                    mm(bank(banks[hh])[0:r, :], K1[:, s, hh, kt * 128:kt * 128 + r], Q1[:, s, hh, q:q + 512],
                       True, False, *free, unit_ready[p, qb])
                    tok = mm(bank(banks[hh])[0:r, :], K2[:, s, hh, kt * 128:kt * 128 + r], Q2[:, s, hh, q:q + 512],
                             False, True, inc=(hh == 1))
                    bg.tick()
                j, _, pfree = Ps.take()
                ex = act.do(lambda e, banks=banks, r=r, j=j: e.activation(
                    P[0:r, j, :, :], PS[0:r, banks[0]:banks[0] + 2, :], ACT.Exp, scale=0.125), tok, *pfree)
                S.free[i] = (ex,)
                return ex, j, r

            held = []
            acc_free = {0: (), 1: ()}
            acc_at = {}

            def attend(p, qb, kt, ex, j, r):
                u = (4 * p + qb) % 2
                if kt == 0:
                    pe.wait(*o_free[0])
                for hh in range(2):
                    h = 2 * p + hh
                    tok = mm(PS[64 * hh:64 * hh + 64, 6, :], V[0:r, kt, h * 64:(h + 1) * 64], P[0:r, j, hh, :],
                             kt == 0, kt == KT - 1, ex, v_ready[kt], inc=(hh == 1))
                bg.tick()
                if kt == 0:
                    held.append((j, tok, ex))
                    return tok
                if kt == 1:
                    j0, tok0, ex0 = held.pop()
                    at = dve.do(lambda e, j0=j0: e.tensor_tensor(acc[:, u, :, :], P[:, j0, :, :], P[:, j, :, :],
                                                                 ALU.add), ex, ex0, *acc_free[u])
                    Ps.free[j0] = (tok0, at)
                else:
                    at = dve.do(lambda e: e.tensor_tensor(acc[0:r, u, :, :], acc[0:r, u, :, :], P[0:r, j, :, :],
                                                          ALU.add), ex, acc_at[u])
                acc_at[u] = at
                Ps.free[j] = (tok, at)
                bg.tick()
                return tok

            def finish(p, qb, tok):
                u = (4 * p + qb) % 2
                at = acc_at[u]
                c1 = act.do(lambda e: e.activation(On[:, u, :], PS[:, 6, :], ACT.Copy), tok, *on_free[u])
                o_free[0] = (c1,)

                def divide():
                    b, ps, free = ring.take()
                    for hh in range(2):
                        tk = mm(ps[64 * hh:64 * hh + 64, :], onesf[:, 0:64], acc[:, u, hh, :], True, True, *free, at,
                                inc=(hh == 1))
                    acc_free[u] = (tk,)
                    d0 = act.do(lambda e, ps=ps: e.activation(R[:], ps, ACT.Copy), tk, *r_free[0])
                    ring.free[b] = (d0,)
                    yield 1
                    for i in range(4):
                        n = slice(128 * i, 128 * i + 128)
                        d1 = dve.do(lambda e, n=n: e.reciprocal(R[:, n], R[:, n]), d0)
                        yield 1
                    d2 = dve.do(lambda e: e.tensor_tensor(On[:, u, :], On[:, u, :], R[:], ALU.mult), d1, c1)
                    r_free[0] = (d2,)
                    yield 1

                def project():
                    d2 = r_free[0][0]
                    for qt in range(4):
                        b, ps, free = ring.take()
                        tk = mm(ps[:, 0:D], On[:, u, qt * 128:(qt + 1) * 128], wo[:, p, :], True, p != 0, *free,
                                d2, inc=(p != 0))
                        if p == 0:
                            tk = mm(ps[:, 0:D], onesf[0:1, :], bo[:], False, True, inc=True)
                        ring.free[b] = (add_residual(4 * qb + qt, ps[:, 0:D], tk),)
                        yield 1
                    on_free[u] = (tk,)
                    if p == 3:
                        yield from norm_group(qb, ring, xn_read[0])
                return divide(), project()

            pull(prepare(0), 99)
            pull(maxima(0, 0), 99)
            units = [(p, qb) for p in range(4) for qb in range(4)]
            ahead = []
            preps = {}
            for u, (p, qb) in enumerate(units):
                for kt in range(KT):
                    ahead.append(((p, qb, kt), scores(p, qb, kt)))
                    if len(ahead) > 1:
                        (p0, qb0, kt0), got = ahead.pop(0)
                        tok = attend(p0, qb0, kt0, *got)
                    if kt == 0:
                        parts = []
                        if u:
                            dv, pj = finish(p0, qb0, tok)
                            parts += [(dv, 5, 0.03, 0.3), (pj, 8 if p0 == 3 else 4, 0.35, 0.6)]
                            if qb0 == 3:
                                stack_free[p0 % 2] = (tok,)
                        if p < 3 and qb == 0:
                            preps[p + 1] = prepare(p + 1)
                        if p < 3 and qb < 3:
                            parts.append((take(preps[p + 1], 6 if qb < 2 else 99), 6, 0.0, 0.9))
                        if u + 1 < len(units):
                            parts.append((late(maxima, units[u + 1]), 38, 0.0, 0.97))
                        bg.add(weave(*parts))
                        bg.rate = (sum(q[1] for q in parts)) / ((KT - 1) * 4 - 2)
                bg.flush()
            (p0, qb0, kt0), got = ahead.pop(0)
            for gen in finish(p0, qb0, attend(p0, qb0, kt0, *got)):
                pull(gen, 99)

        def l0_experts(scope):
            gw = sb(scope, "gw", [128, 2, 8], F32)
            ex = sb(scope, "ex", [128, 2, 8 * D], F32)
            tri = sb(scope, "tri", [128, 128], I32)
            sel8 = sb(scope, "sel8", [128, 64], BF16)
            sel8f = sb(scope, "sel8f", [128, 64], F32)
            base = sb(scope, "base", [128, 128], F32)
            ecode = sb(scope, "ecode", [128, 128], F32)
            G = sb(scope, "G", [128, NT, 8], F32)
            cs = sb(scope, "cs", [128, 8], F32)
            rc = sb(scope, "rc", [128, 8], F32)
            rs = sb(scope, "rs", [128, NT], F32)
            rr_ = sb(scope, "rr_", [128, NT], F32)
            Ge = sb(scope, "Ge", [128, 8, NT], F32)
            GT = sb(scope, "GT", [128, 128], F32)
            W = sb(scope, "Wg", [128, 8, N], F32)
            ind = sb(scope, "ind", [128, 3, N], BF16)
            cnt = sb(scope, "cnt", [128, NT, 8], F32)
            ccs = sb(scope, "ccs", [8, N], F32)
            rk = sb(scope, "rk", [128, NT, 8], F32)
            sl = sb(scope, "sl", [128, NT, 8], F32)
            best = sb(scope, "best", [128, NT], F32)
            w = sb(scope, "w8", [128, NT, 8], F32)
            gs = nc.dram_tensor("gate_rows", [8, N], F32, kind="Internal").ap()
            l_g = landing("l_g")
            l_b = [landing(f"l_b{e}") for e in range(8)]
            l_w.start(sp, gw[:], a["L0_ffn_gate_w"].rearrange("(h p) n -> p h n", p=128))
            for e_ in range(8):
                l_w.start(sp, ex[:, :, e_ * D:(e_ + 1) * D], a["L0_ffn_experts"][e_].rearrange("(h p) n -> p h n", p=128))
            l_w.start(sp, tri[:], a["c_tri"])
            l_w.start(sp, sel8f[:], a["c_sel8"])
            l_w.start(sp, base[:], a["c_base"])
            tw = l_w.start(sp, ecode[:], a["c_ecode"])
            t_xn = normalised()
            dve.wait(tw)
            t_sel = dve.do(lambda e: e.tensor_copy(sel8[:], sel8f[:]))
            pe.wait(tw, t_xn, t_sel)
            for t in range(NT):
                for hf in range(2):
                    tok = mm(PS[:, 0, t * 8:(t + 1) * 8], xnT[:, hf, t * 128:(t + 1) * 128], gw[:, hf, :], hf == 0,
                             hf == 1, inc=(t == NT - 1 and hf == 1))
            g = dve.do(lambda e: e.tensor_scalar(G[:], PS[:, 0, 0:128].rearrange("p (t e) -> p t e", e=8), 1e-6,
                                                 None, ALU.max), tok)
            for _ in range(8):
                c0 = dve.do(lambda e: e.tensor_reduce(cs[:], G[:].rearrange("p t e -> p e t"), AX.X, ALU.add), g)
                c1 = mm(PS[:, 1, 0:8], onesf[:], cs[:], True, True, c0, inc=True)
                c2 = dve.do(lambda e: e.reciprocal(rc[:], PS[:, 1, 0:8]), c1)
                c3 = dve.do(lambda e: e.tensor_tensor(G[:], G[:], rc[:].unsqueeze(1).to_broadcast([128, NT, 8]),
                                                      ALU.mult), c2)
                c4 = dve.do(lambda e: e.tensor_reduce(rs[:], G[:], AX.X, ALU.add), c3)
                c5 = dve.do(lambda e: e.reciprocal(rr_[:], rs[:]), c4)
                g = dve.do(lambda e: e.tensor_tensor(G[:], G[:], rr_[:].unsqueeze(2).to_broadcast([128, NT, 8]),
                                                     ALU.mult), c5)
            g1 = dve.do(lambda e: e.tensor_copy(Ge[:], G[:].rearrange("p t e -> p e t")), g)
            g2 = pe.do(lambda e: e.transpose(PS[:, 2, 0:128], Ge[:].rearrange("p e t -> p (e t)"), identf[:]), g1)
            g3 = act.do(lambda e: e.activation(GT[:], PS[:, 2, 0:128], ACT.Copy), g2)
            g4 = l_g.start(sp, gs.rearrange("e (t n) -> (e t) n", n=128), GT[:], g3)
            here = [l_b[e_].start(sp, W[:, e_, :], gs[e_:e_ + 1, :].to_broadcast([128, N]), g4) for e_ in range(8)]
            ring = Slots([0, 1, 2])
            cc_bank = [0, 1, 2, 3]
            opened = set()
            first_waits = [dve.last(), act.last()]
            pe.wait(*first_waits)
            total = NT - 1
            for t in range(NT):
                for e_ in range(8):
                    blk = W[:, e_, t * 128:(t + 1) * 128].bitcast(I32)
                    b1 = dve.do(lambda e, blk=blk: e.tensor_tensor(blk, blk, tri[:], ALU.add), here[e_])
                    i, _, free = ring.take()
                    n = N - 128 * t
                    b2 = dve.do(lambda e, e_=e_, t=t, i=i, n=n: e.tensor_scalar(
                        ind[:, i, 0:n], W[:, e_, t * 128:N], G[:, t, e_:e_ + 1], 0.0, ALU.is_gt, ALU.add,
                        accum_out=cnt[:, t, e_:e_ + 1]), b1, *free)
                    tok = None
                    for b in range(4):
                        lo = max(512 * b, 128 * (t + 1))
                        if lo >= 512 * (b + 1):
                            continue
                        hi = 512 * (b + 1)
                        lasttile = (hi // 128 - 2 == t) and e_ == 7
                        tok = mm(PS[0:8, cc_bank[b], lo - 512 * b:512], sel8[:, e_ * 8:(e_ + 1) * 8],
                                 ind[:, i, lo - 128 * t:hi - 128 * t], b not in opened, lasttile, b2,
                                 inc=True, loose=True)
                        opened.add(b)
                    ring.free[i] = (tok,) if tok else (b2,)
            e1 = act.do(lambda e: e.activation(ccs[:, 128:N], PS[0:8, 0:4, :].rearrange("p b n -> p (b n)")[:, 128:N],
                                               ACT.Copy), pe.last())
            for t in range(1, NT):
                e2 = pe.do(lambda e, t=t: e.transpose(PS[:, 4, t * 8:(t + 1) * 8], ccs[:, t * 128:(t + 1) * 128],
                                                      identf[0:8, 0:8]), e1)
            bs = base[:].rearrange("p (t e) -> p t e", e=8)
            r0 = dve.do(lambda e: e.tensor_tensor(rk[:], cnt[:], bs, ALU.add), dve.last())
            r1 = dve.do(lambda e: e.tensor_tensor(rk[:, 1:NT, :], rk[:, 1:NT, :],
                                                  PS[:, 4, 8:128].rearrange("p (t e) -> p t e", e=8), ALU.subtract),
                        r0, e2)
            r2 = dve.do(lambda e: e.tensor_scalar(sl[:], rk[:], 255.5, None, ALU.is_lt), r1)
            r3 = dve.do(lambda e: e.scalar_tensor_tensor(out=rk[:], in0=rk[:], scalar=8.0,
                                                         in1=ecode[:].rearrange("p (t e) -> p t e", e=8),
                                                         op0=ALU.mult, op1=ALU.add), r2)
            r4 = dve.do(lambda e: e.tensor_tensor(rk[:], rk[:], sl[:], ALU.mult), r3)
            r5 = dve.do(lambda e: e.tensor_reduce(best[:], rk[:], AX.X, ALU.max), r4)
            r6 = dve.do(lambda e: e.tensor_tensor(w[:], rk[:], best[:].unsqueeze(2).to_broadcast([128, NT, 8]),
                                                  ALU.is_equal), r5)
            r7 = dve.do(lambda e: e.tensor_tensor(w[:], w[:], sl[:], ALU.mult), r6)
            r8 = dve.do(lambda e: e.tensor_tensor(w[:], w[:], G[:], ALU.mult), r7)
            ring = Slots([bank(b) for b in (5, 6, 7)])
            for t in range(NT):
                for pr in range(4):
                    b, ps, free = ring.take()
                    for hf in range(2):
                        tok = mm(ps, xnT[:, hf, t * 128:(t + 1) * 128], ex[:, hf, pr * 512:(pr + 1) * 512], hf == 0,
                                 hf == 1, *free, inc=(hf == 1))
                    for j in range(2):
                        x_ready[t] = dve.do(lambda e, t=t, pr=pr, j=j, ps=ps: e.scalar_tensor_tensor(
                            out=X[:, t, :], in0=ps[:, j * D:(j + 1) * D], scalar=w[:, t, 2 * pr + j:2 * pr + j + 1],
                            in1=X[:, t, :], op0=ALU.mult, op1=ALU.add), tok, r8, x_ready[t])
                    ring.free[b] = (x_ready[t],)

        def single_attention(scope, layer, masked, biased):
            L = f"L{layer}_xattn_"
            wt = {n: sb(scope, n + L, [128, 2, D], F32) for n in ("Wq", "Wk", "Wv")}
            qT = sb(scope, "qT" + L, [128, 2, N], F32)
            kT = sb(scope, "kT" + L, [128, 2, M], F32)
            qh = sb(scope, "qh" + L, [128, 2, N], BF16)
            kh = sb(scope, "kh" + L, [128, 2, M], BF16)
            V = sb(scope, "V" + L, [128, KT, D + 1], F32)
            P = sb(scope, "P" + L, [128, 3, 512], F32)
            mrow = sb(scope, "mrow" + L, [2, N], BF16)
            pm = sb(scope, "pm" + L, [128, 2, 16], F32)
            mx = sb(scope, "mx" + L, [128, 2, 4], F32)
            nm = sb(scope, "nm" + L, [128, 2, 4, 2], BF16)
            for n in wt:
                tw = l_w.start(sp, wt[n][:], a[L + n + "T"].rearrange("(h p) n -> p h n", p=128))
            if biased:
                bq = sb(scope, "bq" + L, [128, 2], F32)
                bk = sb(scope, "bk" + L, [128, 2], F32)
                bv = sb(scope, "bv" + L, [1, D], F32)
                l_w.start(sp, bq[:], a[L + "bq"])
                l_w.start(sp, bk[:], a[L + "bk"])
                tw = l_w.start(sp, bv[:], a[L + "bv"])
            ones_v = pooled(lambda e: e.memset(V[:, :, D:D + 1], 1.0))
            mb_ready = [None] * NT
            mb = load_mask(scope, L, a["mask1"], mb_ready) if masked else None
            t_xn = normalised()
            pe.wait(tw, t_xn, ones_v)
            act.wait(tw)
            dve.wait(tw)
            ring = Slots([bank(4), bank(5)])
            q_ready, k_ready = [], []
            for (src, w_, o, oh, bias, chunks, ready) in (
                    (ctxT, wt["Wk"], kT, kh, "bk", CHUNKS, k_ready),
                    (xnT, wt["Wq"], qT, qh, "bq", [(i * 512, 512) for i in range(4)], q_ready)):
                for c0, cn in chunks:
                    for half in range(2):
                        b, ps, free = ring.take()
                        for hf in range(2):
                            tok = mm(ps[:, 0:cn], w_[:, hf, half * 128:(half + 1) * 128], src[:, hf, c0:c0 + cn],
                                     hf == 0, hf == 1, *free, inc=(hf == 1))
                        o_ = o[:, half, c0:c0 + cn]
                        oh_ = oh[:, half, c0:c0 + cn]
                        if biased:
                            bb = (bq if bias == "bq" else bk)[:, half:half + 1]
                            e1 = dve.do(lambda e, o_=o_, ps=ps, cn=cn, bb=bb: e.tensor_scalar(
                                o_, ps[:, 0:cn], bb, None, ALU.add), tok)
                        else:
                            e1 = dve.do(lambda e, o_=o_, ps=ps, cn=cn: e.tensor_copy(o_, ps[:, 0:cn]), tok)
                        e2 = act.do(lambda e, o_=o_, oh_=oh_: e.activation(oh_, o_, ACT.Copy), e1)
                        ring.free[b] = (e1,)
                    ready.append(e2)
            v_ready = []
            for kt in range(KT):
                r = KROWS[kt]
                b, ps, free = ring.take()
                for hf in range(2):
                    tok = mm(ps[0:r, 0:D], ctxT[:, hf, kt * 128:kt * 128 + r], wt["Wv"][:, hf, :], hf == 0,
                             hf == 1 and not biased, *free, inc=(hf == 1))
                if biased:
                    tok = mm(ps[0:r, 0:D], onesf[0:1, 0:r], bv[:], False, True, inc=True)
                ev = act.do(lambda e, ps=ps, r=r, kt=kt: e.activation(V[0:r, kt, 0:D], ps[0:r, 0:D], ACT.Copy), tok)
                ring.free[b] = (ev,)
                v_ready.append(ev)
            unit_ready = {}
            nm_free = {0: (), 1: ()}

            def maxima(qb):
                u = qb % 2
                pe.wait(q_ready[qb], k_ready[-1])
                tiles = []
                for qt in range(4):
                    q0 = qb * 512 + qt * 128
                    m = (mb[:, 4 * qb + qt, :], mb_ready[4 * qb + qt]) if masked else None
                    tiles.append((qt, ([qh[:, hf, q0:q0 + 128] for hf in range(2)],
                                       lambda k0, kn: [kh[:, hf, k0:k0 + kn] for hf in range(2)], m)))
                yield from head_max(tiles, ring, pm[:, u, :], mb if masked else None)
                tn = max_rows(4, pm[:, u, :], mx[:, u, :], nm[:, u, :, :], nm_free[u])
                b, ps, free = ring.take()
                for qt in range(4):
                    tok = mm(ps[0:2, qt * 128:(qt + 1) * 128], nm[:, u, qt, :], identb[:], True, True, *free, tn,
                             inc=(qt == 3))
                nm_free[u] = (tok,)
                ev = act.do(lambda e, ps=ps: e.activation(mrow[:, qb * 512:(qb + 1) * 512], ps[0:2, :], ACT.Copy),
                            tok)
                ring.free[b] = (ev,)
                unit_ready[qb] = ev
                yield 1

            S = Slots([bank(0), bank(1)])
            Ps = Slots([0, 1, 2])
            obank = [2, 3, 6, 7]
            o_free = [(), (), (), ()]

            def scores(qb, kt):
                r = KROWS[kt]
                i, ps, free = S.take()
                q = qb * 512
                k = kt * 128
                for hf in range(2):
                    mm(ps[0:r, :], kT[:, hf, k:k + r], qT[:, hf, q:q + 512], hf == 0, False, *free, unit_ready[qb])
                tok = mm(ps[0:r, :], onesb[0:2, 0:r], mrow[:, q:q + 512], False, not masked, inc=not masked)
                if masked:
                    for qt in range(4):
                        tok = mm(ps[0:r, qt * 128:(qt + 1) * 128], mb[:, 4 * qb + qt, k:k + r], identb[:], False,
                                 qt == 3, mb_ready[4 * qb + qt], inc=(qt == 3))
                j, _, pfree = Ps.take()
                ex = act.do(lambda e, ps=ps, r=r, j=j: e.activation(P[0:r, j, :], ps[0:r, :], ACT.Exp, scale=0.0625),
                            tok, *pfree)
                S.free[i] = (ex,)
                return ex, j, r

            def attend(qb, kt, ex, j, r):
                for qt in range(4):
                    tok = mm(PS[:, obank[qt], 0:D + 1], P[0:r, j, qt * 128:(qt + 1) * 128], V[0:r, kt, :], kt == 0,
                             kt == KT - 1, ex, v_ready[kt], *(o_free[qt] if kt == 0 else ()), inc=(qt == 3))
                Ps.free[j] = (tok,)
                if kt == KT - 1:
                    for qt in range(4):
                        t = 4 * qb + qt
                        ob = obank[qt]
                        r0 = dve.do(lambda e, ob=ob, qt=qt: e.reciprocal(rden[:, 0, qt:qt + 1], PS[:, ob, D:D + 1]),
                                    tok, dve.last())
                        x_ready[t] = dve.do(lambda e, ob=ob, qt=qt, t=t: e.scalar_tensor_tensor(
                            out=X[:, t, :], in0=PS[:, ob, 0:D], scalar=rden[:, 0, qt:qt + 1], in1=X[:, t, :],
                            op0=ALU.mult, op1=ALU.add), r0, x_ready[t])
                        o_free[qt] = (x_ready[t],)

            pull(maxima(0), 99)
            ahead = []
            steps = [(qb, kt) for qb in range(4) for kt in range(KT)]
            bg = iter(())
            for n, (qb, kt) in enumerate(steps):
                if kt == 0:
                    bg = maxima(qb + 1) if qb < 3 else iter(())
                ahead.append(((qb, kt), scores(qb, kt)))
                pull(bg, 2)
                while ahead and (len(ahead) > 1 or n == len(steps) - 1):
                    s, got = ahead.pop(0)
                    attend(*s, *got)
                if kt == KT - 1:
                    pull(bg, 99)

        def load_mask(scope, L, src, ready, mi=None):
            mb = sb(scope, "mb" + L, [128, NT, M], BF16)
            if mi is None:
                mi = sb(scope, "mi" + L, [128, 2, M], I32)
            l_m = [landing(f"l_m{i}{L}") for i in range(2)]
            free = [(), ()]
            for t in range(NT):
                i = t % 2
                tl = l_m[i].start(sp, mi[:, i, 0:M], src[t * 128:(t + 1) * 128, :], *free[i])
                ready[t] = pooled(lambda e, t=t, i=i: e.tensor_scalar(
                    mb[:, t, :], mi[:, i, 0:M], 0.0, -BIG, ALU.is_equal, ALU.mult), tl)
                free[i] = (ready[t],)
            return mb

        def ternary_rows(scope, tag, wn, rows, cols, inv):
            s = sb(scope, "s" + tag, [128, rows], F32)
            hs = sb(scope, "hs" + tag, [128, 2, rows], F32)
            tm = sb(scope, "tm" + tag, [128, cols], F32)
            last = None
            d0 = dve.do(lambda e: e.tensor_reduce(s[:], wn[:], AX.X, ALU.add, apply_absolute_value=True), dve.last())
            d1 = dve.do(lambda e: e.tensor_scalar(s[:], s[:], inv, 1e-5, ALU.mult, ALU.max), d0)
            d2 = dve.do(lambda e: e.tensor_scalar(hs[:, 0, :], s[:], 0.5, None, ALU.mult), d1)
            d3 = dve.do(lambda e: e.tensor_scalar(hs[:, 1, :], s[:], -0.5, None, ALU.mult), d1)
            for r in range(rows):
                d4 = dve.do(lambda e, r=r: e.tensor_scalar(tm[:], wn[:, r, :], hs[:, 1, r:r + 1], s[:, r:r + 1],
                                                           ALU.is_lt, ALU.mult), d3, d2, dve.last())
                d5 = dve.do(lambda e, r=r: e.tensor_scalar(wn[:, r, :], wn[:, r, :], hs[:, 0, r:r + 1],
                                                           s[:, r:r + 1], ALU.is_gt, ALU.mult), d4)
                last = dve.do(lambda e, r=r: e.tensor_tensor(wn[:, r, :], wn[:, r, :], tm[:], ALU.subtract), d5)
            return last

        def l1_ffn(scope):
            wf = sb(scope, "wf", [128, 8, D], F32)
            wp = sb(scope, "wp", [128, 2, 1024], F32)
            wfT = sb(scope, "wfT", [128, 2, 1024], F32)
            wpT = sb(scope, "wpT", [128, 8, D], F32)
            uT = sb(scope, "uT", [16, 1024], F32)
            vT = sb(scope, "vT", [128, 2, 16], F32)
            bT = sb(scope, "bT", [16, 16], F32)
            gt = sb(scope, "gt", [16, 1], F32)
            z1 = sb(scope, "z1", [16, N], F32)
            z2 = sb(scope, "z2", [16, N], F32)
            r1 = sb(scope, "r1", [128, 3, 512], F32)
            r2 = sb(scope, "r2", [128, 2, 8, 512], F32)
            l_w.start(sp, wf[:], a["L1_ffn_w_fc"].rearrange("(r p) n -> p r n", p=128))
            l_w.start(sp, wp[:], a["L1_ffn_w_proj"].rearrange("(r p) n -> p r n", p=128))
            l_w.start(sp, uT[:], a["L1_ffn_uT"])
            l_w.start(sp, vT[:], a["L1_ffn_vT"].rearrange("(h p) n -> p h n", p=128))
            l_w.start(sp, bT[:], a["L1_ffn_fast_bT"])
            tw = l_w.start(sp, gt[:], a["L1_ffn_gate"].to_broadcast([16, 1]))
            dve.wait(tw)
            pe.wait(tw)
            t1 = ternary_rows(scope, "f", wf, 8, D, 1.0 / D)
            t2 = ternary_rows(scope, "p", wp, 2, 1024, 1.0 / 1024)
            t3 = dve.do(lambda e: e.tensor_scalar(uT[:], uT[:], gt[:, 0:1], None, ALU.mult))
            ring = Slots([bank(b) for b in range(4)])
            for (src, dst, n_out, n_in, tk) in ((wf, wfT, 2, 8, t1), (wp, wpT, 8, 2, t2)):
                for o in range(n_out):
                    for i0_ in range(0, n_in, 4):
                        b, ps, free = ring.take()
                        m = min(4, n_in - i0_)
                        for i in range(m):
                            tok = pe.do(lambda e, ps=ps, i=i, i0_=i0_, o=o, src=src: e.transpose(
                                ps[:, i * 128:(i + 1) * 128], src[:, i0_ + i, o * 128:(o + 1) * 128], identf[:]),
                                tk, *free, inc=(i == m - 1))
                        ev = act.do(lambda e, ps=ps, m=m, o=o, i0_=i0_, dst=dst: e.activation(
                            dst[:, o, i0_ * 128:(i0_ + m) * 128], ps[:, 0:m * 128], ACT.Copy), tok)
                        ring.free[b] = (ev,)
            t_wt = act.last()
            t_xn = normalised()
            pe.wait(t_xn, t_wt, t3)
            up = Slots([bank(b) for b in range(4)])
            down = Slots([bank(b) for b in range(4, 8)])
            for qb in range(4):
                q = slice(qb * 512, (qb + 1) * 512)
                b, ps, free = up.take()
                for hf in range(2):
                    tok = mm(ps[0:16, :], vT[:, hf, :], xnT[:, hf, q], hf == 0, hf == 1, *free, inc=(hf == 1))
                e1 = act.do(lambda e, ps=ps, q=q: e.activation(z1[:, q], ps[0:16, :], ACT.Copy), tok)
                up.free[b] = (e1,)
                b, ps, free = up.take()
                tok = mm(ps[0:16, :], bT[:], z1[:, q], True, True, e1, *free, inc=True)
                e2 = act.do(lambda e, ps=ps, q=q: e.activation(z2[:, q], ps[0:16, :], ACT.Copy), tok)
                up.free[b] = (e2,)
            pe.wait(e2)
            r1s = Slots([0, 1, 2])
            r2_free = [(), ()]
            pend = []

            def rise(qb):
                q = slice(qb * 512, (qb + 1) * 512)
                s = qb % 2
                for f in range(8):
                    b, ps, free = up.take()
                    fs = slice(f * 128, (f + 1) * 128)
                    for hf in range(2):
                        mm(ps, wfT[:, hf, fs], xnT[:, hf, q], hf == 0, False, *free)
                    tok = mm(ps, uT[:, fs], z2[:, q], False, True, inc=True)
                    j, _, rfree = r1s.take()
                    e1 = act.do(lambda e, ps=ps, j=j: e.activation(r1[:, j, :], ps, ACT.Relu), tok, *rfree)
                    up.free[b] = (e1,)
                    e2 = dve.do(lambda e, j=j, s=s, f=f: e.tensor_tensor(r2[:, s, f, :], r1[:, j, :], r1[:, j, :],
                                                                         ALU.mult), e1, *r2_free[s])
                    r1s.free[j] = (e2,)
                return e2

            def fall(qb, tk):
                s = qb % 2
                for qt in range(4):
                    b, ps, free = down.take()
                    for f in range(8):
                        tok = mm(ps[:, 0:D], r2[:, s, f, qt * 128:(qt + 1) * 128], wpT[:, f, :], f == 0, f == 7, tk,
                                 *free, inc=(f == 7))
                    down.free[b] = (add_residual(4 * qb + qt, ps[:, 0:D], tok),)
                r2_free[s] = (tok,)

            tk = rise(0)
            for qb in range(4):
                nx = rise(qb + 1) if qb < 3 else None
                fall(qb, tk)
                tk = nx

        def l2_ffn(scope):
            wu = sb(scope, "wu", [128, 2, 1024], F32)
            wd = sb(scope, "wd", [128, 8, D], F32)
            tm = sb(scope, "tm2", [128, 2048], F32)
            al = sb(scope, "al", [128, 8], F32)
            hT = sb(scope, "hT", [128, 2, 8, 512], F32)
            h2 = sb(scope, "h2", [128, 2, 512], F32)
            ss = sb(scope, "ss", [1, N], F32)
            nr = sb(scope, "nr", [128, NT, 4], F32)
            l_w.start(sp, wu[:], a["L2_ffn_w_upT"].rearrange("(h p) n -> p h n", p=128))
            tw = l_w.start(sp, wd[:], a["L2_ffn_w_downT"].rearrange("(h p) n -> p h n", p=128))
            dve.wait(tw)
            for i, w_ in enumerate((wu, wd)):
                flat = w_[:].rearrange("p a b -> p (a b)")
                d0 = dve.do(lambda e, flat=flat, i=i: e.tensor_reduce(al[:, i:i + 1], flat, AX.X, ALU.add,
                                                                      apply_absolute_value=True), dve.last())
                d1 = mm(PS[:, 0, i:i + 1], onesf[:], al[:, i:i + 1], True, True, d0, inc=True)
                d2 = dve.do(lambda e, i=i: e.tensor_scalar(al[:, 2 + i:3 + i], PS[:, 0, i:i + 1], 0.5 / (1024 * D),
                                                           None, ALU.mult), d1)
                d3 = dve.do(lambda e, i=i: e.tensor_scalar(al[:, 4 + i:5 + i], PS[:, 0, i:i + 1], -0.5 / (1024 * D),
                                                           None, ALU.mult), d1)
                d4 = dve.do(lambda e, flat=flat, i=i: e.tensor_scalar(tm[:], flat, al[:, 4 + i:5 + i], None,
                                                                      ALU.is_lt), d3, d2)
                d5 = dve.do(lambda e, flat=flat, i=i: e.scalar_tensor_tensor(
                    out=flat, in0=flat, scalar=al[:, 2 + i:3 + i], in1=tm[:], op0=ALU.is_gt, op1=ALU.subtract), d4)
            pe.wait(d5)
            ln["rms"] = True
            t_xn = normalised()
            ln["rms"] = False
            pe.wait(t_xn)
            up = Slots([bank(b) for b in range(3)])
            down = Slots([bank(b) for b in range(4, 8)])
            h2s = Slots([0, 1])
            h_free = [(), ()]
            sum_free = [()]

            def rise(qb):
                q = slice(qb * 512, (qb + 1) * 512)
                s = qb % 2
                todo = []
                for f in range(8):
                    b, ps, free = up.take()
                    for hf in range(2):
                        tok = mm(ps, wu[:, hf, f * 128:(f + 1) * 128], xnT[:, hf, q], hf == 0, hf == 1, *free,
                                 inc=(hf == 1))
                    e1 = act.do(lambda e, ps=ps, s=s, f=f: e.activation(hT[:, s, f, :], ps, ACT.Gelu), tok,
                                *h_free[s])
                    up.free[b] = (e1,)
                    j, _, hfree = h2s.take()
                    e2 = dve.do(lambda e, j=j, s=s, f=f: e.tensor_tensor(h2[:, j, :], hT[:, s, f, :], hT[:, s, f, :],
                                                                         ALU.mult), e1, *hfree)
                    todo.append((f, j, e2))
                    if len(todo) == 2 or f == 7:
                        while todo and (len(todo) == 2 or f == 7):
                            f0, j0, e0 = todo.pop(0)
                            tok = mm(PS[0:1, 3, :], onesf[:, 0:1], h2[:, j0, :], f0 == 0, f0 == 7, e0,
                                     *sum_free[0], inc=True)
                            h2s.free[j0] = (tok,)
                ev = act.do(lambda e, q=q: e.activation(ss[:, q], PS[0:1, 3, :], ACT.Copy), tok)
                sum_free[0] = (ev,)
                return e1, ev

            def fall(qb, h_tok, s_tok):
                s = qb % 2
                b, ps, free = down.take()
                ts = slice(4 * qb, 4 * qb + 4)
                for qt in range(4):
                    t = 4 * qb + qt
                    tok = mm(ps[:, qt:qt + 1], ss[:, t * 128:(t + 1) * 128], onesf[0:1, 0:1], True, True, s_tok,
                             *free, inc=(qt == 3))
                n0 = dve.do(lambda e, ps=ps: e.tensor_scalar(nr[:, ts, 0], ps[:, 0:4], 1.0 / 1024, None, ALU.mult),
                            tok)
                down.free[b] = (n0,)
                n1 = act.do(lambda e: e.activation(nr[:, ts, 1], nr[:, ts, 0], ACT.Sqrt), n0)
                n2 = dve.do(lambda e: e.tensor_scalar(nr[:, ts, 2], nr[:, ts, 1], 1e-8, None, ALU.add), n1)
                n3 = dve.do(lambda e: e.reciprocal(nr[:, ts, 3], nr[:, ts, 2]), n2)
                for qt in range(4):
                    t = 4 * qb + qt
                    b, ps, free = down.take()
                    for f in range(8):
                        tok = mm(ps[:, 0:D], hT[:, s, f, qt * 128:(qt + 1) * 128], wd[:, f, :], f == 0, f == 7,
                                 h_tok, *free, inc=(f == 7))
                    x_ready[t] = dve.do(lambda e, t=t, ps=ps: e.scalar_tensor_tensor(
                        out=X[:, t, :], in0=ps[:, 0:D], scalar=nr[:, t, 3:4], in1=X[:, t, :], op0=ALU.mult,
                        op1=ALU.add), tok, n3, x_ready[t])
                    down.free[b] = (x_ready[t],)
                h_free[s] = (tok,)

            tk = rise(0)
            for qb in range(4):
                nx = rise(qb + 1) if qb < 3 else None
                fall(qb, *tk)
                tk = nx

        def l3_attention(scope):
            bq = sb(scope, "bq3", [128, 2], F32)
            bk = sb(scope, "bk3", [128, 2], F32)
            wo = sb(scope, "wo3", [128, 4, D], F32)
            bo = sb(scope, "bo3", [1, D], F32)
            sel = sb(scope, "sel3", [128, 128], F32)
            V = sb(scope, "V3", [128, KT, 272], F32)
            qd = nc.dram_tensor("q_parts", [3, D, N], BF16, kind="Internal").ap()
            kd = nc.dram_tensor("k_parts", [3, D, M], BF16, kind="Internal").ap()
            l_p = landing("l_parts")
            l_w.start(sp, bq[:], a["L3_xattn_bq"])
            l_w.start(sp, bk[:], a["L3_xattn_bk"])
            l_w.start(sp, wo[:], a["L3_WoP"].rearrange("(h p) n -> p h n", p=128))
            l_w.start(sp, bo[:], a["L3_xattn_bo"])
            tw = l_w.start(sp, sel[:], a["c_sel3"])
            ring = Slots([bank(4), bank(5), bank(7)])
            with ExitStack() as tmp:
                wq = sb(tmp, "wq3", [128, 2, D], F32)
                wk = sb(tmp, "wk3", [128, 2, D], F32)
                wv = sb(tmp, "wv3", [128, 2, 272], F32)
                bv = sb(tmp, "bv3", [1, 272], F32)
                T = sb(tmp, "T3", [128, 3, 3, 512], BF16)
                F = sb(tmp, "F3", [128, 3, 512], F32)
                for d, s in ((wk, "L3_xattn_WkT"), (wq, "L3_xattn_WqT"), (wv, "L3_WvP")):
                    l_w.start(sp, d[:], a[s].rearrange("(h p) n -> p h n", p=128))
                tw = l_w.start(sp, bv[:], a["L3_bvP"])
                t_xn = normalised()
                pe.wait(tw, t_xn)
                act.wait(tw)
                dve.wait(tw)
                ts = Slots([0, 1, 2])
                l_t = [landing(f"l_t{i}") for i in range(3)]
                for (src, w_, dd, bias, chunks) in ((ctxT, wk, kd, bk, CHUNKS),
                                                    (xnT, wq, qd, bq, [(i * 512, 512) for i in range(4)])):
                    for c0, cn in chunks:
                        for half in range(2):
                            b, ps, free = ring.take()
                            for hf in range(2):
                                tok = mm(ps[:, 0:cn], w_[:, hf, half * 128:(half + 1) * 128], src[:, hf, c0:c0 + cn],
                                         hf == 0, hf == 1, *free, inc=(hf == 1))
                            j, _, tfree = ts.take()
                            bb = bias[:, half:half + 1]
                            e0 = act.do(lambda e, j=j, ps=ps, cn=cn, bb=bb: e.activation(
                                F[:, j, 0:cn], ps[:, 0:cn], ACT.Identity, bias=bb), tok, *tfree)
                            ring.free[b] = (e0,)
                            e1 = act.do(lambda e, j=j, cn=cn: e.activation(T[:, j, 0, 0:cn], F[:, j, 0:cn], ACT.Copy),
                                        e0, *tfree)
                            e2 = dve.do(lambda e, j=j, cn=cn: e.tensor_tensor(
                                F[:, j, 0:cn], F[:, j, 0:cn], T[:, j, 0, 0:cn], ALU.subtract), e1)
                            e3 = act.do(lambda e, j=j, cn=cn: e.activation(T[:, j, 1, 0:cn], F[:, j, 0:cn], ACT.Copy),
                                        e2)
                            e4 = dve.do(lambda e, j=j, cn=cn: e.tensor_tensor(
                                T[:, j, 2, 0:cn], F[:, j, 0:cn], T[:, j, 1, 0:cn], ALU.subtract), e3)
                            tl = l_t[j].start(sp, dd[:, half * 128:(half + 1) * 128, c0:c0 + cn].rearrange(
                                "s p n -> p s n"), T[:, j, :, 0:cn], e4)
                            ts.free[j] = (tl,)
                for kt in range(KT):
                    r = KROWS[kt]
                    b, ps, free = ring.take()
                    for hf in range(2):
                        mm(ps[0:r, 0:272], ctxT[:, hf, kt * 128:kt * 128 + r], wv[:, hf, :], hf == 0, False, *free)
                    tok = mm(ps[0:r, 0:272], onesf[0:1, 0:r], bv[:], False, True, inc=True)
                    ev = act.do(lambda e, ps=ps, r=r, kt=kt: e.activation(V[0:r, kt, :], ps[0:r, 0:272], ACT.Copy),
                                tok)
                    ring.free[b] = (ev,)
                barrier()
            mb_ready = [None] * NT
            Qs = sb(scope, "Qs", [98, 2, 4, N], BF16)
            Ks = sb(scope, "Ks", [98, 2, 4, M], BF16)
            P = sb(scope, "P3", [128, 4, 2, 512], F32)
            Or = big[:, 0:1024].rearrange("p (u n) -> p u n", u=2)
            Rs = big[:, 1024:2048].rearrange("p (u n) -> p u n", u=2)
            pm = sb(scope, "pm3", [128, 2, 64], F32)
            mx = sb(scope, "mx3", [128, 2, 16], F32)
            nm = sb(scope, "nm3", [128, 2, 16, 2], BF16)
            l_s = [landing(f"l_s{i}") for i in range(2)]
            for i in range(2):
                ones_k = pooled(lambda e, i=i: e.memset(Ks[96:98, i, :, :], 1.0))
            pe.wait(ones_k)
            qparts = (0, 1, 0, 1, 2, 0)
            kparts = (0, 0, 1, 1, 0, 2)
            stack_free = {0: (), 1: ()}
            stack_ready = {}

            def load_stack(g):
                s = g % 2
                for blk in range(6):
                    l_s[s].start(sp, Qs[16 * blk:16 * blk + 16, s, :, :],
                                 qd[qparts[blk], g * 64:(g + 1) * 64, :].rearrange("(h p) n -> p h n", p=16),
                                 *stack_free[s])
                    stack_ready[g] = l_s[s].start(
                        sp, Ks[16 * blk:16 * blk + 16, s, :, :],
                        kd[kparts[blk], g * 64:(g + 1) * 64, :].rearrange("(h p) n -> p h n", p=16))

            load_stack(0)
            mb = load_mask(scope, "L3", a["mask3"], mb_ready, xnT[:].bitcast(I32))
            load_stack(1)
            unit_ready = {}
            nm_free = {0: (), 1: ()}

            def maxima(g, qb):
                s = g % 2
                u = (4 * g + qb) % 2
                pe.wait(stack_ready[g])
                act.wait(stack_ready[g])
                tiles = []
                for h in range(4):
                    for qt in range(4):
                        q0 = qb * 512 + qt * 128
                        t = 4 * qb + qt
                        tiles.append((h * 4 + qt, ([Qs[0:96, s, h, q0:q0 + 128]],
                                                   lambda k0, kn, h=h: [Ks[0:96, s, h, k0:k0 + kn]],
                                                   (mb[:, t, :], mb_ready[t]))))
                yield from head_max(tiles, ring, pm[:, u, :], mb)
                tn = max_rows(16, pm[:, u, :], mx[:, u, :], nm[:, u, :, :], nm_free[u])
                for _ in range(4):
                    yield 1
                for h in range(4):
                    b, ps, free = ring.take()
                    for qt in range(4):
                        tok = mm(ps[96:98, qt * 128:(qt + 1) * 128], nm[:, u, h * 4 + qt, :], identb[:], True, True,
                                 *free, tn, inc=(qt == 3))
                    ev = act.do(lambda e, ps=ps, h=h: e.activation(
                        Qs[96:98, s, h, qb * 512:(qb + 1) * 512], ps[96:98, :], ACT.Copy), tok)
                    ring.free[b] = (ev,)
                    yield 1
                nm_free[u] = (tok,)
                unit_ready[g, qb] = ev

            S = Slots([(0, 1), (2, 3)])
            Ps = Slots([0, 1, 2, 3])
            o_free = [(dve.do(lambda e: e.memset(bank(6), 0.0)),)]
            bg = Background()

            def scores(g, qb, kt, pr):
                s = g % 2
                r = KROWS[kt]
                k = kt * 128
                i, banks, free = S.take()
                for hh in range(2):
                    h = 2 * pr + hh
                    ps = bank(banks[hh])
                    mm(ps[0:r, :], Ks[:, s, h, k:k + r], Qs[:, s, h, qb * 512:(qb + 1) * 512], True, False, *free,
                       unit_ready[g, qb])
                    for qt in range(4):
                        tok = mm(ps[0:r, qt * 128:(qt + 1) * 128], mb[:, 4 * qb + qt, k:k + r], identb[:], False,
                                 qt == 3, mb_ready[4 * qb + qt], inc=(hh == 1 and qt == 3))
                    bg.tick()
                j, _, pfree = Ps.take()
                ex = act.do(lambda e, banks=banks, r=r, j=j: e.activation(
                    P[0:r, j, :, :], PS[0:r, banks[0]:banks[0] + 2, :], ACT.Exp, scale=0.25), tok, *pfree)
                S.free[i] = (ex,)
                return ex, j

            def attend(g, qb, kt, got):
                r = KROWS[kt]
                if kt == 0:
                    pe.wait(*o_free[0])
                for c in range(4):
                    ex, j = got[c // 2]
                    tok = mm(PS[32 * c:32 * c + 17, 6, :], V[0:r, kt, (4 * g + c) * 17:(4 * g + c) * 17 + 17],
                             P[0:r, j, c % 2, :], kt == 0, kt == KT - 1, ex, inc=(c == 3))
                for ex, j in got:
                    Ps.free[j] = (tok,)
                bg.tick()
                return tok

            or_free = {0: (), 1: ()}

            def finish(g, qb, tok):
                u = (4 * g + qb) % 2
                d0 = act.do(lambda e: e.activation(Or[:, u, :], PS[:, 6, :], ACT.Copy), tok, *or_free[u])
                o_free[0] = (d0,)
                done = []

                def divide():
                    b, ps, free = ring.take()
                    tk = mm(ps, sel[:], Or[:, u, :], True, True, *free, d0, inc=True)
                    d1 = act.do(lambda e, ps=ps: e.activation(Rs[:, u, :], ps, ACT.Copy), tk, *or_free[u])
                    ring.free[b] = (d1,)
                    yield 1
                    for i in range(4):
                        n = slice(128 * i, 128 * i + 128)
                        d2 = dve.do(lambda e, n=n: e.reciprocal(Rs[:, u, n], Rs[:, u, n]), d1)
                        yield 1
                    done.append(dve.do(lambda e: e.tensor_tensor(Or[:, u, :], Or[:, u, :], Rs[:, u, :], ALU.mult),
                                       d2, tk))
                    yield 1

                def project():
                    d2 = done[0]
                    for qt in range(4):
                        b, ps, free = ring.take()
                        tk = mm(ps[:, 0:D], Or[:, u, qt * 128:(qt + 1) * 128], wo[:, g, :], True, g != 0, *free, d2,
                                inc=(g != 0))
                        if g == 0:
                            tk = mm(ps[:, 0:D], onesf[0:1, :], bo[:], False, True, inc=True)
                        ring.free[b] = (add_residual(4 * qb + qt, ps[:, 0:D], tk),)
                        yield 1
                    or_free[u] = (tk, d2)
                    if g == 3:
                        yield from norm_group(qb, ring, mb_ready[-1])
                return divide(), project()

            pull(maxima(0, 0), 999)
            units = [(g, qb) for g in range(4) for qb in range(4)]
            ahead = []
            for u, (g, qb) in enumerate(units):
                for kt in range(KT):
                    got = [scores(g, qb, kt, 0)]
                    if ahead:
                        (g0, qb0, kt0), got0 = ahead.pop(0)
                        tok = attend(g0, qb0, kt0, got0)
                    got.append(scores(g, qb, kt, 1))
                    ahead.append(((g, qb, kt), got))
                    if kt == 0:
                        parts = []
                        if u:
                            dv, pj = finish(g0, qb0, tok)
                            parts += [(dv, 6, 0.03, 0.3), (pj, 8 if g0 == 3 else 4, 0.35, 0.6)]
                            if qb0 == 3:
                                stack_free[g0 % 2] = (tok,)
                                if g0 + 2 < 4:
                                    load_stack(g0 + 2)
                        if u + 1 < len(units):
                            parts.append((late(maxima, units[u + 1]), 72, 0.0, 0.97))
                        bg.add(weave(*parts))
                        bg.rate = (sum(q[1] for q in parts)) / ((KT - 1) * 5 - 2)
                bg.flush()
            (g0, qb0, kt0), got0 = ahead.pop(0)
            for gen in finish(g0, qb0, attend(g0, qb0, kt0, got0)):
                pull(gen, 99)

        def l3_ffn(scope):
            w1 = sb(scope, "w1", [128, 3, 2, 1024], F32)
            w2 = sb(scope, "w2", [128, 3, 8, D], F32)
            b1 = sb(scope, "b1", [128, 64], F32)
            b2 = sb(scope, "b2", [1, 8 * D], F32)
            hT = sb(scope, "hT3", [128, 2, 8, 256], F32)
            l_e = [landing(f"l_e{i}") for i in range(3)]
            l_w.start(sp, b1[:], a["L3_ffn_b1"])
            tw = l_w.start(sp, b2[:], a["L3_ffn_b2"])
            w_free = [(), (), ()]
            w_ready = {}

            def load(e_):
                s = e_ % 3
                l_e[s].start(sp, w1[:, s, :, :], a["L3_ffn_w1"][e_].rearrange("(h p) n -> p h n", p=128), *w_free[s])
                w_ready[e_] = l_e[s].start(sp, w2[:, s, :, :],
                                           a["L3_ffn_w2"][e_].rearrange("(h p) n -> p h n", p=128))

            for e_ in range(3):
                load(e_)
            t_xn = normalised()
            pe.wait(tw, t_xn)
            act.wait(tw)
            up = Slots([bank(b) for b in range(4)])
            down = Slots([bank(b) for b in range(4, 8)])
            h_free = [(), ()]

            def rise(e_):
                s = e_ % 2
                for f in range(8):
                    b, ps, free = up.take()
                    for hf in range(2):
                        tok = mm(ps[:, 0:256], w1[:, e_ % 3, hf, f * 128:(f + 1) * 128],
                                 xnT[:, hf, e_ * 256:(e_ + 1) * 256], hf == 0, hf == 1, *free, w_ready[e_],
                                 inc=(hf == 1))
                    e1 = act.do(lambda e, ps=ps, s=s, f=f, e_=e_: e.activation(
                        hT[:, s, f, :], ps[:, 0:256], ACT.Gelu_apprx_tanh, bias=b1[:, e_ * 8 + f:e_ * 8 + f + 1]),
                        tok, *h_free[s])
                    up.free[b] = (e1,)
                return e1

            def fall(e_, tk):
                s = e_ % 2
                for i in range(2):
                    t = 2 * e_ + i
                    b, ps, free = down.take()
                    for f in range(8):
                        mm(ps[:, 0:D], hT[:, s, f, i * 128:(i + 1) * 128], w2[:, e_ % 3, f, :], f == 0, False, tk,
                           *free)
                    tok = mm(ps[:, 0:D], onesf[0:1, :], b2[:, e_ * D:(e_ + 1) * D], False, True, inc=True)
                    down.free[b] = (add_residual(t, ps[:, 0:D], tok),)
                    l_out.start(sp, out_v[:, t, :], X[:, t, :], x_ready[t])
                h_free[s] = (tok,)
                w_free[e_ % 3] = (tok,)

            tk = rise(0)
            for e_ in range(8):
                nx = rise(e_ + 1) if e_ < 7 else None
                fall(e_, tk)
                if e_ + 3 < 8:
                    load(e_ + 3)
                tk = nx

        layers = [l0_attention, l0_experts, lambda s: single_attention(s, 1, True, False), l1_ffn,
                  lambda s: single_attention(s, 2, False, True), l2_ffn, l3_attention, l3_ffn]
        for layer in layers[:phases]:
            with ExitStack() as scope:
                layer(scope)
                barrier()
        if phases < len(layers):
            for t in range(NT):
                l_out.start(sp, out_v[:, t, :], X[:, t, :], x_ready[t])
        sp.wait((l_out.sem, l_out.count))

        block = ctx.enter_context(nc.Block())

        @block.sync
        def _(e):
            sp.play(e)

        @block.gpsimd
        def _(e):
            pool.play(e)

        @block.scalar
        def _(e):
            act.play(e)

        @block.tensor
        def _(e):
            pe.play(e)

        @block.vector
        def _(e):
            dve.play(e)


def arrange(inputs):
    def a(name):
        return np.asarray(inputs[name])

    def T(name):
        return np.ascontiguousarray(a(name).T)

    arrays = {
        "x": a("x").reshape(N, D),
        "ctxT": np.ascontiguousarray(a("ctx_1024").reshape(M, D).T),
        "mask1": a("mask_BxSxS2_ik0").reshape(N, M),
        "mask3": a("mask_1x1xSxS2_ik0").reshape(N, M),
    }
    for n in ("L0_xattn_Wv", "L0_xattn_Wo", "L0_ffn_gate_w", "L0_ffn_experts", "L1_ffn_w_fc", "L1_ffn_w_proj",
              "L3_ffn_w1", "L3_ffn_w2"):
        arrays[n] = a(n)
    for n in ("Wq", "Wk"):
        w = a("L0_xattn_" + n).reshape(D, 8, 1, 64)
        arrays["L0_" + n + "D"] = np.ascontiguousarray(np.broadcast_to(w, (D, 8, 2, 64))).reshape(D, 1024)
    for n in ("L0_xattn_bo", "L2_xattn_bv", "L3_xattn_bo"):
        arrays[n] = a(n).reshape(1, D)
    arrays["L3_ffn_b2"] = a("L3_ffn_b2").reshape(1, 8 * D)
    for n in ("L1_xattn_Wq", "L1_xattn_Wk", "L1_xattn_Wv", "L2_xattn_Wq", "L2_xattn_Wk", "L2_xattn_Wv",
              "L3_xattn_Wq", "L3_xattn_Wk", "L1_ffn_u", "L1_ffn_v", "L1_ffn_fast_b", "L2_ffn_w_up", "L2_ffn_w_down"):
        arrays[n + "T"] = T(n)
    arrays["L1_ffn_gate"] = a("L1_ffn_gate").reshape(1, 1)
    for n in ("L2_xattn_bq", "L2_xattn_bk", "L3_xattn_bq", "L3_xattn_bk"):
        arrays[n] = np.ascontiguousarray(a(n).reshape(2, 128).T)
    arrays["L3_ffn_b1"] = np.ascontiguousarray(a("L3_ffn_b1").reshape(64, 128).T)
    wo = np.zeros((16, 32, D), np.float32)
    wo[:, 0:16, :] = a("L3_xattn_Wo").T.reshape(16, 16, D)
    arrays["L3_WoP"] = wo.reshape(512, D)
    wv = np.zeros((D, 16, 17), np.float32)
    wv[:, :, 0:16] = a("L3_xattn_Wv").T.reshape(D, 16, 16)
    arrays["L3_WvP"] = wv.reshape(D, 272)
    bv = np.zeros((16, 17), np.float32)
    bv[:, 0:16] = a("L3_xattn_bv").reshape(16, 16)
    bv[:, 16] = 1.0
    arrays["L3_bvP"] = bv.reshape(1, 272)
    p = np.arange(128)
    arrays["c_tri"] = (p[None, :] < p[:, None]).astype(np.int32)
    arrays["c_sel3"] = (p[:, None] == 32 * (p[None, :] // 32) + 16).astype(np.float32)
    arrays["c_base"] = np.broadcast_to((128.0 * np.arange(16, dtype=np.float32))[None, :, None],
                                       (128, 16, 8)).reshape(128, 128).copy()
    arrays["c_ecode"] = np.broadcast_to((1.0 + np.arange(8, dtype=np.float32))[None, None, :],
                                        (128, 16, 8)).reshape(128, 128).copy()
    sel8 = np.zeros((128, 8, 8), np.float32)
    sel8[:, np.arange(8), np.arange(8)] = 1.0
    arrays["c_sel8"] = sel8.reshape(128, 64)
    return arrays


def kernel(**inputs):
    import concourse.bacc as _bacc
    from concourse.bass_utils import run_bass_kernel_spmd as _run

    arrays = arrange(inputs)
    nc = _bacc.Bacc("TRN2", target_bir_lowering=False, num_devices=1)
    args, feed = {}, {}
    for name, arr in arrays.items():
        arr = np.ascontiguousarray(arr)
        feed["in_" + name] = arr
        args[name] = nc.dram_tensor("in_" + name, arr.shape, mybir.dt.from_np(arr.dtype), kind="ExternalInput").ap()
    out = nc.dram_tensor("out_0", (N, D), F32, kind="ExternalOutput").ap()
    build(nc, args, out)
    r = _run(nc, [feed], core_ids=[0])
    return r.results[0]["out_0"].reshape(1, N, D)
```

```python
from contextlib import ExitStack

import numpy as np
import concourse.bass as bass
from concourse import mybir

F32 = mybir.dt.float32
BF16 = mybir.dt.bfloat16
F32R = mybir.dt.float32r
I32 = mybir.dt.int32
ALU = mybir.AluOpType
ACT = mybir.ActivationFunctionType
AX = mybir.AxisListType

N = 2048
D = 256
M = 1601
NT = N // 128
KT = 13
KROWS = [128] * 12 + [M - 12 * 128]
CHUNKS = [(0, 401), (401, 400), (801, 400), (1201, 400)]
BIG = 2.0 ** 100
LN_EPS = 1e-5


class Queue:

    def __init__(self, sem):
        self.sem = sem
        self.count = 0
        self.items = []
        self.lists = [self.items]
        self.passed = {}

    def put(self, item, only=None):
        for i, items in enumerate(self.lists):
            if only is None or only == i:
                items.append(item)

    def diverge(self, flag):
        lists = self.lists = [[], []]

        def choose(e):
            v = e.value_load(flag, min_val=0, max_val=1)
            with e.If(v == 1):
                for item in lists[1]:
                    item(e)
            with e.Else():
                for item in lists[0]:
                    item(e)

        self.items.append(choose)

    def merge(self):
        self.lists = [self.items]

    def wait(self, *tokens):
        for sem, value in tokens:
            if self.passed.get(sem, 0) < value:
                self.passed[sem] = value
                self.put(lambda e, s=sem, v=value: e.wait_ge(s, v))

    def do(self, fn, *after, inc=True):
        self.wait(*after)
        if not inc:
            self.put(fn)
            return None
        self.count += 1
        self.put(lambda e: fn(e).then_inc(self.sem, 1))
        return (self.sem, self.count)

    def either(self, general, special):
        self.count += 1
        for i, run in enumerate((general, special)):
            for fn in run[:-1]:
                self.put(fn, i)
            self.put(lambda e, fn=run[-1]: fn(e).then_inc(self.sem, 1), i)
        return (self.sem, self.count)

    def last(self):
        return (self.sem, self.count)

    def play(self, engine):
        for item in self.items:
            item(engine)


class Landing:

    def __init__(self, sem):
        self.sem = sem
        self.count = 0

    def start(self, queue, out, in_, *after):
        queue.wait(*after)
        self.count += 16
        queue.items.append(lambda e: e.dma_start(out, in_).then_inc(self.sem, 16))
        return (self.sem, self.count)


class Slots:

    def __init__(self, views):
        self.views = views
        self.free = [()] * len(views)
        self.at = -1

    def take(self):
        self.at = (self.at + 1) % len(self.views)
        return self.at, self.views[self.at], self.free[self.at]


class Region:

    def __init__(self, nc, at, end):
        self.nc = nc
        self.at = at
        self.end = end

    def place(self, name, shape, dt):
        size = mybir.dt.size(dt)
        for n in shape[1:]:
            size *= n
        t = self.nc.alloc_sbuf_tensor_at(name, shape, dt, offset=self.at)
        self.at += -(-size // 32) * 32
        assert self.at <= self.end, (name, self.at, self.end)
        return t


def build(nc, a, out, phases=99):
    with ExitStack() as ctx:
        sems = {}

        def sem(name):
            sems[name] = ctx.enter_context(nc.semaphore(name))
            return sems[name]

        pe, act, dve, pool, sp = (Queue(sem(n)) for n in ("s_pe", "s_act", "s_dve", "s_pool", "s_sp"))
        engines = (pe, act, dve, pool, sp)
        landings = []

        def landing(name):
            landings.append(Landing(sem(name)))
            return landings[-1]

        def barrier():
            ends = [q.last() for q in (pe, act, dve, pool)] + [(x.sem, x.count) for x in landings]
            for q in engines:
                q.wait(*[t for t in ends if t[1]])

        def pooled(fn, *after):
            return pool.do(fn, *([pool.last()] if pool.count else []), *after)

        def sb(region, name, shape, dt):
            return region.place(name, shape, dt)

        LOW, TOP = -(-nc.sbuf_base // 32) * 32, nc.sbuf_top
        fixed = Region(nc, LOW, TOP)

        PS = ctx.enter_context(nc.psum_tensor("PS", [128, 8, 512], F32))
        X = sb(fixed, "X", [128, NT, D], F32)
        xnT = sb(fixed, "xnT", [128, 2, N], F32)
        identf = sb(fixed, "identf", [128, 128], F32)
        identb = sb(fixed, "identb", [128, 128], BF16)
        onesf = sb(fixed, "onesf", [128, 128], F32)
        onesb = sb(fixed, "onesb", [128, 128], BF16)
        mv = sb(fixed, "mv", [128, NT, 2], F32)
        st = sb(fixed, "st", [128, NT, 6], F32)
        rstd = sb(fixed, "rstd", [128, NT], F32)
        xg = sb(fixed, "xg", [128, 4, D], F32)
        rden = sb(fixed, "rden", [128, 4, 4], F32)
        rr = sb(fixed, "rr", [128, 20], F32)
        BIG_AT = fixed.at
        big = sb(fixed, "big", [128, 4096], F32)
        ctxT = big[:, 0:2 * M].rearrange("p (h n) -> p h n", h=2)
        b1 = sb(fixed, "b1", [128, 64], F32)
        trash = sb(fixed, "trash", [128, 2, 401], BF16)

        l_x = [landing(f"l_x{g}") for g in range(4)]
        l_c = [landing(f"l_c{g}") for g in range(4)]
        l_w = landing("l_w")
        l_out = landing("l_out")

        x_v = a["x"].rearrange("(t p) d -> p t d", p=128)
        out_v = out.rearrange("(t p) d -> p t d", p=128)
        i0 = pooled(lambda e: e.memset(identf[:], 0.0))
        i1 = pooled(lambda e: e.memset(onesf[:], 1.0))
        i2 = pooled(lambda e: e.memset(onesb[:], 1.0))
        i3 = pooled(lambda e: e.affine_select(out=identf[:], in_=identf[:], compare_op=ALU.not_equal, fill=1.0,
                                               base=0, pattern=[[-1, 128]], channel_multiplier=1), i0)
        t_const = pooled(lambda e: e.tensor_copy(identb[:], identf[:]), i3)
        for q in (pe, act, dve):
            q.wait(t_const)

        x_ready = [None] * NT

        def bank(b):
            return PS[:, b, :]

        def mm(o, lhsT, rhs, start, stop, *after, inc=False, loose=False):
            return pe.do(lambda e: e.matmul(o, lhsT, rhs, start=start, stop=stop, skip_group_check=loose), *after,
                         inc=inc)

        def pull(gen, n):
            for _ in range(n):
                if next(gen, None) is None:
                    return

        class Background:

            def __init__(self):
                self.gens = []
                self.rate = 0.0
                self.due = 0.0

            def add(self, *gens):
                self.gens += gens

            def step(self):
                while self.gens:
                    if next(self.gens[0], None) is not None:
                        return
                    self.gens.pop(0)

            def tick(self):
                self.due += self.rate
                while self.due >= 1.0:
                    self.due -= 1.0
                    self.step()

            def flush(self):
                while self.gens:
                    self.step()

        class Stream(Background):

            def __init__(self, maxima, units, stacks, ready, rate):
                super().__init__()
                self.units = units
                self.stacks = stacks
                self.ready = ready
                self.at = 0
                self.rate = rate
                self.add(self.run(maxima))

            def run(self, maxima):
                for i in range(1, len(self.units)):
                    while self.at < i - 2 or self.units[i][0] not in self.stacks:
                        yield 1
                    yield from maxima(*self.units[i])

            def reach(self, u):
                self.at = u
                while self.units[u] not in self.ready:
                    self.step()

        def weave(*parts):
            parts = [[gen, n, lo, hi, 0] for gen, n, lo, hi in parts]
            while parts:
                part = min(parts, key=lambda q: q[2] + (q[3] - q[2]) * (q[4] + 0.5) / q[1])
                part[4] += 1
                if next(part[0], None) is None:
                    parts.remove(part)
                else:
                    yield 1

        def late(fn, args):
            yield from fn(*args)

        def take(gen, n):
            for _ in range(n):
                v = next(gen, None)
                if v is None:
                    return
                yield v

        xn_ready = {}
        xg_free = [()]
        tail = []

        def norm_group(g, ring, *xn_free, rms=False):
            ts = slice(4 * g, 4 * g + 4)
            toks = [dve.do(lambda e, t=t: e.bn_stats(st[:, t, :], X[:, t, :]), x_ready[t])
                    for t in range(4 * g, 4 * g + 4)]
            for t in range(4 * g, 4 * g + 4):
                a2 = dve.do(lambda e, t=t: e.bn_aggr(mv[:, t, :], st[:, t, :]), toks[t - 4 * g])
            v1 = dve.do(lambda e: e.tensor_scalar(rstd[:, ts], mv[:, ts, 1], LN_EPS, None, ALU.add), a2)
            v2 = act.do(lambda e: e.activation(rstd[:, ts], rstd[:, ts], ACT.Sqrt), v1)
            yield 1
            v3 = dve.do(lambda e: e.reciprocal(rstd[:, ts], rstd[:, ts]), v2)
            n = []
            for i in range(4):
                t = 4 * g + i
                n.append(dve.do(lambda e, t=t, i=i: e.tensor_scalar(
                    xg[:, i, :], X[:, t, :], mv[:, t, 0:1], rstd[:, t:t + 1], ALU.subtract, ALU.mult),
                    v3, *xg_free[0]))
            if rms:
                for i in range(4):
                    n[i] = dve.do(lambda e, i=i: e.tensor_tensor_reduce(
                        trash[:, 0, 0:D], xg[:, i, :], xg[:, i, :], 1.0, 0.0, ALU.mult, ALU.add,
                        rr[:, i:i + 1]), n[i], dve.last())
                r1 = dve.do(lambda e: e.tensor_scalar(rr[:, 4:8], rr[:, 0:4], 1.0 / D, None, ALU.mult), n[3])
                r2 = act.do(lambda e: e.activation(rr[:, 8:12], rr[:, 4:8], ACT.Sqrt), r1)
                yield 1
                r3 = dve.do(lambda e: e.tensor_scalar(rr[:, 12:16], rr[:, 8:12], 1e-8, None, ALU.add), r2)
                r4 = dve.do(lambda e: e.reciprocal(rr[:, 16:20], rr[:, 12:16]), r3)
                for i in range(4):
                    n[i] = dve.do(lambda e, i=i: e.tensor_scalar(
                        xg[:, i, :], xg[:, i, :], rr[:, 16 + i:17 + i], None, ALU.mult), r4)
            yield 1
            yield 1
            for hf in range(2):
                b, ps, free = ring.take()
                for i in range(4):
                    last = pe.do(lambda e, ps=ps, i=i, hf=hf: e.transpose(
                        ps[:, i * 128:(i + 1) * 128], xg[:, i, hf * 128:(hf + 1) * 128], identf[:]),
                        n[i], *free, inc=(i == 3))
                ev = act.do(lambda e, ps=ps, hf=hf: e.activation(
                    xnT[:, hf, g * 512:(g + 1) * 512], ps, ACT.Copy), last, *xn_free)
                ring.free[b] = (ev,)
                xg_free[0] = (last,)
                xn_ready[g] = ev
                yield 1

        def add_residual(t, ps, *after):
            x_ready[t] = dve.do(lambda e: e.tensor_tensor(X[:, t, :], ps, X[:, t, :], ALU.add), *after, x_ready[t])
            return x_ready[t]

        def head_max(tile_of, ring, pm, masks):
            for idx, (lhs, rhs_of, mb) in tile_of:
                for c, (k0, kn) in enumerate(CHUNKS):
                    b, ps, free = ring.take()
                    pairs = list(zip(lhs, rhs_of(k0, kn)))
                    for j, (l, r) in enumerate(pairs):
                        tok = mm(ps[:, 0:kn], l, r, j == 0, j == len(pairs) - 1, *free, inc=(j == len(pairs) - 1))
                    o = pm[:, idx * 4 + c:idx * 4 + c + 1]
                    if masks is None:
                        red = dve.do(lambda e, o=o, ps=ps, kn=kn: e.tensor_reduce(o, ps[:, 0:kn], AX.X, ALU.max), tok)
                    else:
                        s = trash_at[0] % 2
                        trash_at[0] += 1
                        red = dve.do(lambda e, o=o, ps=ps, kn=kn, k0=k0, mb=mb, s=s: e.tensor_tensor_reduce(
                            trash[:, s, 0:kn], ps[:, 0:kn], mb[0][:, k0:k0 + kn], 1.0, -3.0e38, ALU.add, ALU.max, o),
                            tok, mb[1], *trash_free[s])
                        trash_free[s] = (red,)
                    ring.free[b] = (red,)
                    yield red

        trash_at = [0]
        trash_free = [(), ()]

        def max_rows(n, pm, mx, nm, before):
            m0 = dve.do(lambda e: e.tensor_reduce(mx[:, 0:n], pm[:, 0:4 * n].rearrange("p (n c) -> p n c", c=4),
                                                  AX.X, ALU.max), dve.last(), *before)
            m1 = dve.do(lambda e: e.tensor_scalar(nm[:, 0:n, 0], mx[:, 0:n], -1.0, None, ALU.mult), m0)
            return dve.do(lambda e: e.scalar_tensor_tensor(out=nm[:, 0:n, 1], in0=mx[:, 0:n], scalar=-1.0,
                                                           in1=nm[:, 0:n, 0], op0=ALU.mult, op1=ALU.subtract), m1)

        def l0_attention(scope, early):
            Q1 = sb(scope, "Q1", [128, 2, 2, N], BF16)
            Q2 = sb(scope, "Q2", [66, 2, 2, N], BF16)
            K1 = sb(scope, "K1", [128, 2, 2, M], BF16)
            K2 = sb(scope, "K2", [66, 2, 2, M], BF16)
            V = sb(scope, "V0", [128, KT, 512], F32)
            P = sb(scope, "P0", [128, 4, 2, 512], F32)
            wqk = sb(scope, "wqk0", [128, 2, 2, 2, 256], F32)
            wv = sb(scope, "wv0", [128, 2, 512], F32)
            wo = sb(scope, "wo0", [128, 4, D], F32)
            bo = sb(scope, "bo0", [1, D], F32)
            acc = sb(scope, "acc0", [128, 2, 2, 512], F32)
            On = sb(scope, "On0", [128, 2, 512], F32)
            R = sb(scope, "R0", [128, 512], F32)
            pm = sb(scope, "pm0", [128, 2, 32], F32)
            mx = sb(scope, "mx0", [128, 2, 8], F32)
            nm = sb(scope, "nm0", [128, 2, 8, 2], BF16)
            l_v = landing("l_v")
            l_qk = [landing(f"l_qk{i}") for i in range(2)]
            w_free = [(), ()]
            w_ready = {}

            def load_qk(p):
                s = p % 2
                for i, n in enumerate(("L0_WqD", "L0_WkD")):
                    w_ready[p] = l_qk[s].start(
                        sp, wqk[:, s, i, :, :],
                        a[n].rearrange("(h p) n -> p h n", p=128)[:, :, p * 256:(p + 1) * 256], *w_free[s])

            def load_x(g):
                t = l_x[g].start(sp, X[:, 4 * g:4 * g + 4, :], x_v[:, 4 * g:4 * g + 4, :])
                x_ready[4 * g:4 * g + 4] = [t] * 4

            t_v = l_v.start(sp, wv[:], a["L0_xattn_Wv"].rearrange("(h p) n -> p h n", p=128))
            t_ctx = []
            for g in range(4):
                cs = slice(g * 512, min(M, (g + 1) * 512))
                t_ctx.append(l_c[g].start(sp, ctxT[:, :, cs], a["ctxT"].rearrange("(h p) n -> p h n", p=128)[:, :, cs]))
                load_x(g)
                if g == 0:
                    load_qk(0)
            load_qk(1)
            l_w.start(sp, wo[:], a["L0_xattn_Wo"].rearrange("(h p) n -> p h n", p=128))
            tw = l_w.start(sp, bo[:], a["L0_xattn_bo"])
            load_experts(early)
            for s in range(2):
                ones_k = pooled(lambda e, s=s: e.memset(K2[64:66, s, :, :], 1.0))
            ring = Slots([bank(4), bank(5), bank(7)])
            pe.wait(t_v, ones_k)
            v_ready = []

            def values():
                for kt in range(KT):
                    r = KROWS[kt]
                    b, ps, free = ring.take()
                    for hf in range(2):
                        tok = mm(ps[0:r, :], ctxT[:, hf, kt * 128:kt * 128 + r], wv[:, hf, :], hf == 0, hf == 1,
                                 *free, t_ctx[kt // 4], inc=(hf == 1))
                    ev = act.do(lambda e, ps=ps, r=r, kt=kt: e.activation(V[0:r, kt, :], ps[0:r, :], ACT.Copy), tok)
                    ring.free[b] = (ev,)
                    v_ready.append(ev)
                    yield 1

            def norms():
                for g in range(4):
                    yield from norm_group(g, ring)

            pull(weave((values(), 13, 0.0, 1.0), (norms(), 20, 0.2, 1.0)), 99)
            pe.wait(tw)
            stack_ready = {}
            stack_free = {0: (), 1: ()}
            xn_read = [None]

            def prepare(p):
                s = p % 2
                free_s = stack_free[s]
                toks = {}
                for hh in range(2):
                    for qb in range(4):
                        b, ps, free = ring.take()
                        for hf in range(2):
                            tok = mm(ps, wqk[:, s, 0, hf, hh * 128:(hh + 1) * 128],
                                     xnT[:, hf, qb * 512:(qb + 1) * 512], hf == 0, hf == 1, *free, xn_ready[qb],
                                     w_ready[p], inc=(hf == 1))
                        q1 = Q1[:, s, hh, qb * 512:(qb + 1) * 512]
                        q2 = Q2[0:64, s, hh, qb * 512:(qb + 1) * 512]
                        e1 = act.do(lambda e, q1=q1, ps=ps: e.activation(q1, ps, ACT.Copy), tok, *free_s)
                        e2 = dve.do(lambda e, q1=q1, q2=q2, ps=ps: e.tensor_tensor(
                            q2, ps[0:64, :], q1[0:64, :], ALU.subtract), e1)
                        ring.free[b] = (e2,)
                        toks["q"] = e2
                        xn_read[0] = tok
                        yield 1
                    for c, (k0, kn) in enumerate(CHUNKS):
                        b, ps, free = ring.take()
                        for hf in range(2):
                            tok = mm(ps[:, 0:kn], wqk[:, s, 1, hf, hh * 128:(hh + 1) * 128], ctxT[:, hf, k0:k0 + kn],
                                     hf == 0, hf == 1, *free, inc=(hf == 1))
                        k1 = K1[:, s, hh, k0:k0 + kn]
                        k2 = K2[0:64, s, hh, k0:k0 + kn]
                        e1 = act.do(lambda e, k1=k1, ps=ps, kn=kn: e.activation(k1, ps[:, 0:kn], ACT.Copy), tok,
                                    *free_s)
                        e2 = dve.do(lambda e, k1=k1, ps=ps, kn=kn: e.tensor_tensor(
                            k1[64:128, :], ps[64:128, 0:kn], k1[64:128, :], ALU.subtract), e1)
                        e3 = pooled(lambda e, k1=k1, k2=k2: e.tensor_copy(k2, k1[0:64, :]), e1)
                        ring.free[b] = (e2,)
                        toks["k"] = (e2, e3)
                        yield 1
                w_free[s] = (tok,)
                stack_ready[p] = [toks["q"], *toks["k"]]
                if p + 2 < 4:
                    load_qk(p + 2)

            unit_ready = {}
            nm_free = {0: (), 1: ()}

            def maxima(p, qb):
                s = p % 2
                u = (4 * p + qb) % 2
                pe.wait(*stack_ready[p])
                tiles = []
                for hh in range(2):
                    for qt in range(4):
                        q0 = qb * 512 + qt * 128
                        tiles.append((hh * 4 + qt, ([Q1[:, s, hh, q0:q0 + 128]],
                                                    lambda k0, kn, hh=hh: [K1[:, s, hh, k0:k0 + kn]], None)))
                yield from head_max(tiles, ring, pm[:, u, :], None)
                tn = max_rows(8, pm[:, u, :], mx[:, u, :], nm[:, u, :, :], nm_free[u])
                for _ in range(4):
                    yield 1
                for hh in range(2):
                    b, ps, free = ring.take()
                    for qt in range(4):
                        tok = mm(ps[64:66, qt * 128:(qt + 1) * 128], nm[:, u, hh * 4 + qt, :], identb[:], True, True,
                                 *free, tn, inc=(qt == 3))
                    ev = act.do(lambda e, ps=ps, hh=hh: e.activation(
                        Q2[64:66, s, hh, qb * 512:(qb + 1) * 512], ps[64:66, :], ACT.Copy), tok)
                    ring.free[b] = (ev,)
                    yield 1
                nm_free[u] = (tok,)
                unit_ready[p, qb] = ev

            S = Slots([(0, 1), (2, 3)])
            Ps = Slots([0, 1, 2, 3])
            o_free = [()]
            on_free = {0: (), 1: ()}
            r_free = [()]
            bg = Background()
            units = [(p, qb) for p in range(4) for qb in range(4)]
            stream = Stream(maxima, units, stack_ready, unit_ready, 0.75)

            def tick():
                bg.tick()
                stream.tick()

            def scores(p, qb, kt):
                s = p % 2
                r = KROWS[kt]
                i, banks, free = S.take()
                q = qb * 512
                for hh in range(2):
                    mm(bank(banks[hh])[0:r, :], K1[:, s, hh, kt * 128:kt * 128 + r], Q1[:, s, hh, q:q + 512],
                       True, False, *free, unit_ready[p, qb])
                    tok = mm(bank(banks[hh])[0:r, :], K2[:, s, hh, kt * 128:kt * 128 + r], Q2[:, s, hh, q:q + 512],
                             False, True, inc=(hh == 1))
                    tick()
                j, _, pfree = Ps.take()
                ex = act.do(lambda e, banks=banks, r=r, j=j: e.activation(
                    P[0:r, j, :, :], PS[0:r, banks[0]:banks[0] + 2, :], ACT.Exp, scale=0.125), tok, *pfree)
                S.free[i] = (ex,)
                return ex, j, r

            held = []
            acc_free = {0: (), 1: ()}
            acc_at = {}

            def attend(p, qb, kt, ex, j, r):
                u = (4 * p + qb) % 2
                if kt == 0:
                    pe.wait(*o_free[0])
                for hh in range(2):
                    h = 2 * p + hh
                    tok = mm(PS[64 * hh:64 * hh + 64, 6, :], V[0:r, kt, h * 64:(h + 1) * 64], P[0:r, j, hh, :],
                             kt == 0, kt == KT - 1, ex, v_ready[kt], inc=(hh == 1))
                tick()
                if kt == 0:
                    held.append((j, tok, ex))
                    return tok
                if kt == 1:
                    j0, tok0, ex0 = held.pop()
                    at = dve.do(lambda e, j0=j0: e.tensor_tensor(acc[:, u, :, :], P[:, j0, :, :], P[:, j, :, :],
                                                                 ALU.add), ex, ex0, *acc_free[u])
                    Ps.free[j0] = (tok0, at)
                else:
                    at = dve.do(lambda e: e.tensor_tensor(acc[0:r, u, :, :], acc[0:r, u, :, :], P[0:r, j, :, :],
                                                          ALU.add), ex, acc_at[u])
                acc_at[u] = at
                Ps.free[j] = (tok, at)
                tick()
                return tok

            def finish(p, qb, tok):
                u = (4 * p + qb) % 2
                at = acc_at[u]
                c1 = act.do(lambda e: e.activation(On[:, u, :], PS[:, 6, :], ACT.Copy), tok, *on_free[u])
                o_free[0] = (c1,)

                def divide():
                    b, ps, free = ring.take()
                    for hh in range(2):
                        tk = mm(ps[64 * hh:64 * hh + 64, :], onesf[:, 0:64], acc[:, u, hh, :], True, True, *free, at,
                                inc=(hh == 1))
                    acc_free[u] = (tk,)
                    d0 = act.do(lambda e, ps=ps: e.activation(R[:], ps, ACT.Copy), tk, *r_free[0])
                    ring.free[b] = (d0,)
                    yield 1
                    for i in range(4):
                        n = slice(128 * i, 128 * i + 128)
                        d1 = dve.do(lambda e, n=n: e.reciprocal(R[:, n], R[:, n]), d0)
                        yield 1
                    d2 = dve.do(lambda e: e.tensor_tensor(On[:, u, :], On[:, u, :], R[:], ALU.mult), d1, c1)
                    r_free[0] = (d2,)
                    yield 1

                def project():
                    d2 = r_free[0][0]
                    for qt in range(4):
                        b, ps, free = ring.take()
                        tk = mm(ps[:, 0:D], On[:, u, qt * 128:(qt + 1) * 128], wo[:, p, :], True, p != 0, *free,
                                d2, inc=(p != 0))
                        if p == 0:
                            tk = mm(ps[:, 0:D], onesf[0:1, :], bo[:], False, True, inc=True)
                        ring.free[b] = (add_residual(4 * qb + qt, ps[:, 0:D], tk),)
                        yield 1
                    on_free[u] = (tk,)
                    if p == 3:
                        yield from norm_group(qb, ring, xn_read[0])
                        yield from gate_logits(qb, ring)
                return divide(), project()

            pull(prepare(0), 99)
            pull(maxima(0, 0), 99)
            ahead = []
            preps = {}
            for u, (p, qb) in enumerate(units):
                stream.reach(u)
                for kt in range(KT):
                    ahead.append(((p, qb, kt), scores(p, qb, kt)))
                    if len(ahead) > 1:
                        (p0, qb0, kt0), got = ahead.pop(0)
                        tok = attend(p0, qb0, kt0, *got)
                    if kt == 0:
                        parts = []
                        if u:
                            dv, pj = finish(p0, qb0, tok)
                            parts += [(dv, 5, 0.03, 0.3), (pj, 11 if p0 == 3 else 4, 0.355, 0.6)]
                            if qb0 == 3:
                                stack_free[p0 % 2] = (tok,)
                        if p < 3 and qb == 0:
                            preps[p + 1] = prepare(p + 1)
                        if p < 3 and qb < 3:
                            parts.append((take(preps[p + 1], 6 if qb < 2 else 99), 6, 0.0, 0.9))
                        bg.add(weave(*parts))
                        bg.rate = (sum(q[1] for q in parts)) / ((KT - 1) * 4 - 2)
                bg.flush()
            (p0, qb0, kt0), got = ahead.pop(0)
            tok = attend(p0, qb0, kt0, *got)
            barrier()
            tail.extend(finish(p0, qb0, tok))

        def load_experts(region):
            for n, shape, dt, src in (
                    ("gw", [128, 2, 8], F32, a["L0_ffn_gate_w"].rearrange("(h p) n -> p h n", p=128)),
                    ("tri", [128, 128], I32, a["c_tri"]), ("sel8f", [128, 64], F32, a["c_sel8"]),
                    ("base", [128, 128], F32, a["c_base"]), ("ecode", [128, 128], F32, a["c_ecode"])):
                xp[n] = sb(region, n, shape, dt)
                l_e0.start(sp, xp[n][:], src)
            xp["ex"] = sb(region, "ex", [128, 2, 8 * D], F32)
            for e_ in range(8):
                xp["loaded"] = l_e0.start(sp, xp["ex"][:, :, e_ * D:(e_ + 1) * D],
                                          a["L0_ffn_experts"][e_].rearrange("(h p) n -> p h n", p=128))
            xp["sel8"] = sb(region, "sel8", [128, 64], BF16)
            xp["G"] = sb(region, "G", [128, NT, 8], F32)

        xp = {}
        l_e0 = landing("l_e0")

        def gate_logits(g, ring):
            b, ps, free = ring.take()
            for i in range(4):
                t = 4 * g + i
                for hf in range(2):
                    tok = mm(ps[:, i * 8:(i + 1) * 8], xnT[:, hf, t * 128:(t + 1) * 128], xp["gw"][:, hf, :], hf == 0,
                             hf == 1, *free, xn_ready[g], xp["loaded"], inc=(i == 3 and hf == 1))
            xp["gated"] = dve.do(lambda e: e.tensor_scalar(
                xp["G"][:, 4 * g:4 * g + 4, :], ps[:, 0:32].rearrange("p (t e) -> p t e", e=8), 1e-6, None, ALU.max),
                tok)
            ring.free[b] = (xp["gated"],)
            yield 1

        def l0_experts(scope, filler, n_filler):
            tri, sel8f, base, ecode, ex, sel8, G = (xp[n] for n in ("tri", "sel8f", "base", "ecode", "ex", "sel8", "G"))
            cs = sb(scope, "cs", [128, 8], F32)
            rc = sb(scope, "rc", [128, 8], F32)
            rs = sb(scope, "rs", [128, NT], F32)
            rr_ = sb(scope, "rr_", [128, NT], F32)
            Ge = sb(scope, "Ge", [128, 8, NT], F32)
            GT = sb(scope, "GT", [128, 128], F32)
            cnt = sb(scope, "cnt", [128, NT, 8], F32)
            rk = sb(scope, "rk", [128, NT, 8], F32)
            sl = sb(scope, "sl", [128, NT, 8], F32)
            best = sb(scope, "best", [128, NT], F32)
            w = sb(scope, "w8", [128, NT, 8], F32)
            W = sb(scope, "Wg", [128, 8, N], F32)
            ind = sb(scope, "ind", [128, 4, N], BF16)
            dump = sb(scope, "dump", [128, N], BF16)
            ccs = sb(scope, "ccs", [8, N], F32)
            gs = nc.dram_tensor("gate_rows", [8, N], F32, kind="Internal").ap()
            l_g = landing("l_g")
            l_b = [landing(f"l_b{e}") for e in range(8)]
            here = []

            def sinkhorn():
                dve.wait(xp["loaded"])
                t_sel = dve.do(lambda e: e.tensor_copy(sel8[:], sel8f[:]))
                g = xp["gated"]
                for _ in range(8):
                    c0 = dve.do(lambda e: e.tensor_reduce(cs[:], G[:].rearrange("p t e -> p e t"), AX.X, ALU.add), g)
                    c1 = mm(PS[:, 2, 0:8], onesf[:], cs[:], True, True, c0, inc=True)
                    yield 1
                    c2 = dve.do(lambda e: e.reciprocal(rc[:], PS[:, 2, 0:8]), c1)
                    c3 = dve.do(lambda e: e.tensor_tensor(G[:], G[:], rc[:].unsqueeze(1).to_broadcast([128, NT, 8]),
                                                          ALU.mult), c2)
                    c4 = dve.do(lambda e: e.tensor_reduce(rs[:], G[:], AX.X, ALU.add), c3)
                    c5 = dve.do(lambda e: e.reciprocal(rr_[:], rs[:]), c4)
                    g = dve.do(lambda e: e.tensor_tensor(G[:], G[:], rr_[:].unsqueeze(2).to_broadcast([128, NT, 8]),
                                                         ALU.mult), c5)
                g1 = dve.do(lambda e: e.tensor_copy(Ge[:], G[:].rearrange("p t e -> p e t")), g)
                g2 = pe.do(lambda e: e.transpose(PS[:, 3, 0:128], Ge[:].rearrange("p e t -> p (e t)"), identf[:]), g1)
                g3 = act.do(lambda e: e.activation(GT[:], PS[:, 3, 0:128], ACT.Copy), g2)
                g4 = l_g.start(sp, gs.rearrange("e (t n) -> (e t) n", n=128), GT[:], g3)
                for e_ in range(8):
                    here.append(l_b[e_].start(sp, W[:, e_, :], gs[e_:e_ + 1, :].to_broadcast([128, N]), g4))
                pe.wait(t_sel)
                yield 1

            before = []
            while tail:
                before.append(tail.pop(0))

            def serial():
                for gen in before:
                    yield from gen
                yield from sinkhorn()

            pull(weave((serial(), 30, 0.0, 1.0), (filler, n_filler, 0.3, 1.0)), 999)
            ring = Slots([0, 1, 2, 3])
            cc_bank = [0, 1, 2, 3]
            opened = set()
            pe.wait(dve.last(), act.last())
            used = {}
            dense = Slots([bank(b) for b in (5, 6, 7)])
            bs = base[:].rearrange("p (t e) -> p t e", e=8)
            ec = ecode[:].rearrange("p (t e) -> p t e", e=8)
            todo = Background()
            copied = {}
            subtracted = [()]

            def count(t, e_, on_act):
                blk = W[:, e_, t * 128:(t + 1) * 128].bitcast(I32)
                b1 = pooled(lambda e: e.tensor_tensor(blk, blk, tri[:], ALU.add), *used.get(e_, (here[e_],)))
                i, _, free = ring.take()
                n = N - 128 * t
                o = cnt[:, t, e_:e_ + 1]
                if on_act:
                    b2 = dve.do(lambda e: e.tensor_scalar(ind[:, i, 0:n], W[:, e_, t * 128:N], G[:, t, e_:e_ + 1],
                                                          None, ALU.is_gt), b1, *free)
                    b3 = act.do(lambda e: e.activation(dump[:, 0:n], ind[:, i, 0:n], ACT.Copy, accum_out=o), b2,
                                act.last())
                else:
                    b2 = b3 = dve.do(lambda e: e.tensor_scalar(
                        ind[:, i, 0:n], W[:, e_, t * 128:N], G[:, t, e_:e_ + 1], 0.0, ALU.is_gt, ALU.add,
                        accum_out=o), b1, *free)
                used[e_] = (b2,)
                tok = None
                for b in (3, 2, 1, 0):
                    lo = max(512 * b, 128 * (t + 1))
                    hi = 512 * (b + 1)
                    if lo >= hi:
                        continue
                    tok = mm(PS[0:8, cc_bank[b], lo - 512 * b:512], sel8[:, e_ * 8:(e_ + 1) * 8],
                             ind[:, i, lo - 128 * t:hi - 128 * t], b not in opened,
                             hi // 128 - 2 == t and e_ == 7, b2, *copied.get((t, b), ()), inc=True, loose=True)
                    opened.add(b)
                ring.free[i] = (tok or b2, b3)
                return b3, tok

            def weigh(t, after):
                if t:
                    c_tok = pe.do(lambda e: e.transpose(PS[:, 4, t * 8:(t + 1) * 8], ccs[:, t * 128:(t + 1) * 128],
                                                        identf[0:8, 0:8]), *copied[t, t // 4], *subtracted[0])
                    yield 1
                r0 = dve.do(lambda e: e.tensor_tensor(rk[:, t, :], cnt[:, t, :], bs[:, t, :], ALU.add), *after)
                if t:
                    r0 = dve.do(lambda e: e.tensor_tensor(rk[:, t, :], rk[:, t, :], PS[:, 4, t * 8:(t + 1) * 8],
                                                          ALU.subtract), r0, c_tok)
                    subtracted[0] = (r0,)
                r2 = dve.do(lambda e: e.tensor_scalar(sl[:, t, :], rk[:, t, :], 255.5, None, ALU.is_lt), r0)
                r3 = dve.do(lambda e: e.scalar_tensor_tensor(out=rk[:, t, :], in0=rk[:, t, :], scalar=8.0,
                                                             in1=ec[:, t, :], op0=ALU.mult, op1=ALU.add), r2)
                yield 1
                r4 = dve.do(lambda e: e.tensor_tensor(rk[:, t, :], rk[:, t, :], sl[:, t, :], ALU.mult), r3)
                r5 = dve.do(lambda e: e.tensor_reduce(best[:, t:t + 1], rk[:, t, :], AX.X, ALU.max), r4)
                r6 = dve.do(lambda e: e.scalar_tensor_tensor(out=w[:, t, :], in0=rk[:, t, :],
                                                             scalar=best[:, t:t + 1], in1=sl[:, t, :],
                                                             op0=ALU.is_equal, op1=ALU.mult), r5)
                r7 = dve.do(lambda e: e.tensor_tensor(w[:, t, :], w[:, t, :], G[:, t, :], ALU.mult), r6)
                yield 1
                for pr in range(4):
                    b, ps, free = dense.take()
                    for hf in range(2):
                        tok = mm(ps, xnT[:, hf, t * 128:(t + 1) * 128], ex[:, hf, pr * 512:(pr + 1) * 512],
                                 hf == 0, hf == 1, *free, inc=(hf == 1))
                    fresh.append((t, pr, b, ps, tok, r7))
                    if len(fresh) > 2:
                        gather()
                    yield 1
                if t % 4 == 3:
                    while fresh:
                        gather()
                        yield 1
                    if t < NT - 1:
                        yield from norm_group(t // 4, dense, tok)

            fresh = []

            def gather():
                t, pr, b, ps, tok, r7 = fresh.pop(0)
                for j in range(2):
                    c = 2 * pr + j
                    x_ready[t] = dve.do(lambda e, c=c, j=j: e.scalar_tensor_tensor(
                        out=X[:, t, :], in0=ps[:, j * D:(j + 1) * D], scalar=w[:, t, c:c + 1], in1=X[:, t, :],
                        op0=ALU.mult, op1=ALU.add), tok, r7, x_ready[t])
                dense.free[b] = (x_ready[t],)

            for t in range(NT):
                if t:
                    b_, o_ = t // 4, t % 4 * 128
                    copied[t, b_] = (act.do(lambda e, t=t, b_=b_, o_=o_: e.activation(
                        ccs[:, t * 128:(t + 1) * 128], PS[0:8, b_, o_:o_ + 128], ACT.Copy), got[1]),)
                for e_ in range(8):
                    got = count(t, e_, e_ % 4 != 3)
                    todo.tick()
                after = (got[0], dve.last(), act.last())
                todo.flush()
                todo.add(weigh(t, after))
                todo.rate = 1.1
            todo.flush()
            barrier()
            tail.append(lambda ring: norm_group(3, ring))

        def keys_values(region, layer, biased):
            L = f"L{layer}_xattn_"
            kv = {"L": L, "biased": biased, "k": [], "v": []}
            kT = kv["kT"] = sb(region, "kT" + L, [128, 2, M], F32)
            kh = kv["kh"] = sb(region, "kh" + L, [128, 2, M], BF16)
            V = kv["V"] = sb(region, "V" + L, [128, KT, D + 1], F32)
            kv["at"] = region.at
            wt = {n: sb(region, n + L, [128, 2, D], F32) for n in ("Wk", "Wv", "Wq")}
            kv["Wq"] = wt["Wq"]
            kv["end"] = region.at
            l_k = landing("l_k" + L)
            for n in wt:
                tw = l_k.start(sp, wt[n][:], a[L + n + "T"].rearrange("(h p) n -> p h n", p=128))
            if biased:
                bk = sb(region, "bk" + L, [128, 2], F32)
                bv = sb(region, "bv" + L, [1, D], F32)
                kv["bq"] = sb(region, "bq" + L, [128, 2], F32)
                l_k.start(sp, kv["bq"][:], a[L + "bq"])
                l_k.start(sp, bk[:], a[L + "bk"])
                tw = l_k.start(sp, bv[:], a[L + "bv"])
            kv["loaded"] = tw
            ones = pooled(lambda e: e.memset(V[:, :, D:D + 1], 1.0))

            def keys(ring):
                for c0, cn in CHUNKS:
                    for half in range(2):
                        b, ps, free = ring.take()
                        for hf in range(2):
                            tok = mm(ps[:, 0:cn], wt["Wk"][:, hf, half * 128:(half + 1) * 128],
                                     ctxT[:, hf, c0:c0 + cn], hf == 0, hf == 1, *free, tw, inc=(hf == 1))
                        ring.free[b] = evacuate(tok, ps[:, 0:cn], kT[:, half, c0:c0 + cn], kh[:, half, c0:c0 + cn],
                                                bk[:, half:half + 1] if biased else None, kv["k"], tw)
                        yield 1

            def values(ring):
                for kt in range(KT):
                    r = KROWS[kt]
                    b, ps, free = ring.take()
                    for hf in range(2):
                        tok = mm(ps[0:r, 0:D], ctxT[:, hf, kt * 128:kt * 128 + r], wt["Wv"][:, hf, :], hf == 0,
                                 hf == 1 and not biased, *free, tw, inc=(hf == 1))
                    if biased:
                        tok = mm(ps[0:r, 0:D], onesf[0:1, 0:r], bv[:], False, True, inc=True)
                    ev = act.do(lambda e, ps=ps, r=r, kt=kt: e.activation(V[0:r, kt, 0:D], ps[0:r, 0:D], ACT.Copy),
                                tok, ones)
                    ring.free[b] = (ev,)
                    kv["v"].append(ev)
                    yield 1

            kv["keys"], kv["values"] = keys, values
            return kv

        def evacuate(tok, ps, full, half, bias, ready, loaded):
            if bias is None:
                e1 = act.do(lambda e: e.activation(full, ps, ACT.Copy), tok)
            else:
                e1 = act.do(lambda e: e.activation(full, ps, ACT.Identity, bias=bias), tok, loaded)
            ready.append(act.do(lambda e: e.activation(half, full, ACT.Copy), e1))
            return (e1,)

        def single_attention(scope, kv, before, mb, mb_ready, aside, n_aside, rms):
            L, biased, kT, kh, V, wq = (kv[n] for n in ("L", "biased", "kT", "kh", "V", "Wq"))
            masked = mb is not None
            qT = sb(scope, "qT" + L, [128, 2, N], F32)
            qh = sb(scope, "qh" + L, [128, 2, N], BF16)
            P = sb(scope, "P" + L, [128, 3, 512], F32)
            mrow = sb(scope, "mrow" + L, [2, N], BF16)
            pm = sb(scope, "pm" + L, [128, 2, 16], F32)
            mx = sb(scope, "mx" + L, [128, 2, 4], F32)
            nm = sb(scope, "nm" + L, [128, 2, 4, 2], BF16)
            ring = Slots([bank(4), bank(5)])
            aside = aside(ring)
            q_ready, q_read = {}, {}

            def queries(g):
                got = []
                for half in range(2):
                    b, ps, free = ring.take()
                    for hf in range(2):
                        tok = mm(ps, wq[:, hf, half * 128:(half + 1) * 128], xnT[:, hf, g * 512:(g + 1) * 512],
                                 hf == 0, hf == 1, *free, xn_ready[g], kv["loaded"], inc=(hf == 1))
                    cs = slice(g * 512, (g + 1) * 512)
                    ring.free[b] = evacuate(tok, ps, qT[:, half, cs], qh[:, half, cs],
                                            kv["bq"][:, half:half + 1] if biased else None, got, kv["loaded"])
                    q_ready[g] = got[-1]
                    q_read[g] = tok
                    yield 1

            unit_ready = {}
            nm_free = {0: (), 1: ()}

            def maxima(qb):
                u = qb % 2
                pe.wait(q_ready[qb], kv["k"][-1])
                tiles = []
                for qt in range(4):
                    q0 = qb * 512 + qt * 128
                    m = (mb[:, 4 * qb + qt, :], mb_ready[4 * qb + qt]) if masked else None
                    tiles.append((qt, ([qh[:, hf, q0:q0 + 128] for hf in range(2)],
                                       lambda k0, kn: [kh[:, hf, k0:k0 + kn] for hf in range(2)], m)))
                yield from head_max(tiles, ring, pm[:, u, :], mb if masked else None)
                tn = max_rows(4, pm[:, u, :], mx[:, u, :], nm[:, u, :, :], nm_free[u])
                yield 1
                yield 1
                b, ps, free = ring.take()
                for qt in range(4):
                    tok = mm(ps[0:2, qt * 128:(qt + 1) * 128], nm[:, u, qt, :], identb[:], True, True, *free, tn,
                             inc=(qt == 3))
                nm_free[u] = (tok,)
                ev = act.do(lambda e, ps=ps: e.activation(mrow[:, qb * 512:(qb + 1) * 512], ps[0:2, :], ACT.Copy),
                            tok)
                ring.free[b] = (ev,)
                unit_ready[qb] = ev
                yield 1

            S = Slots([bank(0), bank(1)])
            Ps = Slots([0, 1, 2])
            obank = [2, 3, 6, 7]
            o_free = [(), (), (), ()]
            bg = Background()

            def scores(qb, kt):
                r = KROWS[kt]
                i, ps, free = S.take()
                q = qb * 512
                k = kt * 128
                for hf in range(2):
                    mm(ps[0:r, :], kT[:, hf, k:k + r], qT[:, hf, q:q + 512], hf == 0, False, *free, unit_ready[qb])
                tok = mm(ps[0:r, :], onesb[0:2, 0:r], mrow[:, q:q + 512], False, not masked, inc=not masked)
                if masked:
                    for qt in range(4):
                        tok = mm(ps[0:r, qt * 128:(qt + 1) * 128], mb[:, 4 * qb + qt, k:k + r], identb[:], False,
                                 qt == 3, mb_ready[4 * qb + qt], inc=(qt == 3))
                bg.tick()
                j, _, pfree = Ps.take()
                ex = act.do(lambda e, ps=ps, r=r, j=j: e.activation(P[0:r, j, :], ps[0:r, :], ACT.Exp, scale=0.0625),
                            tok, *pfree)
                S.free[i] = (ex,)
                return ex, j, r

            def attend(qb, kt, ex, j, r):
                for qt in range(4):
                    tok = mm(PS[:, obank[qt], 0:D + 1], P[0:r, j, qt * 128:(qt + 1) * 128], V[0:r, kt, :], kt == 0,
                             kt == KT - 1, ex, kv["v"][kt], *(o_free[qt] if kt == 0 else ()), inc=(qt == 3))
                    if qt == 1:
                        bg.tick()
                Ps.free[j] = (tok,)
                if kt == KT - 1:
                    for qt in range(4):
                        t = 4 * qb + qt
                        ob = obank[qt]
                        r0 = dve.do(lambda e, ob=ob, qt=qt: e.reciprocal(rden[:, 0, qt:qt + 1], PS[:, ob, D:D + 1]),
                                    tok, dve.last())
                        x_ready[t] = dve.do(lambda e, ob=ob, qt=qt, t=t: e.scalar_tensor_tensor(
                            out=X[:, t, :], in0=PS[:, ob, 0:D], scalar=rden[:, 0, qt:qt + 1], in1=X[:, t, :],
                            op0=ALU.mult, op1=ALU.add), r0, x_ready[t])
                        o_free[qt] = (x_ready[t],)
                bg.tick()

            def first():
                if not kv["k"]:
                    yield from kv["keys"](ring)
                yield from queries(0)
                yield from weave((maxima(0), 19, 0.0, 1.0), (rest(), 23, 0.0, 0.9))

            def rest():
                yield from queries(1)
                yield from queries(2)
                for t in before:
                    yield from t(ring)
                if not kv["v"]:
                    yield from kv["values"](ring)
                yield from queries(3)

            pull(first(), 999)
            ahead = []
            for qb in range(4):
                for kt in range(KT):
                    ahead.append(((qb, kt), scores(qb, kt)))
                    if len(ahead) > 1:
                        (qb0, kt0), got = ahead.pop(0)
                        attend(qb0, kt0, *got)
                    if kt == 0:
                        parts = [(take(aside, n_aside[qb]), n_aside[qb], 0.0, 1.0)]
                        if qb:
                            parts.append((norm_group(qb - 1, ring, q_read[qb - 1], rms=rms), 6, 0.05, 0.7))
                        if qb < 3:
                            parts.append((maxima(qb + 1), 19, 0.0, 0.97))
                        bg.add(weave(*parts))
                        bg.rate = sum(q[1] for q in parts) / ((KT - 1) * 3 - 2)
                bg.flush()
            (qb0, kt0), got = ahead.pop(0)
            attend(qb0, kt0, *got)
            barrier()
            tail.append(lambda ring: norm_group(3, ring, rms=rms))

        def load_mask(mb, mi, L, src, ready, first):
            n = mi.shape[1]
            l_m = [landing(f"l_m{i}{L}") for i in range(n)]
            free = [()] * n
            for t in range(NT):
                i = t % n
                tl = l_m[i].start(sp, mi[:, i, 0:M], src[t * 128:(t + 1) * 128, :], *free[i])
                if t < first:
                    ready[t] = dve.do(lambda e, t=t, i=i: e.tensor_scalar(
                        mb[:, t, :], mi[:, i, 0:M], 0.0, -BIG, ALU.is_equal, ALU.mult), tl)
                else:
                    ready[t] = pooled(lambda e, t=t, i=i: e.tensor_scalar(
                        mb[:, t, :], mi[:, i, 0:M], 0.0, -BIG, ALU.is_equal, ALU.mult), tl)
                free[i] = (ready[t],)

        def split(src, hi, lo, *after, on_act=False):
            if on_act:
                h = act.do(lambda e: e.activation(hi, src, ACT.Copy), *after)
            else:
                h = dve.do(lambda e: e.tensor_copy(hi, src), *after)
            return dve.do(lambda e: e.tensor_tensor(lo, src, hi, ALU.subtract), h)

        def l1_weights(stage, small, uP_at, *after):
            wf_at = stage.at
            wf = sb(stage, "wf", [128, 8, D], F32)
            wpT = nc.alloc_sbuf_tensor_at("wpT", [128, 8, D], F32R, offset=wf_at)
            wp = sb(stage, "wp", [128, 2, 1024], F32)
            wfT = sb(stage, "wfT", [128, 2, 1024], F32R)
            vT = sb(stage, "vT", [128, 2, 16], F32)
            bP = sb(stage, "bP", [16, 96], F32)
            bT = sb(stage, "bT", [16, 16], F32)
            gt = sb(stage, "gt", [128, 1], F32)
            sc = sb(stage, "sc", [128, 10, 4], F32)
            tm = sb(stage, "tmt", [128, 256], F32)
            uT = sb(small, "uT", [96, 1024], F32R)
            u = sb(small, "u1", [128, 8, 16], F32)
            prow = sb(small, "prow", [128, D], F32)
            diag = sb(small, "diag", [128, 128], F32)
            uP = nc.alloc_sbuf_tensor_at("uP", [128, 8, 96], F32, offset=uP_at)
            l_f = landing("l_f")
            sp.wait(*after)
            l_f.start(sp, wf[:], a["L1_ffn_w_fc"].rearrange("(r p) n -> p r n", p=128))
            l_f.start(sp, wp[:], a["L1_ffn_w_proj"].rearrange("(r p) n -> p r n", p=128))
            l_f.start(sp, u[:], a["L1_ffn_u"].rearrange("(r p) n -> p r n", p=128))
            l_f.start(sp, vT[:], a["L1_ffn_vT"].rearrange("(h p) n -> p h n", p=128))
            l_f.start(sp, bT[:], a["L1_ffn_fast_bT"])
            tw = l_f.start(sp, gt[:], a["L1_ffn_gate"].to_broadcast([128, 1]))
            out_ = {"wfT": wfT, "wpT": wpT, "uT": uT, "vT": vT, "bP": bP, "sf": sc, "prow": prow}

            def prepare(ring):
                z0 = pooled(lambda e: e.memset(uP[:], 0.0))
                z1 = pooled(lambda e: e.memset(bP[:], 0.0))
                for i in range(3):
                    zb = pooled(lambda e, i=i: e.tensor_copy(bP[:, 32 * i:32 * i + 16], bT[:]), z1, tw)
                last = ()
                for w_, rows, cols, o in ((wf, 8, D, 0), (wp, 2, 1024, 8)):
                    ts = slice(o, o + rows)
                    d0 = dve.do(lambda e, w_=w_, ts=ts: e.tensor_reduce(sc[:, ts, 0], w_[:], AX.X, ALU.add,
                                                                        apply_absolute_value=True), tw)
                    yield 1
                    d1 = dve.do(lambda e, ts=ts, cols=cols: e.tensor_scalar(sc[:, ts, 0], sc[:, ts, 0], 1.0 / cols,
                                                                            1e-5, ALU.mult, ALU.max), d0)
                    d2 = dve.do(lambda e, ts=ts: e.tensor_scalar(sc[:, ts, 1], sc[:, ts, 0], 0.5, None, ALU.mult),
                                d1)
                    d3 = dve.do(lambda e, ts=ts: e.tensor_scalar(sc[:, ts, 2], sc[:, ts, 0], -0.5, None, ALU.mult),
                                d1)
                    d4 = dve.do(lambda e, ts=ts: e.reciprocal(sc[:, ts, 3], sc[:, ts, 0]), d1)
                    yield 1
                    for r in range(rows):
                        for c0 in range(0, cols, 256):
                            cs = slice(c0, c0 + 256)
                            d5 = dve.do(lambda e, w_=w_, r=r, o=o, cs=cs: e.tensor_scalar(
                                tm[:], w_[:, r, cs], sc[:, o + r, 2:3], None, ALU.is_lt), d3, *last)
                            d6 = dve.do(lambda e, w_=w_, r=r, o=o, cs=cs: e.scalar_tensor_tensor(
                                out=w_[:, r, cs], in0=w_[:, r, cs], scalar=sc[:, o + r, 1:2], in1=tm[:],
                                op0=ALU.is_gt, op1=ALU.subtract), d2, d5)
                            last = (d6,)
                            yield 1
                u0 = dve.do(lambda e: e.tensor_scalar(u[:], u[:], gt[:, 0:1], None, ALU.mult), tw)
                ub = sc[:, 0:8, 3:4].to_broadcast([128, 8, 16])
                for i in range(3):
                    u1 = dve.do(lambda e, i=i: e.tensor_tensor(uP[:, :, 32 * i:32 * i + 16], u[:], ub, ALU.mult),
                                u0, z0, d4)
                yield 1
                ev = ()
                for src, dst, n_out, n_in in ((wf, wfT, 2, 8), (wp, wpT, 8, 2)):
                    done = ev
                    for o in range(n_out):
                        for i0_ in range(0, n_in, 4):
                            b, ps, free = ring.take()
                            m = min(4, n_in - i0_)
                            for i in range(m):
                                tok = pe.do(lambda e, ps=ps, i=i, i0_=i0_, o=o, src=src: e.transpose(
                                    ps[:, i * 128:(i + 1) * 128], src[:, i0_ + i, o * 128:(o + 1) * 128],
                                    identf[:]), *last, *free, inc=(i == m - 1))
                            ev = (act.do(lambda e, ps=ps, m=m, o=o, i0_=i0_, dst=dst: e.activation(
                                dst[:, o, i0_ * 128:(i0_ + m) * 128], ps[:, 0:m * 128], ACT.Copy), tok, *done),)
                            ring.free[b] = ev
                            yield 1
                for i0_ in range(0, 8, 4):
                    b, ps, free = ring.take()
                    for i in range(4):
                        tok = mm(ps[0:96, i * 128:(i + 1) * 128], uP[:, i0_ + i, :], identf[:], True, True, u1,
                                 *free, inc=(i == 3))
                    us = slice(i0_ * 128, i0_ * 128 + 512)
                    e1 = act.do(lambda e, ps=ps, us=us: e.activation(uT[:, us], ps[0:96, :], ACT.Copy), tok)
                    e2 = dve.do(lambda e, ps=ps, us=us: e.tensor_tensor(uT[64:96, us], ps[64:96, :], uT[64:96, us],
                                                                        ALU.subtract), e1)
                    ring.free[b] = (e2,)
                    yield 1
                b, ps, free = ring.take()
                for i in range(2):
                    g0 = dve.do(lambda e, i=i: e.tensor_scalar(diag[:], identf[:], sc[:, 8 + i, 0:1], None, ALU.mult),
                                d1, *((tok,) if i else ()))
                    tok = mm(ps[:, i * 128:(i + 1) * 128], onesf[:], diag[:], True, True, g0, *free, inc=True)
                e3 = act.do(lambda e, ps=ps: e.activation(prow[:], ps[:, 0:D], ACT.Copy), tok)
                ring.free[b] = (e3,)
                out_["ready"] = (e3, e2, zb)
                yield 1
            return out_, prepare

        def l1_ffn(scope, k, before):
            up = Slots([bank(b) for b in (0, 1, 4, 5)])
            wfT, wpT, uT, vT, bP, sf, prow = (k[n] for n in ("wfT", "wpT", "uT", "vT", "bP", "sf", "prow"))
            z1 = sb(scope, "z1", [16, 2, 512], F32)
            z2 = sb(scope, "z2", [96, 2, 512], F32R)
            xh = sb(scope, "xh1", [128, 2, 2, 512], F32R)
            xl = sb(scope, "xl1", [128, 2, 2, 512], F32R)
            r1 = sb(scope, "r1", [128, 2, 512], F32)
            r2 = sb(scope, "r2", [128, 2, 512], F32)
            rh = sb(scope, "rh", [128, 12, 512], F32R)
            rl = sb(scope, "rl", [128, 12, 512], F32R)
            yo = sb(scope, "yo1", [128, 2, D], F32)
            for q_ in (pe, act, dve):
                q_.wait(*k["ready"])
            down = Slots([bank(b) for b in (2, 3, 6, 7)])
            r1s = Slots([0, 1])
            r2s = Slots([0, 1])
            ys = Slots([0, 1])
            chunks = Slots(list(range(12)))
            free2 = {"x": [(), ()], "z": [(), ()]}
            made = {}
            xn_read = {}

            def rise(qb):
                q = slice(qb * 512, (qb + 1) * 512)
                s = qb % 2
                e0 = split(xnT[:, :, q], xh[:, s, :, :], xl[:, s, :, :], xn_ready[qb], *free2["x"][s])
                b, ps, free = up.take()
                for hf in range(2):
                    tok = mm(ps[0:16, :], vT[:, hf, :], xnT[:, hf, q], hf == 0, hf == 1, *free, xn_ready[qb],
                             inc=(hf == 1))
                xn_read[qb] = (e0, tok)
                e1 = act.do(lambda e, ps=ps: e.activation(z1[:, s, :], ps[0:16, :], ACT.Copy), tok, *free2["z"][s])
                up.free[b] = (e1,)
                b, ps, free = up.take()
                tok = mm(ps[0:96, :], bP[:], z1[:, s, :], True, True, e1, *free, inc=True)
                free2["z"][s] = (tok,)
                e2 = act.do(lambda e, ps=ps: e.activation(z2[:, s, :], ps[0:96, :], ACT.Copy), tok, *free2["x"][s])
                e3 = dve.do(lambda e, ps=ps: e.tensor_tensor(z2[32:64, s, :], ps[32:64, :], z2[32:64, s, :],
                                                             ALU.subtract), e2)
                up.free[b] = (e3,)
                yield 1
                for f in range(8):
                    b, ps, free = up.take()
                    fs = slice(f * 128, (f + 1) * 128)
                    for hf in range(2):
                        mm(ps, wfT[:, hf, fs], xh[:, s, hf, :], hf == 0, False, *free, e0)
                        mm(ps, wfT[:, hf, fs], xl[:, s, hf, :], False, False)
                    tok = mm(ps, uT[:, fs], z2[:, s, :], False, True, e3, inc=True)
                    j, _, rfree = r1s.take()
                    e4 = act.do(lambda e, ps=ps, j=j, f=f: e.activation(r1[:, j, :], ps, ACT.Relu,
                                                                        scale=sf[:, f, 0:1]), tok, *rfree)
                    up.free[b] = (e4,)
                    i, _, rfree = r2s.take()
                    e5 = act.do(lambda e, j=j, i=i: e.activation(r2[:, i, :], r1[:, j, :], ACT.Square), e4, *rfree)
                    r1s.free[j] = (e5,)
                    c, _, cfree = chunks.take()
                    made[qb, f] = (c, split(r2[:, i, :], rh[:, c, :], rl[:, c, :], e5, *cfree))
                    r2s.free[i] = (made[qb, f][1],)
                    yield 1
                free2["x"][s] = (tok,)

            def fall(qb):
                out_ = [down.take() for _ in range(4)]
                for f in range(8):
                    c, e6 = made[qb, f]
                    for qt, (b, ps, free) in enumerate(out_):
                        qs = slice(qt * 128, (qt + 1) * 128)
                        mm(ps[:, 0:D], rh[:, c, qs], wpT[:, f, :], f == 0, False, e6, *free)
                        tok = mm(ps[:, 0:D], rl[:, c, qs], wpT[:, f, :], False, f == 7, inc=True)
                    chunks.free[c] = (tok,)
                    yield 1
                for qt, (b, ps, free) in enumerate(out_):
                    t = 4 * qb + qt
                    j, _, yfree = ys.take()
                    y0 = dve.do(lambda e, ps=ps, j=j: e.tensor_tensor(yo[:, j, :], ps[:, 0:D], prow[:], ALU.mult),
                                tok, *yfree)
                    down.free[b] = (y0,)
                    x_ready[t] = dve.do(lambda e, t=t, j=j: e.tensor_tensor(X[:, t, :], yo[:, j, :], X[:, t, :],
                                                                            ALU.add), y0, x_ready[t])
                    ys.free[j] = (x_ready[t],)

            ffn_order(rise, fall, up, xn_read, before, False)

        def ffn_order(rise, fall, up, xn_read, before, rms):
            pull(weave((rise(0), 9, 0.0, 1.0), *[(t(up), 6, 0.0, 1.0) for t in before]), 99)
            pe.wait(dve.last(), act.last())
            for qb in range(4):
                parts = [(fall(qb), 9, 0.0, 1.0)]
                if qb < 3:
                    parts.append((rise(qb + 1), 9, 0.0, 1.0))
                if qb:
                    parts.append((norm_group(qb - 1, up, *xn_read[qb - 1], rms=rms), 6, 0.05, 0.9))
                pull(weave(*parts), 99)
            barrier()
            tail.append(lambda ring: norm_group(3, ring, rms=rms))

        def l2_weights(region):
            at = region.at
            wu = sb(region, "wu", [128, 2048], F32)
            wd = sb(region, "wd", [128, 2048], F32)
            tu = nc.alloc_sbuf_tensor_at("tu", [128, 2048], F32R, offset=at)
            td = nc.alloc_sbuf_tensor_at("td", [128, 2048], F32R, offset=at + 8192)
            tm = sb(region, "tm2", [128, 512], F32)
            al = sb(region, "al", [128, 2, 4], F32)
            l_f = landing("l_f2")
            l_f.start(sp, wu[:].rearrange("p (h n) -> p h n", h=2), a["L2_ffn_w_upT"].rearrange("(h p) n -> p h n", p=128))
            tw = l_f.start(sp, wd[:].rearrange("p (h n) -> p h n", h=8),
                           a["L2_ffn_w_downT"].rearrange("(h p) n -> p h n", p=128))
            out_ = {"wu": tu[:].rearrange("p (h n) -> p h n", h=2), "wd": td[:].rearrange("p (h n) -> p h n", h=8)}

            def prepare(b0):
                last = ()
                for i, (w_, t_) in enumerate(((wu, tu), (wd, td))):
                    d0 = dve.do(lambda e, w_=w_, i=i: e.tensor_reduce(al[:, i, 0:1], w_[:], AX.X, ALU.add,
                                                                      apply_absolute_value=True), tw)
                    yield 1
                    b, ps, free = b0.take()
                    d1 = mm(ps[:, 0:1], onesf[:], al[:, i, 0:1], True, True, d0, *free, inc=True)
                    d2 = dve.do(lambda e, i=i, ps=ps: e.tensor_scalar(al[:, i, 1:2], ps[:, 0:1], 0.5 / (1024 * D),
                                                                      None, ALU.mult), d1)
                    d3 = dve.do(lambda e, i=i, ps=ps: e.tensor_scalar(al[:, i, 2:3], ps[:, 0:1], -0.5 / (1024 * D),
                                                                      None, ALU.mult), d1)
                    b0.free[b] = (d3,)
                    yield 1
                    for c in range(4):
                        cs = slice(c * 512, c * 512 + 512)
                        d4 = dve.do(lambda e, w_=w_, i=i, cs=cs: e.tensor_scalar(tm[:], w_[:, cs], al[:, i, 2:3],
                                                                                 None, ALU.is_lt), d3, d2, *last)
                        d5 = dve.do(lambda e, w_=w_, t_=t_, i=i, cs=cs: e.scalar_tensor_tensor(
                            out=t_[:, cs], in0=w_[:, cs], scalar=al[:, i, 1:2], in1=tm[:], op0=ALU.is_gt,
                            op1=ALU.subtract), d4)
                        last = (d5,)
                        yield 1
                out_["ready"] = last
            return out_, prepare

        def l2_ffn(scope, scope1, scope2, k, before):
            up = Slots([bank(b) for b in (0, 1, 4)])
            sums = Slots([bank(5)])
            wu, wd = k["wu"], k["wd"]
            xh = sb(scope1, "xh2", [128, 2, 2, 512], F32R)
            xl = sb(scope2, "xl2", [128, 2, 2, 512], F32R)
            hT = sb(scope, "hT2", [128, 2, 512], F32)
            h2 = sb(scope1, "h2", [128, 1, 512], F32)
            hs = sb(scope1, "hs", [128, 2, 512], F32)
            hh = sb(scope, "hh2", [128, 12, 512], F32R)
            hl = sb(scope, "hl2", [128, 12, 512], F32R)
            nr = sb(scope, "nr", [128, NT, 4], F32)
            for q_ in (pe, dve):
                q_.wait(*k["ready"])
            chunks = Slots(list(range(12)))
            xn_read = {}
            down = Slots([bank(b) for b in (2, 3, 6, 7)])
            hTs = Slots([0, 1])
            h2s = Slots([0])
            free2 = {"x": [(), ()], "s": [(), ()]}
            made, summed = {}, {}

            def rise(qb):
                q = slice(qb * 512, (qb + 1) * 512)
                s = qb % 2
                e0 = split(xnT[:, :, q], xh[:, s, :, :], xl[:, s, :, :], xn_ready[qb], *free2["x"][s])
                xn_read[qb] = (e0,)
                yield 1
                acc = None
                for f in range(8):
                    b, ps, free = up.take()
                    fs = slice(f * 128, (f + 1) * 128)
                    for hf in range(2):
                        mm(ps, wu[:, hf, fs], xh[:, s, hf, :], hf == 0, False, *free, e0)
                        tok = mm(ps, wu[:, hf, fs], xl[:, s, hf, :], False, hf == 1, inc=(hf == 1))
                    j, _, jfree = hTs.take()
                    e1 = act.do(lambda e, ps=ps, j=j: e.activation(hT[:, j, :], ps, ACT.Gelu), tok, *jfree)
                    up.free[b] = (e1,)
                    i, _, ifree = h2s.take()
                    o = hs[:, s, :] if f == 0 else h2[:, i, :]
                    ofree = free2["s"][s] if f == 0 else ifree
                    e2 = act.do(lambda e, j=j, o=o: e.activation(o, hT[:, j, :], ACT.Square), e1, *ofree)
                    c, _, cfree = chunks.take()
                    e3 = split(hT[:, j, :], hh[:, c, :], hl[:, c, :], e1, *cfree)
                    made[qb, f] = (c, e3)
                    hTs.free[j] = (e2, e3)
                    if f == 0:
                        acc = e2
                    else:
                        acc = dve.do(lambda e, i=i: e.tensor_tensor(hs[:, s, :], hs[:, s, :], h2[:, i, :], ALU.add),
                                     e2, acc)
                        h2s.free[i] = (acc,)
                    yield 1
                free2["x"][s] = (tok,)
                summed[qb] = acc

            def norms(qb):
                s = qb % 2
                ts = slice(4 * qb, 4 * qb + 4)
                acc = summed[qb]
                b, ps, free = sums.take()
                for qt in range(4):
                    tok = mm(ps[:, qt:qt + 1], hs[:, s, qt * 128:(qt + 1) * 128], onesf[:, 0:1], True, True, acc,
                             *free, inc=(qt == 3))
                free2["s"][s] = (tok,)
                n0 = dve.do(lambda e, ps=ps: e.tensor_scalar(nr[:, ts, 0], ps[:, 0:4], 1.0 / 1024, None, ALU.mult),
                            tok)
                sums.free[b] = (n0,)
                n1 = act.do(lambda e: e.activation(nr[:, ts, 1], nr[:, ts, 0], ACT.Sqrt), n0)
                n2 = dve.do(lambda e: e.tensor_scalar(nr[:, ts, 2], nr[:, ts, 1], 1e-8, None, ALU.add), n1)
                return dve.do(lambda e: e.reciprocal(nr[:, ts, 3], nr[:, ts, 2]), n2)

            def fall(qb):
                out_ = [down.take() for _ in range(4)]
                for f in range(8):
                    c, e3 = made[qb, f]
                    for qt, (b, ps, free) in enumerate(out_):
                        qs = slice(qt * 128, (qt + 1) * 128)
                        mm(ps[:, 0:D], hh[:, c, qs], wd[:, f, :], f == 0, False, e3, *free)
                        tok = mm(ps[:, 0:D], hl[:, c, qs], wd[:, f, :], False, f == 7, inc=True)
                    chunks.free[c] = (tok,)
                    if f == 1:
                        n3 = norms(qb)
                    yield 1
                for qt, (b, ps, free) in enumerate(out_):
                    t = 4 * qb + qt
                    x_ready[t] = dve.do(lambda e, t=t, ps=ps: e.scalar_tensor_tensor(
                        out=X[:, t, :], in0=ps[:, 0:D], scalar=nr[:, t, 3:4], in1=X[:, t, :], op0=ALU.mult,
                        op1=ALU.add), tok, n3, x_ready[t])
                    down.free[b] = (x_ready[t],)

            ffn_order(rise, fall, up, xn_read, before, False)

        def l3_projections(region):
            wk = sb(region, "wk3", [128, 2, D], F32)
            wq = sb(region, "wq3", [128, 2, D], F32)
            bq = sb(region, "bq3", [128, 2], F32)
            bk = sb(region, "bk3", [128, 2], F32)
            l_j = landing("l_j")
            for d, n in ((wk, "WkT"), (wq, "WqT")):
                l_j.start(sp, d[:], a["L3_xattn_" + n].rearrange("(h p) n -> p h n", p=128))
            l_j.start(sp, bq[:], a["L3_xattn_bq"])
            return wk, wq, bk, bq, l_j.start(sp, bk[:], a["L3_xattn_bk"])

        def l3_attention(V, Ks, scope, P_at, Qs, kq, mb, mb_ready, before, next_load):
            wk, wq, bk, bq, t_kq = kq
            wo = sb(scope, "wo3", [64, 4, D], F32)
            bo = sb(scope, "bo3", [1, D], F32)
            T = sb(scope, "T3", [128, 3, 3, 512], BF16)
            pm = sb(scope, "pm3", [128, 2, 64], F32)
            mx = sb(scope, "mx3", [128, 2, 16], F32)
            nm = sb(scope, "nm3", [128, 2, 16, 3], BF16)
            P = nc.alloc_sbuf_tensor_at("P3", [128, 4, 2, 512], F32, offset=P_at)
            tmp = Region(nc, P_at + 4096 + 64, P_at + 16384)
            F = sb(tmp, "F3", [128, 3, 512], F32)
            wv = sb(tmp, "wv3", [128, 2, 272], F32)
            bv = sb(tmp, "bv3", [1, 272], F32)
            Or = big[:, 0:1024].rearrange("p (u n) -> p u n", u=2)
            OT = big[:, 1024:1536].rearrange("p (u t n) -> p u t n", u=2, t=4)
            On = big[0:64, 1536:2560].rearrange("p (u n) -> p u n", u=2)
            rs = big[:, 2560:2592].rearrange("p (u t n) -> p u t n", u=2, t=4)
            qd = nc.dram_tensor("q_parts", [3, D, N], BF16, kind="Internal").ap()
            kd = nc.dram_tensor("k_parts", [3, D, M], BF16, kind="Internal").ap()
            l_w.start(sp, wv[:], a["L3_WvP"].rearrange("(h p) n -> p h n", p=128))
            tw = l_w.start(sp, bv[:], a["L3_bvP"])
            l_o3 = landing("l_o3")
            l_o3.start(sp, wo[:], a["L3_xattn_WoT"].rearrange("(h p) n -> p h n", p=64))
            t_wo = l_o3.start(sp, bo[:], a["L3_xattn_bo"])
            ring = Slots([bank(4), bank(5), bank(7)])
            ts = Slots([0, 1, 2])
            l_t = [landing(f"l_t{i}") for i in range(3)]
            l_s = [landing(f"l_s{i}") for i in range(2)]
            written = {}
            act.wait(t_kq)
            same = sb(tmp, "same3", [99, 401], F32)
            pick = sb(tmp, "pick3", [128, 6], BF16)
            flags = sb(tmp, "flags3", [99, 4], F32)
            flag = sb(tmp, "flag3", [99, 1], I32)
            ones = sb(tmp, "ones3", [1, 401], BF16)
            m0 = pooled(lambda e: e.memset(ones[:], 1.0))
            m1 = pooled(lambda e: e.memset(pick[:], 0.0))
            m2 = pooled(lambda e: e.memset(pick[:, 2:3], 1.0), m1)
            m3 = pooled(lambda e: e.memset(pick[:, 3:5], 1.0), m1)
            m4 = pooled(lambda e: e.memset(nm[:, :, :, 2:3], 1.0))
            pe.wait(m0, m2, m3, m4)

            def uniform():
                got = []
                for c, (k0, kn) in enumerate(CHUNKS):
                    ps = bank(c)[96:99, 0:kn]
                    for t in range(NT):
                        mm(ps, pick[:, 0:3], mb[:, t, k0:k0 + kn], t == 0, False, mb_ready[t])
                        if t % 8 == 7:
                            yield 1
                    tok = mm(ps, pick[0:1, 3:6], ones[:, 0:kn], False, True, inc=True)
                    d0 = dve.do(lambda e, ps=ps, kn=kn: e.tensor_scalar(same[96:99, 0:kn], ps, 0.0, None,
                                                                        ALU.is_equal), tok, *got)
                    d1 = dve.do(lambda e, ps=ps, kn=kn: e.scalar_tensor_tensor(
                        out=same[96:99, 0:kn], in0=ps, scalar=-BIG * N, in1=same[96:99, 0:kn], op0=ALU.is_equal,
                        op1=ALU.add), d0)
                    d2 = dve.do(lambda e, c=c, kn=kn: e.tensor_reduce(flags[96:99, c:c + 1], same[96:99, 0:kn], AX.X,
                                                                      ALU.min), d1)
                    got = (d2,)
                    for i in range(2):
                        e0 = act.do(lambda e, i=i, ps=ps, k0=k0, kn=kn: e.activation(
                            Ks[96:99, i, :, k0:k0 + kn], ps.unsqueeze(1).to_broadcast([3, 4, kn]), ACT.Copy), d1)
                    S.free[c // 2] = (e0,)
                    yield 1
                d3 = dve.do(lambda e: e.tensor_reduce(flags[96:99, 0:1], flags[96:99, 0:4], AX.X, ALU.min), d2)
                d4 = dve.do(lambda e: e.tensor_copy(flag[96:99, :], flags[96:99, 0:1]), d3)
                known.append((d4, e0))
                yield 1

            known = []
            S = Slots([(0, 1), (2, 3)])

            def project(keys, half, c):
                src, w_, dd, bias = (ctxT, wk, kd, bk) if keys else (xnT, wq, qd, bq)
                c0, cn = CHUNKS[c] if keys else (512 * c, 512)
                b, ps, free = ring.take()
                for hf in range(2):
                    tok = mm(ps[:, 0:cn], w_[:, hf, half * 128:(half + 1) * 128], src[:, hf, c0:c0 + cn], hf == 0,
                             hf == 1, *free, t_kq, *(() if keys else (xn_ready[c],)), inc=(hf == 1))
                j, _, tfree = ts.take()
                e0 = act.do(lambda e: e.activation(F[:, j, 0:cn], ps[:, 0:cn], ACT.Identity,
                                                   bias=bias[:, half:half + 1]), tok, *tfree)
                ring.free[b] = (e0,)
                e1 = act.do(lambda e: e.activation(T[:, j, 0, 0:cn], F[:, j, 0:cn], ACT.Copy), e0, *tfree)
                e2 = dve.do(lambda e: e.tensor_tensor(F[:, j, 0:cn], F[:, j, 0:cn], T[:, j, 0, 0:cn], ALU.subtract),
                            e1)
                e3 = act.do(lambda e: e.activation(T[:, j, 1, 0:cn], F[:, j, 0:cn], ACT.Copy), e2)
                e4 = dve.do(lambda e: e.tensor_tensor(T[:, j, 2, 0:cn], F[:, j, 0:cn], T[:, j, 1, 0:cn],
                                                      ALU.subtract), e3)
                tl = l_t[j].start(sp, dd[:, half * 128:(half + 1) * 128, c0:c0 + cn].rearrange("s p n -> p s n"),
                                  T[:, j, :, 0:cn], e4)
                ts.free[j] = (tl,)
                written.setdefault(half, []).append(tl)
                if not keys:
                    xn_read.setdefault(c, []).append(tok)

            def values():
                for kt in range(KT):
                    r = KROWS[kt]
                    b, ps, free = ring.take()
                    for hf in range(2):
                        mm(ps[0:r, 0:272], ctxT[:, hf, kt * 128:kt * 128 + r], wv[:, hf, :], hf == 0, False, *free, tw)
                    tok = mm(ps[0:r, 0:272], onesf[0:1, 0:r], bv[:], False, True, inc=True)
                    ev = act.do(lambda e, ps=ps, r=r, kt=kt: e.activation(V[0:r, kt, :], ps[0:r, 0:272], ACT.Copy),
                                tok)
                    ring.free[b] = (ev,)
                    yield 1

            xn_read = {}
            qparts = (0, 1, 0, 1, 2, 0)
            kparts = (0, 0, 1, 1, 0, 2)
            stack_free = {0: (), 1: ()}
            stack_ready = {}

            def load_stack(g):
                s = g % 2
                sp.wait(*written[g // 2])
                for blk in range(6):
                    l_s[s].start(sp, Qs[16 * blk:16 * blk + 16, s, :, :],
                                 qd[qparts[blk], g * 64:(g + 1) * 64, :].rearrange("(h p) n -> p h n", p=16),
                                 *stack_free[s])
                    stack_ready[g] = l_s[s].start(
                        sp, Ks[16 * blk:16 * blk + 16, s, :, :],
                        kd[kparts[blk], g * 64:(g + 1) * 64, :].rearrange("(h p) n -> p h n", p=16))

            def firsts():
                for c in range(4):
                    project(True, 0, c)
                    yield 1
                for c in range(4):
                    project(False, 0, c)
                    yield 1

            def seconds():
                for c in range(4):
                    project(True, 1, c)
                    yield 1
                    project(False, 1, c)
                    yield 1

            def serial(gens):
                for gen in gens:
                    yield from gen

            parts = [(t(ring), 6, 0.0, 0.9) for t in before]
            pull(weave((firsts(), 8, 0.0, 1.0), *parts), 999)
            load_stack(0)
            load_stack(1)
            unit_ready = {}
            nm_free = {0: (), 1: ()}

            def maxima(g, qb):
                s = g % 2
                u = (4 * g + qb) % 2
                pe.wait(stack_ready[g])
                act.wait(stack_ready[g])
                tiles = []
                for h in range(4):
                    for qt in range(4):
                        q0 = qb * 512 + qt * 128
                        t = 4 * qb + qt
                        tiles.append((h * 4 + qt, ([Qs[0:96, s, h, q0:q0 + 128]],
                                                   lambda k0, kn, h=h: [Ks[0:96, s, h, k0:k0 + kn]],
                                                   (mb[:, t, :], mb_ready[t]))))
                yield from head_max(tiles, ring, pm[:, u, :], mb)
                tn = max_rows(16, pm[:, u, :], mx[:, u, :], nm[:, u, :, :], nm_free[u])
                for _ in range(4):
                    yield 1
                for h in range(4):
                    b, ps, free = ring.take()
                    for qt in range(4):
                        tok = mm(ps[96:99, qt * 128:(qt + 1) * 128], nm[:, u, h * 4 + qt, :], identb[:], True, True,
                                 *free, tn, inc=(qt == 3))
                    ev = act.do(lambda e, ps=ps, h=h: e.activation(
                        Qs[96:99, s, h, qb * 512:(qb + 1) * 512], ps[96:99, :], ACT.Copy), tok)
                    ring.free[b] = (ev,)
                    yield 1
                nm_free[u] = (tok,)
                unit_ready[g, qb] = ev

            Ps = Slots([0, 1, 2, 3])
            o_free = [(dve.do(lambda e: e.memset(bank(6), 0.0)),)]
            bg = Background()
            units = [(g, qb) for g in range(4) for qb in range(4)]
            stream = Stream(maxima, units, stack_ready, unit_ready, 1.15)

            def tick():
                bg.tick()
                stream.tick()

            def scores(g, qb, kt, pr):
                s = g % 2
                r = KROWS[kt]
                k = kt * 128
                i, banks, free = S.take()
                pe.wait(*free, unit_ready[g, qb])
                q = slice(qb * 512, (qb + 1) * 512)
                for hh in range(2):
                    h = 2 * pr + hh
                    ps = bank(banks[hh])[0:r, :]
                    whole = [lambda e, ps=ps, h=h: e.matmul(ps, Ks[0:99, s, h, k:k + r], Qs[0:99, s, h, q],
                                                            start=True, stop=True)]
                    masked = [lambda e, ps=ps, h=h: e.matmul(ps, Ks[0:98, s, h, k:k + r], Qs[0:98, s, h, q],
                                                             start=True, stop=False)]
                    for qt in range(4):
                        masked.append(lambda e, ps=ps, qt=qt: e.matmul(
                            ps[:, qt * 128:(qt + 1) * 128], mb[:, 4 * qb + qt, k:k + r], identb[:], start=False,
                            stop=(qt == 3)))
                    tok = pe.either(masked, whole)
                    tick()
                j, _, pfree = Ps.take()
                ex = act.do(lambda e, banks=banks, r=r, j=j: e.activation(
                    P[0:r, j, :, :], PS[0:r, banks[0]:banks[0] + 2, :], ACT.Exp, scale=0.25), tok, *pfree)
                S.free[i] = (ex,)
                return ex, j

            def attend(g, qb, kt, got):
                r = KROWS[kt]
                if kt == 0:
                    pe.wait(*o_free[0])
                for c in range(4):
                    ex, j = got[c // 2]
                    tok = mm(PS[32 * c:32 * c + 17, 6, :], V[0:r, kt, (4 * g + c) * 17:(4 * g + c) * 17 + 17],
                             P[0:r, j, c % 2, :], kt == 0, kt == KT - 1, ex, inc=(c == 3))
                for ex, j in got:
                    Ps.free[j] = (tok,)
                tick()
                return tok

            or_free = {0: (), 1: ()}

            def finish(g, qb, tok):
                u = (4 * g + qb) % 2
                d0 = act.do(lambda e: e.activation(Or[:, u, :], PS[:, 6, :], ACT.Copy), tok, *or_free[u])
                o_free[0] = (d0,)
                done = []

                def divide():
                    b, ps, free = ring.take()
                    for qt in range(4):
                        tk = pe.do(lambda e, ps=ps, qt=qt: e.transpose(
                            ps[:, qt * 128:(qt + 1) * 128], Or[:, u, qt * 128:(qt + 1) * 128], identf[:]), d0, *free,
                            inc=(qt == 3))
                    rows = ps.rearrange("p (t c n) -> p t c n", t=4, c=4)
                    d1 = dve.do(lambda e: e.reciprocal(rs[:, u, :, :], rows[:, :, :, 16]), tk)
                    d2 = dve.do(lambda e: e.tensor_tensor(
                        OT[:, u, :, :].rearrange("p t (c n) -> p t c n", c=4), rows[:, :, :, 0:16],
                        rs[:, u, :, :].unsqueeze(3).to_broadcast([128, 4, 4, 16]), ALU.mult), d1, *or_free[u])
                    ring.free[b] = (d2,)
                    yield 1
                    yield 1
                    yield 1
                    b, ps, free = ring.take()
                    for qt in range(4):
                        tk = pe.do(lambda e, ps=ps, qt=qt: e.transpose(
                            ps[0:64, qt * 128:(qt + 1) * 128], OT[:, u, qt, :], identf[:]), d2, *free, inc=(qt == 3))
                    done.append(act.do(lambda e, ps=ps: e.activation(On[:, u, :], ps[0:64, :], ACT.Copy), tk,
                                       *or_free[u]))
                    ring.free[b] = (done[0],)
                    yield 1

                def project():
                    d2 = done[0]
                    for qt in range(4):
                        b, ps, free = ring.take()
                        tk = mm(ps[:, 0:D], On[:, u, qt * 128:(qt + 1) * 128], wo[:, g, :], True, g != 0, *free, d2,
                                inc=(g != 0))
                        if g == 0:
                            tk = mm(ps[:, 0:D], onesf[0:1, :], bo[:], False, True, inc=True)
                        ring.free[b] = (add_residual(4 * qb + qt, ps[:, 0:D], tk),)
                        yield 1
                    or_free[u] = (tk, d2)
                    if g == 3:
                        yield from norm_group(qb, ring, *xn_read[qb])
                return divide(), project()

            pull(weave((maxima(0, 0), 74, 0.0, 1.0), (serial([uniform(), values(), seconds()]), 34, 0.0, 0.8)), 999)
            d4, e0 = known[0]
            pe.wait(d4, e0, mb_ready[-1])
            pe.diverge(flag[98:99, :])
            for i in range(4):
                Ps.free[i] = (pe.last(), act.last(), dve.last())
            pe.wait(t_wo)
            ahead = []
            for u, (g, qb) in enumerate(units):
                stream.reach(u)
                for kt in range(KT):
                    got = [scores(g, qb, kt, 0)]
                    if ahead:
                        (g0, qb0, kt0), got0 = ahead.pop(0)
                        tok = attend(g0, qb0, kt0, got0)
                    got.append(scores(g, qb, kt, 1))
                    ahead.append(((g, qb, kt), got))
                    if kt == 0:
                        parts = []
                        if u:
                            dv, pj = finish(g0, qb0, tok)
                            parts += [(dv, 5, 0.03, 0.5), (pj, 8 if g0 == 3 else 4, 0.55, 1.0)]
                            if qb0 == 3:
                                stack_free[g0 % 2] = (tok,)
                                if g0 + 2 < 4:
                                    load_stack(g0 + 2)
                                elif g0 == 2:
                                    next_load(tok)
                        bg.add(weave(*parts))
                        bg.rate = (sum(q[1] for q in parts)) / ((KT - 1) * 5 - 2)
                bg.flush()
            (g0, qb0, kt0), got0 = ahead.pop(0)
            tok = attend(g0, qb0, kt0, got0)
            pe.merge()
            barrier()
            tail.extend(finish(g0, qb0, tok))

        class Experts:

            def __init__(self, at):
                self.W = nc.alloc_sbuf_tensor_at("We", [128, 3, 4096], F32, offset=at)
                self.WL = nc.alloc_sbuf_tensor_at("WeL", [128, 3, 4096], F32R, offset=at)
                self.land = [[landing(f"l_e{i}{j}") for j in range(2)] for i in range(3)]
                self.free = [[(), ()] for _ in range(3)]
                self.ready = {}

            def load(self, e_, j, *after):
                s = e_ % 3
                if e_ < 8:
                    self.ready[e_, j] = self.land[s][j].start(
                        sp, self.W[:, s, 2048 * j:2048 * j + 2048].rearrange("p (h n) -> p h n", h=(2, 8)[j]),
                        a[("L3_ffn_w1", "L3_ffn_w2")[j]][e_].rearrange("(h p) n -> p h n", p=128),
                        *self.free[s][j], *after)

        def l3_ffn(xe, high, scope, scope2, before):
            W, WL, load, w_free, w_ready = xe.W, xe.WL, xe.load, xe.free, xe.ready
            WH = sb(high, "WeH", [128, 3, 4096], F32R)
            b2 = nc.alloc_sbuf_tensor_at("b2", [1, 8 * D], F32, offset=BIG_AT + 8192)
            b2l = nc.alloc_sbuf_tensor_at("b2l", [1, 8 * D], F32R, offset=BIG_AT + 8192)
            b2h = nc.alloc_sbuf_tensor_at("b2h", [1, 8 * D], F32R, offset=BIG_AT)
            oner = sb(scope, "oner", [1, 128], F32R)
            xh = sb(scope, "xh3", [128, 2, 2, 256], F32R)
            xl = sb(scope, "xl3", [128, 2, 2, 256], F32R)
            hT = sb(scope, "hT3", [128, 2, 256], F32)
            hh = sb(scope2, "hh3", [128, 2, 8, 256], F32R)
            hl = sb(scope2, "hl3", [128, 2, 8, 256], F32R)
            parts_ready = {}

            for i in range(1, 3):
                load(i, 0)
                load(i, 1)
            b0 = pooled(lambda e: e.tensor_copy(oner[:], onesf[0:1, :]))

            def part(e_):
                s = u = e_ % 3
                got = []
                for c in range(4):
                    cs = slice(1024 * c, 1024 * c + 1024)
                    h = act.do(lambda e, cs=cs: e.activation(WH[:, u, cs], W[:, s, cs], ACT.Copy),
                               w_ready[e_, c // 2], *w_free[s][c // 2])
                    if c < 3:
                        g = dve.do(lambda e, cs=cs: e.tensor_tensor(WL[:, s, cs], W[:, s, cs], WH[:, u, cs],
                                                                    ALU.subtract), h)
                    else:
                        g = pooled(lambda e, cs=cs: e.tensor_tensor(WL[:, s, cs], W[:, s, cs], WH[:, u, cs],
                                                                    ALU.subtract), h)
                    got.append(g)
                    parts_ready[e_] = list(got)
                    yield 1

            up = Slots([bank(b) for b in range(4)])
            down = Slots([bank(b) for b in range(4, 8)])
            hTs = Slots([0, 1])
            x_free = [(), ()]
            h_free = [(), ()]
            made = {}

            x_parts = {}

            def split_x(e_):
                s = e_ % 2
                if e_ < 8:
                    x_parts[e_] = split(xnT[:, :, e_ * 256:(e_ + 1) * 256], xh[:, s, :, :], xl[:, s, :, :],
                                        xn_ready[e_ // 2], *x_free[s])

            def rise(e_):
                s, u, w = e_ % 2, e_ % 3, e_ % 3
                e0 = x_parts[e_]
                for f in range(8):
                    b, ps, free = up.take()
                    ps = ps[:, 0:256]
                    for hf in range(2):
                        fs = slice(hf * 1024 + f * 128, hf * 1024 + f * 128 + 128)
                        mm(ps, WH[:, u, fs], xh[:, s, hf, :], hf == 0, False, *free, e0, *parts_ready[e_][:2])
                        mm(ps, WH[:, u, fs], xl[:, s, hf, :], False, False)
                        tok = mm(ps, WL[:, w, fs], xh[:, s, hf, :], False, hf == 1, inc=(hf == 1))
                    j, _, jfree = hTs.take()
                    e1 = act.do(lambda e, ps=ps, j=j, f=f: e.activation(
                        hT[:, j, :], ps, ACT.Gelu_apprx_tanh, bias=b1[:, e_ * 8 + f:e_ * 8 + f + 1]), tok, *jfree)
                    up.free[b] = (e1,)
                    e2 = split(hT[:, j, :], hh[:, s, f, :], hl[:, s, f, :], e1, *h_free[s])
                    hTs.free[j] = (e2,)
                    yield 1
                    if f == 3:
                        split_x(e_ + 1)
                x_free[s] = (tok,)
                w_free[w][0] = (tok,)
                load(e_ + 3, 0)
                made[e_] = e2

            def fall(e_):
                s, u, w = e_ % 2, e_ % 3, e_ % 3
                for i in range(2):
                    t = 2 * e_ + i
                    qs = slice(i * 128, (i + 1) * 128)
                    b, ps, free = down.take()
                    ps = ps[:, 0:D]
                    for f in range(8):
                        fs = slice(2048 + f * D, 2048 + (f + 1) * D)
                        mm(ps, hh[:, s, f, qs], WH[:, u, fs], f == 0, False, made[e_], *free, *parts_ready[e_])
                        mm(ps, hl[:, s, f, qs], WH[:, u, fs], False, False)
                        mm(ps, hh[:, s, f, qs], WL[:, w, fs], False, False)
                        if f % 2:
                            yield 1
                    es = slice(e_ * D, (e_ + 1) * D)
                    mm(ps, oner[:], b2h[:, es], False, False, bl, b0)
                    tok = mm(ps, oner[:], b2l[:, es], False, True, inc=True)
                    down.free[b] = (add_residual(t, ps, tok),)
                    l_out.start(sp, out_v[:, t, :], X[:, t, :], x_ready[t])
                h_free[s] = (tok,)
                w_free[w][1] = (tok,)
                load(e_ + 3, 1)

            def serial():
                for gen in before:
                    yield from gen

            split_x(0)
            pull(part(0), 99)
            pull(weave((rise(0), 8, 0.0, 1.0), (part(1), 4, 0.0, 1.0), (serial(), 17, 0.0, 1.0)), 99)
            pe.wait(dve.last(), act.last())
            tw = l_w.start(sp, b2[:], a["L3_ffn_b2"], dve.last(), act.last(), pe.last())
            bl = split(b2[:], b2h[:], b2l[:], tw, pe.last(), on_act=True)
            for e_ in range(8):
                parts = [(fall(e_), 8, 0.0, 1.0)]
                if e_ < 7:
                    parts.append((rise(e_ + 1), 8, 0.0, 1.0))
                if e_ < 6:
                    parts.append((part(e_ + 2), 4, 0.0, 1.0))
                pull(weave(*parts), 99)

        LOW = fixed.at
        t_b1 = l_w.start(sp, b1[:], a["L3_ffn_b1"])
        act.wait(t_b1)

        def taken():
            got = list(tail)
            tail.clear()
            return got

        def run():
            early = Region(nc, TOP - 18880, TOP)
            l0_attention(Region(nc, LOW, early.at), early)
            yield 1
            first_kv = Region(nc, LOW, early.at)
            kv = keys_values(first_kv, 1, False)
            ring = Slots([bank(0), bank(1)])

            def both():
                yield from kv["keys"](ring)
                yield from kv["values"](ring)

            l0_experts(Region(nc, kv["end"], TOP - 18880), both(), 21)
            yield 1

            stage = Region(nc, kv["end"], TOP)
            mi = nc.alloc_sbuf_tensor_at("mi1", [128, 2, M], I32, offset=stage.at)
            scope = Region(nc, kv["end"] + 26624, TOP)
            mb = sb(scope, "mb1", [128, NT, M], BF16)
            ready = [None] * NT
            load_mask(mb, mi, "L1", a["mask1"], ready, 4)
            made = {}

            def ternary(ring):
                k, prepare = l1_weights(stage, Region(nc, kv["at"], kv["end"]), BIG_AT + 12832, ready[-1], ready[-2], pe.last())
                made.update(k=k)
                yield 1
                yield 1
                yield from prepare(ring)

            single_attention(scope, kv, taken(), mb, ready, ternary, (1, 1, 20, 20), False)
            yield 1
            l1_ffn(Region(nc, stage.at, TOP), made["k"], taken())
            yield 1

            low = Region(nc, LOW, TOP)
            kv = keys_values(low, 2, True)
            after = Region(nc, LOW + 75008, TOP)
            k2, prepare2 = l2_weights(after)
            mi_at = after.at
            mi = sb(after, "mi3", [128, 1, M], I32)
            mb_at = TOP - 51232
            mb = nc.alloc_sbuf_tensor_at("mb3", [128, NT, M], BF16, offset=mb_at)
            ready = [None] * NT
            load_mask(mb, mi, "L3", a["mask3"], ready, 0)
            single_attention(Region(nc, low.at, LOW + 75008), kv, taken(), None, None,
                             prepare2, (1, 4, 4, 4), True)
            yield 1

            ks_at, P_at = LOW + 14144, LOW + 54976
            kq = l3_projections(Region(nc, P_at, P_at + 4160))
            l2_ffn(Region(nc, LOW, P_at), Region(nc, P_at + 4160, LOW + 75008), Region(nc, mi_at, mb_at), k2, taken())
            yield 1

            V = nc.alloc_sbuf_tensor_at("V3", [128, KT, 272], F32, offset=LOW)
            Ks = nc.alloc_sbuf_tensor_at("Ks", [99, 2, 4, M], BF16, offset=ks_at)
            Qs = nc.alloc_sbuf_tensor_at("Qs", [99, 2, 4, N], BF16, offset=P_at + 16384)
            xe = Experts(P_at + 16384)

            def next_load(tok):
                xe.load(0, 0, tok)
                xe.load(0, 1)

            l3_attention(V, Ks, Region(nc, ks_at + 25632, P_at), P_at, Qs, kq, mb, ready, taken(), next_load)
            yield 1
            l3_ffn(xe, Region(nc, LOW, P_at), Region(nc, LOW + 49152, P_at + 16384),
                   Region(nc, P_at + 16384 + 49152, TOP), taken())
            yield 1

        n = 0
        for _ in run():
            n += 1
            if n == phases:
                break
        if n < 8:
            for gen in taken():
                if not callable(gen):
                    pull(gen, 99)
            for t in range(NT):
                l_out.start(sp, out_v[:, t, :], X[:, t, :], x_ready[t])
        sp.wait((l_out.sem, l_out.count))

        block = ctx.enter_context(nc.Block())

        @block.sync
        def _(e):
            sp.play(e)

        @block.gpsimd
        def _(e):
            pool.play(e)

        @block.scalar
        def _(e):
            act.play(e)

        @block.tensor
        def _(e):
            pe.play(e)

        @block.vector
        def _(e):
            dve.play(e)


def arrange(inputs):
    def a(name):
        return np.asarray(inputs[name])

    def T(name):
        return np.ascontiguousarray(a(name).T)

    arrays = {
        "x": a("x").reshape(N, D),
        "ctxT": np.ascontiguousarray(a("ctx_1024").reshape(M, D).T),
        "mask1": a("mask_BxSxS2_ik0").reshape(N, M),
        "mask3": a("mask_1x1xSxS2_ik0").reshape(N, M),
    }
    for n in ("L0_xattn_Wv", "L0_xattn_Wo", "L0_ffn_gate_w", "L0_ffn_experts", "L1_ffn_w_fc", "L1_ffn_w_proj", "L1_ffn_u",
              "L3_ffn_w1", "L3_ffn_w2"):
        arrays[n] = a(n)
    for n in ("Wq", "Wk"):
        w = a("L0_xattn_" + n).reshape(D, 8, 1, 64)
        arrays["L0_" + n + "D"] = np.ascontiguousarray(np.broadcast_to(w, (D, 8, 2, 64))).reshape(D, 1024)
    for n in ("L0_xattn_bo", "L2_xattn_bv", "L3_xattn_bo"):
        arrays[n] = a(n).reshape(1, D)
    arrays["L3_ffn_b2"] = a("L3_ffn_b2").reshape(1, 8 * D)
    for n in ("L1_xattn_Wq", "L1_xattn_Wk", "L1_xattn_Wv", "L2_xattn_Wq", "L2_xattn_Wk", "L2_xattn_Wv",
              "L3_xattn_Wq", "L3_xattn_Wk", "L3_xattn_Wo", "L1_ffn_v", "L1_ffn_fast_b", "L2_ffn_w_up", "L2_ffn_w_down"):
        arrays[n + "T"] = T(n)
    arrays["L1_ffn_gate"] = a("L1_ffn_gate").reshape(1, 1)
    for n in ("L2_xattn_bq", "L2_xattn_bk", "L3_xattn_bq", "L3_xattn_bk"):
        arrays[n] = np.ascontiguousarray(a(n).reshape(2, 128).T)
    arrays["L3_ffn_b1"] = np.ascontiguousarray(a("L3_ffn_b1").reshape(64, 128).T)
    wv = np.zeros((D, 16, 17), np.float32)
    wv[:, :, 0:16] = a("L3_xattn_Wv").T.reshape(D, 16, 16)
    arrays["L3_WvP"] = wv.reshape(D, 272)
    bv = np.zeros((16, 17), np.float32)
    bv[:, 0:16] = a("L3_xattn_bv").reshape(16, 16)
    bv[:, 16] = 1.0
    arrays["L3_bvP"] = bv.reshape(1, 272)
    p = np.arange(128)
    arrays["c_tri"] = (p[None, :] < p[:, None]).astype(np.int32)
    arrays["c_base"] = np.broadcast_to((128.0 * np.arange(16, dtype=np.float32))[None, :, None],
                                       (128, 16, 8)).reshape(128, 128).copy()
    arrays["c_ecode"] = np.broadcast_to((1.0 + np.arange(8, dtype=np.float32))[None, None, :],
                                        (128, 16, 8)).reshape(128, 128).copy()
    sel8 = np.zeros((128, 8, 8), np.float32)
    sel8[:, np.arange(8), np.arange(8)] = 1.0
    arrays["c_sel8"] = sel8.reshape(128, 64)
    return arrays


def kernel(**inputs):
    import concourse.bacc as _bacc
    from concourse.bass_utils import run_bass_kernel_spmd as _run

    arrays = arrange(inputs)
    nc = _bacc.Bacc("TRN2", target_bir_lowering=False, num_devices=1)
    args, feed = {}, {}
    for name, arr in arrays.items():
        arr = np.ascontiguousarray(arr)
        feed["in_" + name] = arr
        args[name] = nc.dram_tensor("in_" + name, arr.shape, mybir.dt.from_np(arr.dtype), kind="ExternalInput").ap()
    out = nc.dram_tensor("out_0", (N, D), F32, kind="ExternalOutput").ap()
    build(nc, args, out)
    r = _run(nc, [feed], core_ids=[0])
    return r.results[0]["out_0"].reshape(1, N, D)
```
